# Optimizing a Trainium2 kernel written in Bass

```python
import numpy as np
import jax
import jax.numpy as jnp

def _softmax(x, axis=-1):
    return jax.nn.softmax(x, axis=axis)

def _gelu(x):
    return jax.nn.gelu(x, approximate=True)

def _silu(x):
    return jax.nn.silu(x)

def _sigmoid(x):
    return jax.nn.sigmoid(x)

def _layernorm(x, axis=-1, eps=1e-05):
    m = jnp.mean(x, axis=axis, keepdims=True)
    v = jnp.var(x, axis=axis, keepdims=True)
    return (x - m) / jnp.sqrt(v + eps)

def _scatter_add(tgt, idx, src, axis=0):
    return tgt.at[idx].add(src)

def _segment_sum(src, seg, n):
    return jax.ops.segment_sum(src, seg, n)
kernel_name = 'mk_perceiver_d4_seqx_r8_6fdcb4'

def setup_inputs(seed: int=0):
    np.random.seed(seed)
    _w = jnp.asarray

    def _rec_inputs():
        import jax
        import jax.numpy as jnp
        _rk = jax.random.key(seed)
        x = 6.313e-05 + 0.9998 * jax.random.normal(jax.random.fold_in(_rk, 1), (16, 64, 128), jnp.float32)
        _lenS = 64 - jax.random.randint(jax.random.fold_in(_rk, 7), (16,), 0, max(1, 64 // 4) + 1, jnp.int32)
        _lenS2 = 1601 - jax.random.randint(jax.random.fold_in(_rk, 8), (16,), 0, max(1, 1601 // 4) + 1, jnp.int32)
        _ctx_1024P = jax.random.normal(jax.random.fold_in(_rk, 11), (16, 16, 128), jnp.float32)
        _ctx_1024c = jax.random.dirichlet(jax.random.fold_in(_rk, 511), 0.3 * jnp.ones((16,), jnp.float32), (16, 1601))
        _ctx_1024t = jnp.einsum('bsk,bkd->bsd', _ctx_1024c, _ctx_1024P)
        _ctx_1024t = _ctx_1024t * jax.lax.rsqrt(jnp.mean(jnp.square(_ctx_1024t)) + 1e-12) * 0.953939
        ctx_1024 = -0.000214406 + 1.00034 * (_ctx_1024t + 0.3 * jax.random.normal(jax.random.fold_in(_rk, 611), (16, 1601, 128), jnp.float32))
        _validS = jnp.arange(64)[None, :] < _lenS[:, None]
        _validS2 = jnp.arange(1601)[None, :] < _lenS2[:, None]
        _causal = jnp.tril(jnp.ones((64, 64), dtype=bool))
        mask_BxS2_bf1 = jnp.ones((16, 1601), dtype=bool)
        return (x, ctx_1024, mask_BxS2_bf1)
    x, ctx_1024, mask_BxS2_bf1 = _rec_inputs()

    def _L0_xattn_setup():
        import jax, jax.numpy as jnp
        import numpy as np
        from jax import lax
        BIG = jnp.float32(1e+30)

        def _pairwise_euclidean(a, b):
            aa = jnp.sum(a * a, axis=-1)[:, None]
            bb = jnp.sum(b * b, axis=-1)[None, :]
            ab = a @ b.T
            return jnp.sqrt(jnp.maximum(aa + bb - 2.0 * ab, 0.0))

        def _dtw_cost(D):
            row0 = jnp.cumsum(D[0])

            def row_step(prev_row, d_row):
                first = d_row[0] + prev_row[0]

                def col_step(left, inp):
                    d_ij, up, diag = inp
                    r = d_ij + jnp.minimum(jnp.minimum(up, left), diag)
                    return (r, r)
                _, rest = lax.scan(col_step, first, (d_row[1:], prev_row[1:], prev_row[:-1]))
                row = jnp.concatenate([first[None], rest])
                return (row, row)
            _, rows = lax.scan(row_step, row0, D[1:])
            return jnp.concatenate([row0[None], rows], axis=0)

        def _backtrack(R, T1, T2):
            L = T1 + T2 - 1

            def step(carry, _):
                i, j, done = carry
                valid = jnp.logical_not(done)
                cd = jnp.where((i > 0) & (j > 0), R[jnp.maximum(i - 1, 0), jnp.maximum(j - 1, 0)], BIG)
                cu = jnp.where(i > 0, R[jnp.maximum(i - 1, 0), j], BIG)
                cl = jnp.where(j > 0, R[i, jnp.maximum(j - 1, 0)], BIG)
                choice = jnp.argmin(jnp.stack([cd, cu, cl]))
                ni = jnp.where(choice <= 1, i - 1, i)
                nj = jnp.where((choice == 0) | (choice == 2), j - 1, j)
                at_origin = (i == 0) & (j == 0)
                ni = jnp.where(at_origin, 0, ni)
                nj = jnp.where(at_origin, 0, nj)
                return ((ni, nj, done | at_origin), (i, j, valid))
            init = (jnp.int32(T1 - 1), jnp.int32(T2 - 1), jnp.bool_(False))
            _, (i_idx, j_idx, valid) = lax.scan(step, init, None, length=L)
            return (i_idx, j_idx, valid)

        def _align_one(small, large):
            T_small, d = small.shape
            T_large = large.shape[0]
            D = _pairwise_euclidean(small, large)
            R = _dtw_cost(D)
            i_idx, j_idx, valid = _backtrack(R, T_small, T_large)
            contrib = small[i_idx] * valid[:, None].astype(small.dtype)
            expanded = jnp.zeros((T_large, d), dtype=small.dtype).at[j_idx].add(contrib)
            return expanded
        key = jax.random.key(seed)
        k1, k2 = jax.random.split(key)
        teacher = jax.random.normal(k1, (16, 50, 128), dtype=jnp.float32)
        student = jax.random.normal(k2, (16, 75, 128), dtype=jnp.float32)
        return {'teacher_features': teacher, 'student_features': student}
    _L0_xattn_all = _L0_xattn_setup()
    _L0_xattn_in = {k: v for k, v in _L0_xattn_all.items() if k in ()}
    del _L0_xattn_all

    def _L0_attn_setup():
        import jax, jax.numpy as jnp
        import numpy as np
        EMBED_DIM = 128
        NUM_HEADS = 16
        HEAD_DIM = EMBED_DIM // NUM_HEADS
        EPSILON = 1e-06
        SCORE_SCALE = 1.0
        B, L = (2, 256)
        key = jax.random.key(seed)
        k0, k1, k2, k3, k4 = jax.random.split(key, 5)
        s_in = 1.0 / np.sqrt(EMBED_DIM)
        return {'x': jax.random.normal(k0, (B, L, EMBED_DIM), dtype=jnp.float32), 'w_qkv': jax.random.normal(k1, (EMBED_DIM, 3 * EMBED_DIM), dtype=jnp.float32) * s_in, 'b_qkv': jnp.zeros((3 * EMBED_DIM,), dtype=jnp.float32), 'w_out': jax.random.normal(k2, (EMBED_DIM, EMBED_DIM), dtype=jnp.float32) * s_in, 'b_out': jnp.zeros((EMBED_DIM,), dtype=jnp.float32)}
    _L0_attn_all = _L0_attn_setup()
    _L0_attn_in = {k: v for k, v in _L0_attn_all.items() if k in ('w_qkv', 'b_qkv', 'w_out', 'b_out')}
    del _L0_attn_all

    def _L0_ffn_setup():
        import jax, jax.numpy as jnp
        import numpy as np
        BLOCK = 16
        _GRID = jnp.array([0.0, 0.5, 1.0, 1.5, 2.0, 3.0, 4.0, 6.0], dtype=jnp.float32)
        _MID = jnp.array([0.25, 0.75, 1.25, 1.75, 2.5, 3.5, 5.0], dtype=jnp.float32)

        def fp4_quant_dequant(x):
            shape = x.shape
            xb = x.reshape(shape[:-1] + (shape[-1] // BLOCK, BLOCK))
            scale = jnp.max(jnp.abs(xb), axis=-1, keepdims=True) / 6.0
            scale = jnp.maximum(scale, jnp.float32(1e-12))
            xn = xb / scale
            idx = jnp.searchsorted(_MID, jnp.abs(xn))
            q = _GRID[idx] * jnp.sign(xn) * scale
            return q.reshape(shape)

        def fp4_linear(x, w):
            xq = fp4_quant_dequant(x)
            wq = fp4_quant_dequant(w)
            return jnp.einsum('bsk,nk->bsn', xq, wq)
        key = jax.random.key(seed)
        k1, k2, k3, k4 = jax.random.split(key, 4)
        H, I = (128, 352)
        x = jax.random.normal(k1, (4, 512, H), dtype=jnp.float32)
        w_gate = jax.random.normal(k2, (I, H), dtype=jnp.float32) * 0.02
        w_up = jax.random.normal(k3, (I, H), dtype=jnp.float32) * 0.02
        w_down = jax.random.normal(k4, (H, I), dtype=jnp.float32) * 0.02
        return {'x': x, 'w_gate': w_gate, 'w_up': w_up, 'w_down': w_down}
    _L0_ffn_all = _L0_ffn_setup()
    _L0_ffn_in = {k: v for k, v in _L0_ffn_all.items() if k in ('w_gate', 'w_up', 'w_down')}
    del _L0_ffn_all

    def _L1_xattn_setup():
        import jax, jax.numpy as jnp
        import numpy as np
        B, N, M = (2, 256, 256)
        QUERY_DIM = 128
        CONTEXT_DIM = 128
        HEADS = 16
        DIM_HEAD = 64
        INNER = HEADS * DIM_HEAD
        SCALE = DIM_HEAD ** (-0.5)
        key = jax.random.key(seed)
        ks = jax.random.split(key, 7)
        x = jax.random.normal(ks[0], (B, N, QUERY_DIM), dtype=jnp.float32)
        context = jax.random.normal(ks[1], (B, M, CONTEXT_DIM), dtype=jnp.float32)
        mask = jnp.ones((B, M), dtype=bool)
        s = 0.02
        Wq = jax.random.normal(ks[2], (QUERY_DIM, INNER), dtype=jnp.float32) * s
        Wk = jax.random.normal(ks[3], (CONTEXT_DIM, INNER), dtype=jnp.float32) * s
        Wv = jax.random.normal(ks[4], (CONTEXT_DIM, INNER), dtype=jnp.float32) * s
        Wo = jax.random.normal(ks[5], (INNER, QUERY_DIM), dtype=jnp.float32) * s
        bo = jnp.zeros((QUERY_DIM,), dtype=jnp.float32)
        return {'x': x, 'context': context, 'mask': mask, 'Wq': Wq, 'Wk': Wk, 'Wv': Wv, 'Wo': Wo, 'bo': bo}
    _L1_xattn_all = _L1_xattn_setup()
    _L1_xattn_in = {k: v for k, v in _L1_xattn_all.items() if k in ('Wq', 'Wk', 'Wv', 'Wo', 'bo')}
    del _L1_xattn_all

    def _L1_attn_setup():
        import jax, jax.numpy as jnp
        import numpy as np
        D_MODEL = 128
        N_HEADS = 16
        D_HIDDEN = 512
        BATCH = 2
        N_CTX = 256

        def _split_heads(t, n_heads):
            B, S, D = t.shape
            return t.reshape(B, S, n_heads, D // n_heads).transpose(0, 2, 1, 3)
        key = jax.random.key(seed)
        ks = jax.random.split(key, 4)
        scale = 0.02
        x = jax.random.normal(ks[0], (BATCH, N_CTX, D_MODEL), dtype=jnp.float32)
        Wk = jax.random.normal(ks[1], (D_MODEL, D_MODEL), dtype=jnp.float32) * scale
        bk = jnp.zeros((D_MODEL,), dtype=jnp.float32)
        Wv = jax.random.normal(ks[2], (D_MODEL, D_HIDDEN), dtype=jnp.float32) * scale
        bv = jnp.zeros((D_HIDDEN,), dtype=jnp.float32)
        Wf = jax.random.normal(ks[3], (D_HIDDEN, D_MODEL), dtype=jnp.float32) * scale
        bf = jnp.zeros((D_MODEL,), dtype=jnp.float32)
        return {'x': x, 'Wk': Wk, 'bk': bk, 'Wv': Wv, 'bv': bv, 'Wf': Wf, 'bf': bf}
    _L1_attn_all = _L1_attn_setup()
    _L1_attn_in = {k: v for k, v in _L1_attn_all.items() if k in ('Wk', 'bk', 'Wv', 'bv', 'Wf', 'bf')}
    del _L1_attn_all

    def _L1_ffn_setup():
        import jax, jax.numpy as jnp
        import numpy as np
        E = 8
        K = 2
        D = 128
        H = 512
        CAP_FACTOR = 1.0
        key = jax.random.key(seed)
        ks = jax.random.split(key, 5)
        x = jax.random.normal(ks[0], (4, 256, D), jnp.float32)
        gate_w = jax.random.normal(ks[1], (E, D), jnp.float32) * 0.02
        fc1_w = jax.random.normal(ks[2], (E, H, D), jnp.float32) * 0.02
        fc1_b = jnp.zeros((E, 1, H), jnp.float32)
        fc2_w = jax.random.normal(ks[3], (E, H, D), jnp.float32) * 0.02
        fc2_b = jnp.zeros((E, 1, D), jnp.float32)
        return {'x': x, 'gate_w': gate_w, 'fc1_w': fc1_w, 'fc1_b': fc1_b, 'fc2_w': fc2_w, 'fc2_b': fc2_b}
    _L1_ffn_all = _L1_ffn_setup()
    _L1_ffn_in = {k: v for k, v in _L1_ffn_all.items() if k in ('gate_w', 'fc1_w', 'fc1_b', 'fc2_w', 'fc2_b')}
    del _L1_ffn_all

    def _L2_xattn_setup():
        import jax, jax.numpy as jnp
        import numpy as np
        HIDDEN = 128
        HEADS = 16
        HEAD_DIM = 64
        key = jax.random.key(seed)
        ks = jax.random.split(key, 7)
        B, Q, K = (2, 256, 512)
        s = 1.0 / np.sqrt(HIDDEN)
        return {'query': jax.random.normal(ks[0], (B, Q, HIDDEN), dtype=jnp.float32), 'key': jax.random.normal(ks[1], (B, K, HIDDEN), dtype=jnp.float32), 'value': jax.random.normal(ks[2], (B, K, HIDDEN), dtype=jnp.float32), 'w_q': jax.random.normal(ks[3], (HIDDEN, HEADS * HEAD_DIM), dtype=jnp.float32) * s, 'w_k': jax.random.normal(ks[4], (HIDDEN, HEADS * HEAD_DIM), dtype=jnp.float32) * s, 'w_v': jax.random.normal(ks[5], (HIDDEN, HEADS * HEAD_DIM), dtype=jnp.float32) * s, 'w_o': jax.random.normal(ks[6], (HEADS * HEAD_DIM, HIDDEN), dtype=jnp.float32) * s}
    _L2_xattn_all = _L2_xattn_setup()
    _L2_xattn_in = {k: v for k, v in _L2_xattn_all.items() if k in ('w_q', 'w_k', 'w_v', 'w_o')}
    del _L2_xattn_all

    def _L2_attn_setup():
        import math
        import jax, jax.numpy as jnp
        import numpy as np
        NUM_HEADS = 16
        EMBED = 128
        B, T = (2, 256)
        key = jax.random.key(seed)
        k1, k2 = jax.random.split(key)
        x = jax.random.normal(k1, (B, T, EMBED), dtype=jnp.float32)
        bound = 1.0 / math.sqrt(NUM_HEADS * EMBED)
        weight = jax.random.uniform(k2, (NUM_HEADS * EMBED, EMBED), dtype=jnp.float32, minval=-bound, maxval=bound)
        return {'x': x, 'weight': weight}
    _L2_attn_all = _L2_attn_setup()
    _L2_attn_in = {k: v for k, v in _L2_attn_all.items() if k in ('weight',)}
    del _L2_attn_all

    def _L2_ffn_setup():
        import jax, jax.numpy as jnp
        import numpy as np
        B, T, D_IN, D_OUT = (4, 256, 128, 128)
        N_EXPERTS, N_ACTIVE = (8, 2)
        key = jax.random.key(seed)
        k1, k2, k3, k4, k5 = jax.random.split(key, 5)
        s_in = 1.0 / np.sqrt(D_IN)
        x = jax.random.normal(k1, (B, T, D_IN), dtype=jnp.float32)
        w_router = jax.random.uniform(k2, (N_EXPERTS, D_IN), jnp.float32, -s_in, s_in)
        b_router = jax.random.uniform(k3, (N_EXPERTS,), jnp.float32, -s_in, s_in)
        w_experts = jax.random.uniform(k4, (N_EXPERTS, D_OUT, D_IN), jnp.float32, -s_in, s_in)
        b_experts = jax.random.uniform(k5, (N_EXPERTS, D_OUT), jnp.float32, -s_in, s_in)
        return {'x': x, 'w_router': w_router, 'b_router': b_router, 'w_experts': w_experts, 'b_experts': b_experts}
    _L2_ffn_all = _L2_ffn_setup()
    _L2_ffn_in = {k: v for k, v in _L2_ffn_all.items() if k in ('w_router', 'b_router', 'w_experts', 'b_experts')}
    del _L2_ffn_all

    def _L3_xattn_setup():
        import jax, jax.numpy as jnp
        import numpy as np
        import math
        D_MODEL = 128
        N_HEADS = 16
        HEAD_DIM = D_MODEL // N_HEADS
        TOP_K = 32
        SCALE = math.sqrt(HEAD_DIM)

        def _split_heads(t, n):
            B, L, _ = t.shape
            return t.reshape(B, L, N_HEADS, HEAD_DIM).transpose(0, 2, 1, 3)
        key = jax.random.key(seed)
        ks = jax.random.split(key, 12)
        B, S, N = (2, 256, 256)
        std = 1.0 / math.sqrt(D_MODEL)
        inp = {'x': jax.random.normal(ks[0], (B, S, D_MODEL), dtype=jnp.float32), 'knowledge_embeddings': jax.random.normal(ks[1], (B, N, D_MODEL), dtype=jnp.float32), 'Wq': jax.random.normal(ks[2], (D_MODEL, D_MODEL), dtype=jnp.float32) * std, 'bq': jnp.zeros((D_MODEL,), dtype=jnp.float32), 'Wk': jax.random.normal(ks[3], (D_MODEL, D_MODEL), dtype=jnp.float32) * std, 'bk': jnp.zeros((D_MODEL,), dtype=jnp.float32), 'Wv': jax.random.normal(ks[4], (D_MODEL, D_MODEL), dtype=jnp.float32) * std, 'bv': jnp.zeros((D_MODEL,), dtype=jnp.float32), 'Wo': jax.random.normal(ks[5], (D_MODEL, D_MODEL), dtype=jnp.float32) * std, 'bo': jnp.zeros((D_MODEL,), dtype=jnp.float32)}
        return inp
    _L3_xattn_all = _L3_xattn_setup()
    _L3_xattn_in = {k: v for k, v in _L3_xattn_all.items() if k in ('Wq', 'bq', 'Wk', 'bk', 'Wv', 'bv', 'Wo', 'bo')}
    del _L3_xattn_all

    def _L3_attn_setup():
        import jax, jax.numpy as jnp
        import numpy as np
        from math import log2, ceil
        HEADS, DIM_HEAD, BLOCK, EPS = (16, 64, 16, 1e-08)
        key = jax.random.key(seed)
        k1, k2, k3, k4 = jax.random.split(key, 4)
        b, n, dim = (4, 512, 128)
        inner = HEADS * DIM_HEAD
        return {'x': jax.random.normal(k1, (b, n, dim), jnp.float32), 'w_qkv': jax.random.normal(k2, (inner * 3, dim), jnp.float32) * 0.02, 'w_out': jax.random.normal(k3, (dim, inner), jnp.float32) * 0.02, 'b_out': jax.random.normal(k4, (dim,), jnp.float32) * 0.02}
    _L3_attn_all = _L3_attn_setup()
    _L3_attn_in = {k: v for k, v in _L3_attn_all.items() if k in ('w_qkv', 'w_out', 'b_out')}
    del _L3_attn_all

    def _L3_ffn_setup():
        import jax, jax.numpy as jnp
        import numpy as np
        D = 128
        F = 128
        E = 8
        K = 2
        B, T = (2, 256)

        def _moe_forward(x, router_w, w1, w2, shared_gate_up, shared_down, shared_gate_w):
            b, t, d = x.shape
            xf = x.reshape(-1, d)
            n = xf.shape[0]
            logits = xf @ router_w
            probs = jax.nn.softmax(logits, axis=-1)
            topw, topi = jax.lax.top_k(probs, K)
            combine = jnp.zeros((n, E), dtype=probs.dtype).at[jnp.arange(n)[:, None], topi].add(topw)
            h = jax.nn.silu(jnp.einsum('nd,edf->nef', xf, w1))
            ye = jnp.einsum('nef,efd->ned', h, w2)
            routed = jnp.einsum('ne,ned->nd', combine, ye)
            gu = xf @ shared_gate_up
            gate, up = (gu[:, :F], gu[:, F:])
            shared = jax.nn.silu(gate) * up @ shared_down
            shared = jax.nn.sigmoid(xf @ shared_gate_w) * shared
            return (routed + shared).reshape(b, t, d)
        key = jax.random.key(seed)
        ks = jax.random.split(key, 7)
        std = 0.02
        x = jax.random.normal(ks[0], (B, T, D), dtype=jnp.float32)
        router_w = jax.random.normal(ks[1], (D, E), dtype=jnp.float32) * std
        w1 = jax.random.normal(ks[2], (E, D, F), dtype=jnp.float32) * std
        w2 = jax.random.normal(ks[3], (E, F, D), dtype=jnp.float32) * std
        shared_gate_up = jax.random.normal(ks[4], (D, 2 * F), dtype=jnp.float32) * std
        shared_down = jax.random.normal(ks[5], (F, D), dtype=jnp.float32) * std
        shared_gate_w = jax.random.normal(ks[6], (D, 1), dtype=jnp.float32) * std
        return {'x': x, 'router_w': router_w, 'w1': w1, 'w2': w2, 'shared_gate_up': shared_gate_up, 'shared_down': shared_down, 'shared_gate_w': shared_gate_w}
    _L3_ffn_all = _L3_ffn_setup()
    _L3_ffn_in = {k: v for k, v in _L3_ffn_all.items() if k in ('router_w', 'w1', 'w2', 'shared_gate_up', 'shared_down', 'shared_gate_w')}
    del _L3_ffn_all
    return {'x': x, 'ctx_1024': ctx_1024, 'mask_BxS2_bf1': mask_BxS2_bf1, 'L0_attn_w_qkv': _L0_attn_in['w_qkv'], 'L0_attn_b_qkv': _L0_attn_in['b_qkv'], 'L0_attn_w_out': _L0_attn_in['w_out'], 'L0_attn_b_out': _L0_attn_in['b_out'], 'L0_ffn_w_gate': _L0_ffn_in['w_gate'], 'L0_ffn_w_up': _L0_ffn_in['w_up'], 'L0_ffn_w_down': _L0_ffn_in['w_down'], 'L1_xattn_Wq': _L1_xattn_in['Wq'], 'L1_xattn_Wk': _L1_xattn_in['Wk'], 'L1_xattn_Wv': _L1_xattn_in['Wv'], 'L1_xattn_Wo': _L1_xattn_in['Wo'], 'L1_xattn_bo': _L1_xattn_in['bo'], 'L1_attn_Wk': _L1_attn_in['Wk'], 'L1_attn_bk': _L1_attn_in['bk'], 'L1_attn_Wv': _L1_attn_in['Wv'], 'L1_attn_bv': _L1_attn_in['bv'], 'L1_attn_Wf': _L1_attn_in['Wf'], 'L1_attn_bf': _L1_attn_in['bf'], 'L1_ffn_gate_w': _L1_ffn_in['gate_w'], 'L1_ffn_fc1_w': _L1_ffn_in['fc1_w'], 'L1_ffn_fc1_b': _L1_ffn_in['fc1_b'], 'L1_ffn_fc2_w': _L1_ffn_in['fc2_w'], 'L1_ffn_fc2_b': _L1_ffn_in['fc2_b'], 'L2_xattn_w_q': _L2_xattn_in['w_q'], 'L2_xattn_w_k': _L2_xattn_in['w_k'], 'L2_xattn_w_v': _L2_xattn_in['w_v'], 'L2_xattn_w_o': _L2_xattn_in['w_o'], 'L2_attn_weight': _L2_attn_in['weight'], 'L2_ffn_w_router': _L2_ffn_in['w_router'], 'L2_ffn_b_router': _L2_ffn_in['b_router'], 'L2_ffn_w_experts': _L2_ffn_in['w_experts'], 'L2_ffn_b_experts': _L2_ffn_in['b_experts'], 'L3_xattn_Wq': _L3_xattn_in['Wq'], 'L3_xattn_bq': _L3_xattn_in['bq'], 'L3_xattn_Wk': _L3_xattn_in['Wk'], 'L3_xattn_bk': _L3_xattn_in['bk'], 'L3_xattn_Wv': _L3_xattn_in['Wv'], 'L3_xattn_bv': _L3_xattn_in['bv'], 'L3_xattn_Wo': _L3_xattn_in['Wo'], 'L3_xattn_bo': _L3_xattn_in['bo'], 'L3_attn_w_qkv': _L3_attn_in['w_qkv'], 'L3_attn_w_out': _L3_attn_in['w_out'], 'L3_attn_b_out': _L3_attn_in['b_out'], 'L3_ffn_router_w': _L3_ffn_in['router_w'], 'L3_ffn_w1': _L3_ffn_in['w1'], 'L3_ffn_w2': _L3_ffn_in['w2'], 'L3_ffn_shared_gate_up': _L3_ffn_in['shared_gate_up'], 'L3_ffn_shared_down': _L3_ffn_in['shared_down'], 'L3_ffn_shared_gate_w': _L3_ffn_in['shared_gate_w']}

def reference(x, ctx_1024, mask_BxS2_bf1, L0_attn_w_qkv, L0_attn_b_qkv, L0_attn_w_out, L0_attn_b_out, L0_ffn_w_gate, L0_ffn_w_up, L0_ffn_w_down, L1_xattn_Wq, L1_xattn_Wk, L1_xattn_Wv, L1_xattn_Wo, L1_xattn_bo, L1_attn_Wk, L1_attn_bk, L1_attn_Wv, L1_attn_bv, L1_attn_Wf, L1_attn_bf, L1_ffn_gate_w, L1_ffn_fc1_w, L1_ffn_fc1_b, L1_ffn_fc2_w, L1_ffn_fc2_b, L2_xattn_w_q, L2_xattn_w_k, L2_xattn_w_v, L2_xattn_w_o, L2_attn_weight, L2_ffn_w_router, L2_ffn_b_router, L2_ffn_w_experts, L2_ffn_b_experts, L3_xattn_Wq, L3_xattn_bq, L3_xattn_Wk, L3_xattn_bk, L3_xattn_Wv, L3_xattn_bv, L3_xattn_Wo, L3_xattn_bo, L3_attn_w_qkv, L3_attn_w_out, L3_attn_b_out, L3_ffn_router_w, L3_ffn_w1, L3_ffn_w2, L3_ffn_shared_gate_up, L3_ffn_shared_down, L3_ffn_shared_gate_w):
    import jax
    import jax.numpy as jnp

    def _L0_xattn_ref(teacher_features, student_features):
        import jax, jax.numpy as jnp
        import numpy as np
        from jax import lax
        BIG = jnp.float32(1e+30)

        def _pairwise_euclidean(a, b):
            aa = jnp.sum(a * a, axis=-1)[:, None]
            bb = jnp.sum(b * b, axis=-1)[None, :]
            ab = a @ b.T
            return jnp.sqrt(jnp.maximum(aa + bb - 2.0 * ab, 0.0))

        def _dtw_cost(D):
            row0 = jnp.cumsum(D[0])

            def row_step(prev_row, d_row):
                first = d_row[0] + prev_row[0]

                def col_step(left, inp):
                    d_ij, up, diag = inp
                    r = d_ij + jnp.minimum(jnp.minimum(up, left), diag)
                    return (r, r)
                _, rest = lax.scan(col_step, first, (d_row[1:], prev_row[1:], prev_row[:-1]))
                row = jnp.concatenate([first[None], rest])
                return (row, row)
            _, rows = lax.scan(row_step, row0, D[1:])
            return jnp.concatenate([row0[None], rows], axis=0)

        def _backtrack(R, T1, T2):
            L = T1 + T2 - 1

            def step(carry, _):
                i, j, done = carry
                valid = jnp.logical_not(done)
                cd = jnp.where((i > 0) & (j > 0), R[jnp.maximum(i - 1, 0), jnp.maximum(j - 1, 0)], BIG)
                cu = jnp.where(i > 0, R[jnp.maximum(i - 1, 0), j], BIG)
                cl = jnp.where(j > 0, R[i, jnp.maximum(j - 1, 0)], BIG)
                choice = jnp.argmin(jnp.stack([cd, cu, cl]))
                ni = jnp.where(choice <= 1, i - 1, i)
                nj = jnp.where((choice == 0) | (choice == 2), j - 1, j)
                at_origin = (i == 0) & (j == 0)
                ni = jnp.where(at_origin, 0, ni)
                nj = jnp.where(at_origin, 0, nj)
                return ((ni, nj, done | at_origin), (i, j, valid))
            init = (jnp.int32(T1 - 1), jnp.int32(T2 - 1), jnp.bool_(False))
            _, (i_idx, j_idx, valid) = lax.scan(step, init, None, length=L)
            return (i_idx, j_idx, valid)

        def _align_one(small, large):
            T_small, d = small.shape
            T_large = large.shape[0]
            D = _pairwise_euclidean(small, large)
            R = _dtw_cost(D)
            i_idx, j_idx, valid = _backtrack(R, T_small, T_large)
            contrib = small[i_idx] * valid[:, None].astype(small.dtype)
            expanded = jnp.zeros((T_large, d), dtype=small.dtype).at[j_idx].add(contrib)
            return expanded
        return jax.vmap(_align_one)(teacher_features, student_features)

    def _L0_attn_ref(x, w_qkv, b_qkv, w_out, b_out):
        import jax, jax.numpy as jnp
        import numpy as np
        EMBED_DIM = 128
        NUM_HEADS = 16
        HEAD_DIM = EMBED_DIM // NUM_HEADS
        EPSILON = 1e-06
        SCORE_SCALE = 1.0
        B, L = (2, 256)
        Bq, Lq, E = x.shape
        qkv = x @ w_qkv + b_qkv
        q, k, v = jnp.split(qkv, 3, axis=-1)
        q = q.reshape(Bq, Lq, NUM_HEADS, HEAD_DIM).transpose(0, 2, 1, 3)
        k = k.reshape(Bq, Lq, NUM_HEADS, HEAD_DIM).transpose(0, 2, 1, 3)
        v = v.reshape(Bq, Lq, NUM_HEADS, HEAD_DIM).transpose(0, 2, 1, 3)
        dot = jnp.einsum('bhid,bhjd->bhij', q, k)
        q_norm_sq = jnp.sum(q * q, axis=-1, keepdims=True)
        k_norm_sq = jnp.sum(k * k, axis=-1, keepdims=True)
        vals = q_norm_sq + k_norm_sq.transpose(0, 1, 3, 2)
        scores = dot * dot / (vals - 2.0 * dot + EPSILON) * SCORE_SCALE
        mask = jnp.triu(jnp.ones((Lq, Lq), dtype=scores.dtype), k=1) * -1000000000.0
        scores = scores + mask[None, None, :, :]
        attn = jax.nn.softmax(scores, axis=-1)
        out = jnp.einsum('bhij,bhjd->bhid', attn, v)
        out = out.transpose(0, 2, 1, 3).reshape(Bq, Lq, E)
        return out @ w_out + b_out

    def _L0_ffn_ref(x, w_gate, w_up, w_down):
        import jax, jax.numpy as jnp
        import numpy as np
        BLOCK = 16
        _GRID = jnp.array([0.0, 0.5, 1.0, 1.5, 2.0, 3.0, 4.0, 6.0], dtype=jnp.float32)
        _MID = jnp.array([0.25, 0.75, 1.25, 1.75, 2.5, 3.5, 5.0], dtype=jnp.float32)

        def fp4_quant_dequant(x):
            shape = x.shape
            xb = x.reshape(shape[:-1] + (shape[-1] // BLOCK, BLOCK))
            scale = jnp.max(jnp.abs(xb), axis=-1, keepdims=True) / 6.0
            scale = jnp.maximum(scale, jnp.float32(1e-12))
            xn = xb / scale
            idx = jnp.searchsorted(_MID, jnp.abs(xn))
            q = _GRID[idx] * jnp.sign(xn) * scale
            return q.reshape(shape)

        def fp4_linear(x, w):
            xq = fp4_quant_dequant(x)
            wq = fp4_quant_dequant(w)
            return jnp.einsum('bsk,nk->bsn', xq, wq)
        gate = fp4_linear(x, w_gate)
        y = fp4_linear(x, w_up)
        h = jax.nn.silu(gate) * y
        return fp4_linear(h, w_down)

    def _L1_xattn_ref(x, context, mask, Wq, Wk, Wv, Wo, bo):
        import jax, jax.numpy as jnp
        import numpy as np
        B, N, M = (2, 256, 256)
        QUERY_DIM = 128
        CONTEXT_DIM = 128
        HEADS = 16
        DIM_HEAD = 64
        INNER = HEADS * DIM_HEAD
        SCALE = DIM_HEAD ** (-0.5)
        b, n, _ = x.shape
        m = context.shape[1]
        q = (x @ Wq).reshape(b, n, HEADS, DIM_HEAD)
        k = (context @ Wk).reshape(b, m, HEADS, DIM_HEAD)
        v = (context @ Wv).reshape(b, m, HEADS, DIM_HEAD)
        dots = jnp.einsum('bnhd,bmhd->bhnm', q, k) * SCALE
        neg = -jnp.finfo(dots.dtype).max
        dots = jnp.where(mask[:, None, None, :], dots, neg)
        attn = jax.nn.softmax(dots, axis=-1)
        out = jnp.einsum('bhnm,bmhd->bnhd', attn, v).reshape(b, n, INNER)
        return out @ Wo + bo

    def _L1_attn_ref(x, Wk, bk, Wv, bv, Wf, bf):
        import jax, jax.numpy as jnp
        import numpy as np
        D_MODEL = 128
        N_HEADS = 16
        D_HIDDEN = 512
        BATCH = 2
        N_CTX = 256

        def _split_heads(t, n_heads):
            B, S, D = t.shape
            return t.reshape(B, S, n_heads, D // n_heads).transpose(0, 2, 1, 3)
        B, S, D = x.shape
        H = N_HEADS
        Q = _split_heads(x, H)
        K = _split_heads(x @ Wk + bk, H)
        V = _split_heads(x @ Wv + bv, H)
        causal = jnp.tril(jnp.ones((S, S), dtype=bool))
        mask = jnp.where(causal, 0.0, -jnp.inf).astype(x.dtype)
        scores = jnp.einsum('bhqd,bhkd->bhqk', Q, K) + mask
        attn = jax.nn.softmax(scores, axis=-1)
        o = jnp.einsum('bhqk,bhkd->bhqd', attn, V)
        o = o.transpose(0, 2, 1, 3).reshape(B, S, -1)
        return x + jax.nn.gelu(o, approximate=False) @ Wf + bf

    def _L1_ffn_ref(x, gate_w, fc1_w, fc1_b, fc2_w, fc2_b):
        import jax, jax.numpy as jnp
        import numpy as np
        E = 8
        K = 2
        D = 128
        H = 512
        CAP_FACTOR = 1.0
        B, S, Dm = x.shape
        xf = x.reshape(-1, Dm)
        N = xf.shape[0]
        cap = int(K * CAP_FACTOR * ((N + E - 1) // E))
        logits = xf @ gate_w.T
        scores = jax.nn.softmax(logits, axis=-1)
        topv, topi = jax.lax.top_k(scores, K)
        gates = topv / jnp.sum(topv, axis=-1, keepdims=True)
        offset = jnp.zeros((E,), jnp.int32)
        locs = []
        for j in range(K):
            mask = jax.nn.one_hot(topi[:, j], E, dtype=jnp.int32)
            loc_in = jnp.cumsum(mask, axis=0) - 1 + offset[None, :]
            locs.append(jnp.take_along_axis(loc_in, topi[:, j:j + 1], axis=1)[:, 0])
            offset = offset + mask.sum(axis=0)
        loc = jnp.stack(locs, axis=1)
        valid = loc < cap
        flat_idx = jnp.where(valid, topi * cap + loc, 0)
        w = valid.astype(xf.dtype)
        disp = jnp.zeros((E * cap, Dm), xf.dtype)
        disp = disp.at[flat_idx.reshape(-1)].add((xf[:, None, :] * w[:, :, None]).reshape(-1, Dm))
        de = disp.reshape(E, cap, Dm)
        h = jax.nn.relu(jnp.einsum('ecd,ehd->ech', de, fc1_w) + fc1_b)
        eo = jnp.einsum('ech,ehd->ecd', h, fc2_w) + fc2_b
        gathered = eo.reshape(E * cap, Dm)[flat_idx]
        out = jnp.sum(gathered * (gates * w)[:, :, None], axis=1)
        return out.reshape(B, S, Dm)

    def _L2_xattn_ref(query, key, value, w_q, w_k, w_v, w_o):
        import jax, jax.numpy as jnp
        import numpy as np
        HIDDEN = 128
        HEADS = 16
        HEAD_DIM = 64
        B, Q, _ = query.shape
        Kl = key.shape[1]
        scale = HEAD_DIM ** (-0.5)
        q = (query @ w_q).reshape(B, Q, HEADS, HEAD_DIM).transpose(0, 2, 1, 3)
        k = (key @ w_k).reshape(B, Kl, HEADS, HEAD_DIM).transpose(0, 2, 1, 3)
        v = (value @ w_v).reshape(B, Kl, HEADS, HEAD_DIM).transpose(0, 2, 1, 3)
        scores = jnp.einsum('bhqd,bhkd->bhqk', q, k) * scale
        attn = jax.nn.softmax(scores, axis=-1)
        out = jnp.einsum('bhqk,bhkd->bhqd', attn, v)
        out = out.transpose(0, 2, 1, 3).reshape(B, Q, HEADS * HEAD_DIM)
        return out @ w_o

    def _L2_attn_ref(x, weight):
        import math
        import jax, jax.numpy as jnp
        import numpy as np
        NUM_HEADS = 16
        EMBED = 128
        B, T = (2, 256)
        b, t, c = x.shape
        nh = NUM_HEADS
        hs = c // nh
        y = x.reshape(b, t, nh, hs).transpose(0, 2, 1, 3)
        scores = jnp.einsum('bhtk,bhsk->bhts', y, y) / math.sqrt(hs)
        attn = jax.nn.softmax(scores, axis=-1)
        o = jnp.einsum('bhts,bsc->bhtc', attn, x)
        o = o.transpose(0, 2, 1, 3).reshape(b, t, nh * c)
        return o @ weight

    def _L2_ffn_ref(x, w_router, b_router, w_experts, b_experts):
        import jax, jax.numpy as jnp
        import numpy as np
        B, T, D_IN, D_OUT = (4, 256, 128, 128)
        N_EXPERTS, N_ACTIVE = (8, 2)
        gamma = jax.nn.softmax(jnp.einsum('btd,ed->bte', x, w_router) + b_router, axis=-1)
        _, expert_ids = jax.lax.top_k(gamma, N_ACTIVE)
        mask = (expert_ids[..., None] == jnp.arange(N_EXPERTS)).any(axis=-2)
        y_all = jnp.einsum('btd,eod->bteo', x, w_experts) + b_experts
        y = jnp.einsum('bte,bteo->bto', mask.astype(x.dtype), y_all)
        return y

    def _L3_xattn_ref(x, knowledge_embeddings, Wq, bq, Wk, bk, Wv, bv, Wo, bo):
        import jax, jax.numpy as jnp
        import numpy as np
        import math
        D_MODEL = 128
        N_HEADS = 16
        HEAD_DIM = D_MODEL // N_HEADS
        TOP_K = 32
        SCALE = math.sqrt(HEAD_DIM)

        def _split_heads(t, n):
            B, L, _ = t.shape
            return t.reshape(B, L, N_HEADS, HEAD_DIM).transpose(0, 2, 1, 3)
        B, S, _ = x.shape
        N = knowledge_embeddings.shape[1]
        Q = _split_heads(x @ Wq.T + bq, N_HEADS)
        K = _split_heads(knowledge_embeddings @ Wk.T + bk, N_HEADS)
        V = _split_heads(knowledge_embeddings @ Wv.T + bv, N_HEADS)
        scores = jnp.einsum('bhsd,bhnd->bhsn', Q, K) / SCALE
        k = min(TOP_K, N)
        topk_scores, topk_indices = jax.lax.top_k(scores, k)
        sparse_weights = jax.nn.softmax(topk_scores, axis=-1)
        sel_V = jnp.take_along_axis(V[:, :, None, :, :], topk_indices[..., None], axis=3)
        context = jnp.einsum('bhsk,bhskd->bhsd', sparse_weights, sel_V)
        context = context.transpose(0, 2, 1, 3).reshape(B, S, D_MODEL)
        return context @ Wo.T + bo

    def _L3_attn_ref(x, w_qkv, w_out, b_out):
        import jax, jax.numpy as jnp
        import numpy as np
        from math import log2, ceil
        HEADS, DIM_HEAD, BLOCK, EPS = (16, 64, 16, 1e-08)
        b, n, dim = x.shape
        pad_to_len = 2 ** ceil(log2(n))
        if pad_to_len != n:
            x = jnp.pad(x, ((0, 0), (0, pad_to_len - n), (0, 0)))
        qkv = x @ w_qkv.T
        q, k, v = jnp.split(qkv, 3, axis=-1)

        def split_heads(t):
            return t.reshape(b, pad_to_len, HEADS, DIM_HEAD).transpose(0, 2, 1, 3).reshape(b * HEADS, pad_to_len, DIM_HEAD)
        q = split_heads(q) * DIM_HEAD ** (-0.5)
        k = split_heads(k)
        v = split_heads(v)
        num_levels = int(log2(pad_to_len // BLOCK)) - 1
        qkvs = [(q, k, v)]
        for _ in range(num_levels):
            q = q.reshape(q.shape[0], -1, 2, DIM_HEAD).mean(2)
            k = k.reshape(k.shape[0], -1, 2, DIM_HEAD).mean(2)
            v = v.reshape(v.shape[0], -1, 2, DIM_HEAD).sum(2)
            qkvs.append((q, k, v))
        neg_max = -jnp.finfo(x.dtype).max
        idx = jnp.arange(pad_to_len)
        Ysum = jnp.zeros((b * HEADS, pad_to_len, DIM_HEAD), x.dtype)
        Asum = jnp.zeros((b * HEADS, pad_to_len), x.dtype)
        for lvl, (ql, kl, vl) in enumerate(qkvs):
            B = ql.shape[0]
            nb = ql.shape[1] // BLOCK
            ql = ql.reshape(B, nb, BLOCK, DIM_HEAD)
            kl = kl.reshape(B, nb, BLOCK, DIM_HEAD)
            vl = vl.reshape(B, nb, BLOCK, DIM_HEAD)
            if lvl == 0:
                S = jnp.einsum('bnid,bnjd->bnij', ql, kl)
                S = jnp.where(jnp.triu(jnp.ones((BLOCK, BLOCK), bool), 1), neg_max, S)
                S = S - S.max(-1, keepdims=True)
                A = jnp.exp(S)
                y = jnp.einsum('bnij,bnjd->bnid', A, vl).reshape(B, pad_to_len, DIM_HEAD)
                Av = A.sum(-1).reshape(B, pad_to_len)
            else:
                q2 = ql.reshape(B, nb // 2, 2, BLOCK, DIM_HEAD)[:, :, 1]
                k1b = kl.reshape(B, nb // 2, 2, BLOCK, DIM_HEAD)[:, :, 0]
                v1b = vl.reshape(B, nb // 2, 2, BLOCK, DIM_HEAD)[:, :, 0]
                S = jnp.einsum('bnid,bnjd->bnij', q2, k1b)
                S = S - S.max(-1, keepdims=True)
                A = jnp.exp(S)
                y = jnp.einsum('bnij,bnjd->bnid', A, v1b)
                Av = A.sum(-1)
                y = jnp.pad(y[:, :, None], ((0, 0), (0, 0), (1, 0), (0, 0), (0, 0))).reshape(B, -1, DIM_HEAD)
                Av = jnp.pad(Av[:, :, None], ((0, 0), (0, 0), (1, 0), (0, 0))).reshape(B, -1)
                y = jnp.repeat(y, 2 ** lvl, axis=1)
                Av = jnp.repeat(Av, 2 ** lvl, axis=1)
            seq_key = (idx >> lvl << lvl) + (2 ** lvl - 1)
            keep = seq_key <= idx
            Ysum = Ysum + jnp.where(keep[None, :, None], y, 0.0)
            Asum = Asum + jnp.where(keep[None, :], Av, 0.0)
        out = Ysum / (Asum + EPS)[..., None]
        out = out.reshape(b, HEADS, pad_to_len, DIM_HEAD).transpose(0, 2, 1, 3).reshape(b, pad_to_len, HEADS * DIM_HEAD)
        out = out @ w_out.T + b_out
        return out[:, :n]

    def _L3_ffn_ref(x, router_w, w1, w2, shared_gate_up, shared_down, shared_gate_w):
        import jax, jax.numpy as jnp
        import numpy as np
        D = 128
        F = 128
        E = 8
        K = 2
        B, T = (2, 256)

        def _moe_forward(x, router_w, w1, w2, shared_gate_up, shared_down, shared_gate_w):
            b, t, d = x.shape
            xf = x.reshape(-1, d)
            n = xf.shape[0]
            logits = xf @ router_w
            probs = jax.nn.softmax(logits, axis=-1)
            topw, topi = jax.lax.top_k(probs, K)
            combine = jnp.zeros((n, E), dtype=probs.dtype).at[jnp.arange(n)[:, None], topi].add(topw)
            h = jax.nn.silu(jnp.einsum('nd,edf->nef', xf, w1))
            ye = jnp.einsum('nef,efd->ned', h, w2)
            routed = jnp.einsum('ne,ned->nd', combine, ye)
            gu = xf @ shared_gate_up
            gate, up = (gu[:, :F], gu[:, F:])
            shared = jax.nn.silu(gate) * up @ shared_down
            shared = jax.nn.sigmoid(xf @ shared_gate_w) * shared
            return (routed + shared).reshape(b, t, d)
        return _moe_forward(x, router_w, w1, w2, shared_gate_up, shared_down, shared_gate_w)
    x = x + _L0_xattn_ref(ctx_1024, _layernorm(x, axis=-1))
    x = x + _L0_attn_ref(_layernorm(x, axis=-1), L0_attn_w_qkv, L0_attn_b_qkv, L0_attn_w_out, L0_attn_b_out)
    x = x + _L0_ffn_ref(_layernorm(x, axis=-1), L0_ffn_w_gate, L0_ffn_w_up, L0_ffn_w_down)
    x = x + _L1_xattn_ref(_layernorm(x, axis=-1), ctx_1024, mask_BxS2_bf1, L1_xattn_Wq, L1_xattn_Wk, L1_xattn_Wv, L1_xattn_Wo, L1_xattn_bo)
    x = x + _L1_attn_ref(_layernorm(x, axis=-1), L1_attn_Wk, L1_attn_bk, L1_attn_Wv, L1_attn_bv, L1_attn_Wf, L1_attn_bf)
    x = x + _L1_ffn_ref(_layernorm(x, axis=-1), L1_ffn_gate_w, L1_ffn_fc1_w, L1_ffn_fc1_b, L1_ffn_fc2_w, L1_ffn_fc2_b)
    x = x + _L2_xattn_ref(_layernorm(x, axis=-1), ctx_1024, ctx_1024, L2_xattn_w_q, L2_xattn_w_k, L2_xattn_w_v, L2_xattn_w_o)
    x = x + _L2_attn_ref(_layernorm(x, axis=-1), L2_attn_weight)
    x = x + _L2_ffn_ref(_layernorm(x, axis=-1), L2_ffn_w_router, L2_ffn_b_router, L2_ffn_w_experts, L2_ffn_b_experts)
    x = x + _L3_xattn_ref(_layernorm(x, axis=-1), ctx_1024, L3_xattn_Wq, L3_xattn_bq, L3_xattn_Wk, L3_xattn_bk, L3_xattn_Wv, L3_xattn_bv, L3_xattn_Wo, L3_xattn_bo)
    x = x + _L3_attn_ref(_layernorm(x, axis=-1), L3_attn_w_qkv, L3_attn_w_out, L3_attn_b_out)
    x = x + _L3_ffn_ref(_layernorm(x, axis=-1), L3_ffn_router_w, L3_ffn_w1, L3_ffn_w2, L3_ffn_shared_gate_up, L3_ffn_shared_down, L3_ffn_shared_gate_w)
    return x

_drawn_inputs = setup_inputs


def setup_inputs(seed=0):
    import zlib

    import numpy as np

    out = dict(_drawn_inputs(seed))
    spreads = {'L0_attn_b_qkv': (0.0, 0.8),
     'L0_attn_b_out': (0.0, 0.8),
     'L1_xattn_bo': (0.0, 0.8),
     'L1_attn_bk': (0.0, 2.0),
     'L1_attn_bv': (0.0, 0.8),
     'L1_attn_bf': (0.0, 0.8),
     'L1_ffn_fc1_b': (0.0, 0.8),
     'L1_ffn_fc2_b': (0.0, 0.8),
     'L3_xattn_bq': (0.0, 0.8),
     'L3_xattn_bk': (0.0, 2.0),
     'L3_xattn_bv': (0.0, 0.8),
     'L3_xattn_bo': (0.0, 2.0)}
    factors = {'L0_attn_w_qkv': 3.771,
     'L0_attn_w_out': 3.704,
     'L0_ffn_w_gate': 8.0,
     'L0_ffn_w_up': 8.0,
     'L0_ffn_w_down': 8.0,
     'L1_xattn_Wq': 8.0,
     'L1_xattn_Wk': 8.0,
     'L1_xattn_Wv': 8.0,
     'L1_xattn_Wo': 8.0,
     'L1_attn_Wk': 8.0,
     'L1_attn_Wv': 8.0,
     'L1_attn_Wf': 8.0,
     'L1_ffn_gate_w': 8.0,
     'L1_ffn_fc1_w': 8.0,
     'L1_ffn_fc2_w': 8.0,
     'L2_xattn_w_q': 6.956,
     'L2_xattn_w_k': 6.904,
     'L2_xattn_w_v': 2.839,
     'L2_xattn_w_o': 2.797,
     'L2_attn_weight': 8.0,
     'L2_ffn_w_router': 6.566,
     'L2_ffn_b_router': 8.0,
     'L2_ffn_w_experts': 5.75,
     'L2_ffn_b_experts': 8.0,
     'L3_xattn_Wq': 6.83,
     'L3_xattn_Wk': 6.687,
     'L3_xattn_Wv': 5.406,
     'L3_xattn_Wo': 5.378,
     'L3_attn_w_qkv': 8.0,
     'L3_attn_w_out': 8.0,
     'L3_attn_b_out': 64.0,
     'L3_ffn_router_w': 39.168,
     'L3_ffn_w1': 39.542,
     'L3_ffn_w2': 35.861,
     'L3_ffn_shared_gate_up': 21.525,
     'L3_ffn_shared_down': 8.0,
     'L3_ffn_shared_gate_w': 35.96}
    for name, (base, spread) in spreads.items():
        noise = np.random.default_rng([zlib.crc32(name.encode()), seed]).standard_normal(out[name].shape)
        drawn = base * np.exp(spread * noise) if base else spread * noise
        out[name] = jnp.asarray(drawn.astype(out[name].dtype))
    for name, factor in factors.items():
        out[name] = (out[name] * factor).astype(out[name].dtype)
    return out
```

```python
from contextlib import ExitStack

import concourse.bass as bass
from concourse import mybir

FIRST_STAGE, LAST_STAGE = 0, 11

ALU = mybir.AluOpType
ACT = mybir.ActivationFunctionType
F32 = mybir.dt.float32
U8 = mybir.dt.uint8
X = mybir.AxisListType.X
ds = bass.ds

B, S, D = 16, 64, 128
NT = B * S // 128
K = 1601
KC = [(c * 128, min(128, K - c * 128)) for c in range((K + 127) // 128)]
KB = [(c * 512, min(512, K - c * 512)) for c in range((K + 511) // 512)]
H = 16
E = 8
NEG = -1.0e30
LN_EPS = 1e-5
ONE = 1
SEMS = 100


def settle(eng):
    eng.nop(nofuse=True)


class Link:

    def __init__(self, eng, sem, base=0):
        self.eng, self.sem, self.base, self.n = eng, sem, base, 0

    def __call__(self, ins):
        self.n += 1
        ins.then_inc(self.sem, 1)
        self.eng.wait_ge(self.sem, self.base + self.n + ONE)
        if not isinstance(self.base, int):
            settle(self.eng)
        return ins


class Core:

    def __init__(self, nc, ctx, dram):
        self.nc, self.ctx, self.dram, self.n = nc, ctx, dram, 0
        self.pool = [nc.alloc_semaphore(f"stage_sem_{n}") for n in range(SEMS)]
        self.used = 0
        self.credit(self.pool)
        self.x = self.keep("x", [128, NT, D])
        self.xn = self.keep("xn", [128, NT, D])
        self.xnT = self.keep("xnT", [128, NT * 128])
        self.ident = self.keep("ident", [128, 128])
        self.ones = self.keep("ones", [128, 128])
        self.headmask = self.keep("headmask", [128, H])
        self.bias_row = self.keep("bias_row", [128, D])

    def keep(self, name, shape, dt=F32):
        return self.ctx.enter_context(self.nc.sbuf_tensor(name, shape, dt))

    def sem(self, name):
        self.used += 1
        return self.pool[self.used - 1]

    def credit(self, sems):
        for sem in sems:
            self.nc.gpsimd.sem_inc(sem, ONE)
        self.nc.all_engine_barrier()

    def end_stage(self):
        used = self.pool[:self.used]
        for sem in used:
            self.nc.gpsimd.sem_clear(sem)
        self.credit(used)
        self.used = 0

    def sb(self, st, name, shape, dt=F32):
        self.n += 1
        return st.enter_context(self.nc.sbuf_tensor(f"{name}_{self.n}", shape, dt))

    def ps(self, st, name, shape, dt=F32):
        self.n += 1
        return st.enter_context(self.nc.psum_tensor(f"{name}_{self.n}", shape, dt))


def row_bcast(vec, n=128):
    return vec.rearrange("(a d) -> a d", a=1).to_broadcast([n, vec.shape[0]])


def bc(ap, shape):
    return ap.to_broadcast(shape)


def constants(c):
    nc = c.nc
    loaded, made, filled = c.sem("x_loaded"), c.sem("const_made"), c.sem("const_filled")
    with nc.Block() as block:
        @block.sync
        def _(sp):
            sp.dma_start(c.x[:], c.dram["x"].rearrange("(t b) s d -> (b s) t d", b=2)).then_inc(loaded, 16)
            sp.wait_ge(loaded, 16 + ONE)

        @block.gpsimd
        def _(pool):
            pool.memset(c.ident[:], 0.0).then_inc(filled, 1)
            pool.memset(c.ones[:], 1.0).then_inc(filled, 1)
            pool.memset(c.headmask[:], 1.0).then_inc(filled, 1)
            pool.wait_ge(filled, 3 + ONE)
            pool.affine_select(out=c.ident[:], in_=c.ident[:], compare_op=ALU.not_equal, fill=1.0, base=0,
                               pattern=[[-1, 128]], channel_multiplier=1).then_inc(made, 1)
            pool.affine_select(out=c.headmask[:], in_=c.headmask[:], compare_op=ALU.is_ge, fill=0.0, base=0,
                               pattern=[[-8, H]], channel_multiplier=1).then_inc(made, 1)
            pool.wait_ge(made, 2 + ONE)
            pool.affine_select(out=c.headmask[:], in_=c.headmask[:], compare_op=ALU.is_ge, fill=0.0, base=7,
                               pattern=[[8, H]], channel_multiplier=-1).then_inc(made, 1)
            pool.wait_ge(made, 3 + ONE)


def transpose_context(c):
    nc = c.nc
    with ExitStack() as st:
        nat = c.sb(st, "ctx_nat", [128, 2, len(KC), D])
        trn = c.sb(st, "ctx_trn", [128, 2, K])
        pt = [c.ps(st, f"ctx_pt{g}", [128, 512]) for g in range(4)]
        loaded = [c.sem("nat_loaded0"), c.sem("nat_loaded1")]
        turned, copied = c.sem("ctx_turned"), c.sem("ctx_copied")
        stored = [c.sem("trn_stored0"), c.sem("trn_stored1")]
        ctx = c.dram["ctx_1024"]
        with nc.Block() as block:
            def load(sp, b, j):
                n = K // 128
                sp.dma_start(nat[:, j, 0:n, :], ctx[b:b + 1 if isinstance(b, int) else None] if 0 else
                             ctx[ds(b, 1), 0:n * 128, :].rearrange("b (c p) d -> p (b c) d", p=128)
                             ).then_inc(loaded[j], 16)
                sp.dma_start(nat[0:K - n * 128, j, n, :],
                             ctx[ds(b, 1), n * 128:K, :].rearrange("b p d -> p (b d)")).then_inc(loaded[j], 16)

            @block.sync
            def _(sp):
                load(sp, 0, 0)
                load(sp, 1, 1)
                with sp.Fori(0, B // 2 - 1) as i:
                    for j in range(2):
                        sp.wait_ge(turned, (i * 2 + j + 1) * 4 + ONE)
                        settle(sp)
                        load(sp, i * 2 + (2 + j), j)

            @block.tensor
            def _(pe):
                with pe.Fori(0, B // 2) as i:
                    for j in range(2):
                        pe.wait_ge(loaded[j], (i + 1) * 32 + ONE)
                        for g in range(4):
                            pe.wait_ge(copied, (i * 2 + j) * 4 + ONE)
                            for k in range(4 * g, min(4 * g + 4, len(KC))):
                                n = KC[k][1]
                                last = pe.transpose(pt[g][:, (k % 4) * 128:(k % 4) * 128 + n],
                                                    nat[0:n, j, k, :], c.ident[0:n, 0:n])
                            last.then_inc(turned, 1)

            @block.vector
            def _(dve):
                with dve.Fori(0, B // 2) as i:
                    for j in range(2):
                        dve.wait_ge(stored[j], i * 16 + ONE)
                        for g in range(4):
                            o, n = KB[g]
                            dve.wait_ge(turned, (i * 2 + j) * 4 + g + 1 + ONE)
                            dve.tensor_copy(trn[:, j, o:o + n], pt[g][:, 0:n]).then_inc(copied, 1)

            @block.scalar
            def _(act):
                with act.Fori(0, B // 2) as i:
                    for j in range(2):
                        act.wait_ge(copied, (i * 2 + j + 1) * 4 + ONE)
                        act.dma_start(c.ctxT[ds(i * 2 + j, 1)].rearrange("b p k -> p (b k)"),
                                      trn[:, j, :]).then_inc(stored[j], 16)
                for j in range(2):
                    act.wait_ge(stored[j], 16 * (B // 2) + ONE)


def layernorm(c):
    nc = c.nc
    with ExitStack() as st:
        mean = c.sb(st, "ln_mean", [128, NT, 1])
        var = c.sb(st, "ln_var", [128, NT, 1])
        std = c.sb(st, "ln_std", [128, NT, 1])
        inv = c.sb(st, "ln_inv", [128, NT, 1])
        sq = c.sb(st, "ln_sq", [128, NT, D])
        pt = c.ps(st, "ln_pt", [128, NT * 128])
        order, var_ready, std_ready = c.sem("ln_order"), c.sem("ln_var_ready"), c.sem("ln_std_ready")
        xn_ready, turned, done = c.sem("xn_ready"), c.sem("xn_turned"), c.sem("xnT_done")
        with nc.Block() as block:
            @block.vector
            def _(dve):
                link = Link(dve, order)
                link(dve.reduce_sum(mean[:, :, 0], c.x[:], axis=X))
                link(dve.tensor_scalar(mean[:, :, 0], mean[:, :, 0], 1.0 / D, None, ALU.mult))
                link(dve.tensor_tensor(c.xn[:], c.x[:], bc(mean[:], [128, NT, D]), ALU.subtract))
                link(dve.tensor_tensor(sq[:], c.xn[:], c.xn[:], ALU.mult))
                link(dve.reduce_sum(var[:, :, 0], sq[:], axis=X))
                dve.tensor_scalar(var[:, :, 0], var[:, :, 0], 1.0 / D, LN_EPS, ALU.mult, ALU.add
                                  ).then_inc(var_ready, 1)
                dve.wait_ge(std_ready, 1 + ONE)
                link(dve.reciprocal(inv[:, :, 0], std[:, :, 0]))
                dve.tensor_tensor(c.xn[:], c.xn[:], bc(inv[:], [128, NT, D]), ALU.mult).then_inc(xn_ready, 1)
                for h in range(2):
                    dve.wait_ge(turned, h + 1 + ONE)
                    dve.tensor_copy(c.xnT[:, h * 512:h * 512 + 512], pt[:, h * 512:h * 512 + 512]
                                    ).then_inc(done, 1)
                dve.wait_ge(done, 2 + ONE)

            @block.scalar
            def _(act):
                act.wait_ge(var_ready, 1 + ONE)
                act.activation(std[:, :, 0], var[:, :, 0], ACT.Sqrt).then_inc(std_ready, 1)

            @block.tensor
            def _(pe):
                pe.wait_ge(xn_ready, 1 + ONE)
                for t in range(NT):
                    last = pe.transpose(pt[:, t * 128:t * 128 + 128], c.xn[:, t, :], c.ident[:])
                    if t % 4 == 3:
                        last.then_inc(turned, 1)


def load_all(c, pairs):
    nc = c.nc
    loaded = c.sem("loaded")
    with nc.Block() as block:
        @block.sync
        def _(sp):
            for out, src in pairs:
                sp.dma_start(out, src).then_inc(loaded, 16)
            sp.wait_ge(loaded, 16 * len(pairs) + ONE)


def turn_all(c, jobs):
    nc = c.nc
    with ExitStack() as st:
        pt = [c.ps(st, f"turn{j}", [128, 512]) for j in range(2)]
        turned, copied = c.sem("turned"), c.sem("turn_copied")
        with nc.Block() as block:
            @block.tensor
            def _(pe):
                for n, (out, src) in enumerate(jobs):
                    if n >= 2:
                        pe.wait_ge(copied, n - 1 + ONE)
                    p, f = src.shape
                    pe.transpose(pt[n % 2][0:f, 0:p], src, c.ident[0:p, 0:p]).then_inc(turned, 1)

            @block.vector
            def _(dve):
                for n, (out, src) in enumerate(jobs):
                    p, f = src.shape
                    dve.wait_ge(turned, n + 1 + ONE)
                    dve.tensor_copy(out, pt[n % 2][0:f, 0:p]).then_inc(copied, 1)
                dve.wait_ge(copied, len(jobs) + ONE)


def multiply_all(c, jobs):
    nc = c.nc
    with ExitStack() as st:
        pm = [c.ps(st, f"mul{j}", [128, 512]) for j in range(2)]
        summed, copied = c.sem("summed"), c.sem("sum_copied")
        with nc.Block() as block:
            @block.tensor
            def _(pe):
                for n, (out, terms) in enumerate(jobs):
                    if n >= 2:
                        pe.wait_ge(copied, n - 1 + ONE)
                    p, f = out.shape
                    for k, (lhsT, rhs) in enumerate(terms):
                        last = pe.matmul(pm[n % 2][0:p, 0:f], lhsT, rhs, start=(k == 0),
                                         stop=(k == len(terms) - 1))
                    last.then_inc(summed, 1)

            @block.vector
            def _(dve):
                for n, (out, terms) in enumerate(jobs):
                    p, f = out.shape
                    dve.wait_ge(summed, n + 1 + ONE)
                    dve.tensor_copy(out, pm[n % 2][0:p, 0:f]).then_inc(copied, 1)
                dve.wait_ge(copied, len(jobs) + ONE)


def head_blocks(c, st, lhsT, rhs, out):
    nc = c.nc
    spread = c.sb(st, "spread", [128, H, D])
    spread_done = c.sem("spread_done")
    with nc.Block() as block:
        @block.vector
        def _(dve):
            for h in range(H):
                dve.tensor_scalar(spread[:, h, :], rhs, c.headmask[:, h:h + 1], None, ALU.mult
                                  ).then_inc(spread_done, 1)
            dve.wait_ge(spread_done, H + ONE)
    flat_in = spread[:].rearrange("p h d -> p (h d)")
    flat_out = out.rearrange("p h d -> p (h d)")
    multiply_all(c, [(flat_out[:, n:n + 512], [(lhsT, flat_in[:, n:n + 512])]) for n in range(0, H * D, 512)])


def cross_attention(c, M, N, scale, masked=False, topk=None):
    nc = c.nc
    TB = H // 2
    with ExitStack() as st:
        ctxT = c.sb(st, "ctxT", [128, 2, K])
        ctxN = c.sb(st, "ctxN", [128, 2, len(KC), D])
        stat = c.sb(st, "stat", [128, H, S])
        P = c.sb(st, "P", [128, 2, K])
        PT = c.sb(st, "PT", [128, 2, len(KC), 128])
        UT = c.sb(st, "UT", [128, TB, 128])
        U = c.sb(st, "U", [128, 2, 128])
        mx = c.sb(st, "mx", [128, 2])
        ls = c.sb(st, "ls", [128, 2])
        li = c.sb(st, "li", [128, 2])
        if masked or topk:
            SS = c.sb(st, "SS", [128, 2, K])
        if masked:
            mask8 = c.sb(st, "mask8", [128, 2, K], U8)
            maskf = c.sb(st, "maskf", [128, 2, K])
        if topk:
            KT = c.sb(st, "KT", [128, K])
            top = c.sb(st, "top", [128, 4, 8])
            EX = c.sb(st, "EX", [128, K])
        psS = c.ps(st, "psS", [128, 2048])
        psT = c.ps(st, "psT", [128, 2, 512])
        psU = c.ps(st, "psU", [128, 512])
        psZ = c.ps(st, "psZ", [128, 512])

        loaded = [c.sem("ctx_loaded0"), c.sem("ctx_loaded1")]
        qp_ready, stat_ready = c.sem("qp_ready"), c.sem("stat_ready")
        kp_ready, kt_ready = c.sem("kp_ready"), c.sem("kt_ready")
        scores_ready, max_ready, exp_done = c.sem("scores_ready"), c.sem("max_ready"), c.sem("exp_done")
        p_ready = c.sem("p_ready") if topk else exp_done
        score_free = exp_done if not (masked or topk) else max_ready
        turned, pt_ready = c.sem("turned"), c.sem("pt_ready")
        u_ready, li_ready, us_ready = c.sem("u_ready"), c.sem("li_ready"), c.sem("us_ready")
        ut_turned, ut_ready = c.sem("ut_turned"), c.sem("ut_ready")
        y_ready, x_done, order = c.sem("y_ready"), c.sem("x_done"), c.sem("order")
        LOADS = 16 * (4 if masked else 3)

        with nc.Block() as block:
            def load(sp, b, j):
                n = K // 128
                sp.dma_start(ctxT[:, j, :], c.ctxT[ds(b, 1)].rearrange("b p k -> p (b k)")).then_inc(loaded[j], 16)
                sp.dma_start(ctxN[:, j, 0:n, :], c.dram["ctx_1024"][ds(b, 1), 0:n * 128, :].rearrange(
                    "b (c p) d -> p (b c) d", p=128)).then_inc(loaded[j], 16)
                sp.dma_start(ctxN[0:K - n * 128, j, n, :], c.dram["ctx_1024"][ds(b, 1), n * 128:K, :].rearrange(
                    "b p d -> p (b d)")).then_inc(loaded[j], 16)
                if masked:
                    sp.dma_start(mask8[:, j, :], c.dram["mask_BxS2_bf1"][ds(b, 1)].to_broadcast([128, K])
                                 ).then_inc(loaded[j], 16)

            @block.sync
            def _(sp):
                load(sp, 0, 0)
                load(sp, 1, 1)
                with sp.Fori(0, B // 2 - 1) as i:
                    for j in range(2):
                        sp.wait_ge(y_ready, i * 2 + (j + 1) + ONE)
                        settle(sp)
                        if masked:
                            sp.wait_ge(max_ready, (i * 2 + (j + 1)) * TB + ONE)
                        settle(sp)
                        load(sp, i * 2 + (2 + j), j)

            @block.tensor
            def _(pe):
                with pe.Fori(0, B // 2) as i:
                    for j in range(2):
                        b = i * 2 + j
                        g = b * TB

                        def scores(n):
                            pe.wait_ge(score_free, g + n + ONE)
                            src = KT[:] if topk else ctxT[:, j, :]
                            for o, w in KB:
                                last = pe.matmul(psS[:, o:o + w], stat[:, 2 * n:2 * n + 2, :], src[:, o:o + w],
                                                 start=True, stop=True)
                            last.then_inc(scores_ready, 1)

                        def values(n):
                            pe.wait_ge(p_ready, g + (n + 1) + ONE)
                            for q in range(4):
                                if q >= 2:
                                    pe.wait_ge(pt_ready, (g + n) * 4 + (q - 1) + ONE)
                                elif n or q == 1:
                                    pe.wait_ge(pt_ready, (g + n) * 4 + ONE)
                                else:
                                    pe.wait_ge(pt_ready, g * 4 + ONE)
                                for k in range(4 * q, min(4 * q + 4, len(KC))):
                                    o, w = KC[k]
                                    last = pe.transpose(psT[0:w, q % 2, (k % 4) * 128:(k % 4) * 128 + 128],
                                                        P[:, n % 2, o:o + w], c.ident[:])
                                last.then_inc(turned, 1)
                            pe.wait_ge(us_ready, g + n + ONE)
                            for k, (o, w) in enumerate(KC):
                                if k % 4 == 0:
                                    pe.wait_ge(pt_ready, (g + n) * 4 + (k // 4 + 1) + ONE)
                                last = pe.matmul(psU[:, 0:128], PT[0:w, n % 2, k, :], ctxN[0:w, j, k, :],
                                                 start=(k == 0), stop=(k == len(KC) - 1))
                            last.then_inc(u_ready, 1)

                        def turn_u(n):
                            pe.wait_ge(us_ready, g + (n + 1) + ONE)
                            pe.wait_ge(ut_ready, g + n + ONE)
                            pe.transpose(psZ[:, 0:128], U[:, n % 2, :], c.ident[:]).then_inc(ut_turned, 1)

                        pe.wait_ge(loaded[j], (i + 1) * LOADS + ONE)
                        if topk:
                            QT, WkT, bk = topk
                            pe.wait_ge(score_free, g + ONE)
                            for o, w in KB:
                                last = pe.matmul(psS[:, o:o + w], WkT, ctxT[:, j, o:o + w], start=True, stop=True)
                            last.then_inc(kp_ready, 1)
                            pe.wait_ge(kt_ready, b + 1 + ONE)
                        else:
                            pe.wait_ge(pt_ready, g * 4 + ONE)
                            for h in range(H):
                                last = pe.matmul(psT[:, h // 8, (h % 8) * S:(h % 8) * S + S], M[:, h, :],
                                                 c.xnT[:, ds(b * S, S)], start=True, stop=True)
                            last.then_inc(qp_ready, 1)
                        pe.wait_ge(stat_ready, b + 1 + ONE)
                        for n in range(TB + 2):
                            if n < TB:
                                scores(n)
                            if 1 <= n <= TB:
                                values(n - 1)
                            if n >= 2:
                                turn_u(n - 2)
                        pe.wait_ge(ut_ready, g + TB + ONE)
                        pe.wait_ge(x_done, b + ONE)
                        for h in range(H):
                            last = pe.matmul(psZ[j * S:j * S + S, 128:256], UT[:, h // 2, (h % 2) * S:(h % 2) * S + S],
                                             N[:, h, :], start=(h == 0), stop=(h == H - 1))
                        last.then_inc(y_ready, 1)

            @block.scalar
            def _(act):
                with act.Fori(0, B // 2) as i:
                    for j in range(2):
                        b = i * 2 + j
                        g = b * TB
                        if topk:
                            act.wait_ge(kp_ready, b + 1 + ONE)
                            act.activation(KT[:], psS[:, 0:K], ACT.Identity, bias=topk[2]).then_inc(kt_ready, 1)
                        else:
                            act.wait_ge(qp_ready, b + 1 + ONE)
                            act.activation(stat[:].rearrange("p h s -> p (h s)"),
                                           psT[:].rearrange("p a b -> p (a b)"), ACT.Copy, scale=scale
                                           ).then_inc(stat_ready, 1)

                        def exps(n):
                            act.wait_ge(max_ready, g + (n + 1) + ONE)
                            if not topk:
                                act.wait_ge(u_ready, g + (n - 1 if n else 0) + ONE)
                            src = SS[:, n % 2, :] if masked else psS[:, 0:K]
                            if topk:
                                src = SS[:, 0, :]
                            act.activation(EX[:] if topk else P[:, n % 2, :], src, ACT.Exp,
                                           bias=mx[:, n % 2:n % 2 + 1],
                                           **({} if topk else {"accum_out": ls[:, n % 2:n % 2 + 1]})
                                           ).then_inc(exp_done, 1)

                        def norm(n):
                            act.wait_ge(u_ready, g + (n + 1) + ONE)
                            act.wait_ge(li_ready, g + (n + 1) + ONE)
                            act.wait_ge(ut_turned, g + (n - 1 if n else 0) + ONE)
                            act.activation(U[:, n % 2, :], psU[:, 0:128], ACT.Copy,
                                           scale=li[:, n % 2:n % 2 + 1]).then_inc(us_ready, 1)

                        for n in range(TB + 1):
                            if n < TB:
                                exps(n)
                            if n >= 1:
                                norm(n - 1)

            @block.vector
            def _(dve):
                with dve.Fori(0, B // 2) as i:
                    for j in range(2):
                        b = i * 2 + j
                        g = b * TB
                        link = Link(dve, order, b * LINKS_XA[bool(masked) + 2 * bool(topk)])
                        if masked:
                            dve.wait_ge(loaded[j], (i + 1) * LOADS + ONE)
                            link(dve.tensor_copy(maskf[:, j, :], mask8[:, j, :]))
                            link(dve.tensor_scalar(maskf[:, j, :], maskf[:, j, :], -1.0, -NEG, ALU.add, ALU.mult))
                        if topk:
                            dve.wait_ge(scores_ready, g + ONE)
                            last = dve.tensor_tensor(
                                stat[:], bc(topk[0][:, ds(b * S, S)].rearrange("p (a s) -> p a s", a=1), [128, H, S]),
                                bc(c.headmask[:].rearrange("p (h a) -> p h a", a=1), [128, H, S]), ALU.mult)
                            last.then_inc(stat_ready, 1)

                        def maxima(n):
                            m = mx[:, n % 2:n % 2 + 1]
                            dve.wait_ge(scores_ready, g + (n + 1) + ONE)
                            if topk:
                                link(dve.tensor_copy(SS[:, 0, :], psS[:, 0:K]))
                                link(dve.max(top[:, 0, :], SS[:, 0, :]))
                                dve.tensor_scalar(m, top[:, 0, 0:1], -1.0, None, ALU.mult).then_inc(max_ready, 1)
                                link(dve.match_replace(SS[:, 1, :], top[:, 0, :], SS[:, 0, :], -3.0e38))
                                for r in range(1, 4):
                                    link(dve.max(top[:, r, :], SS[:, 1, :]))
                                    link(dve.match_replace(SS[:, 1, :], top[:, r, :], SS[:, 1, :], -3.0e38))
                                dve.wait_ge(exp_done, g + (n + 1) + ONE)
                                dve.wait_ge(u_ready, g + (n - 1 if n else 0) + ONE)
                                dve.scalar_tensor_tensor(out=P[:, n % 2, :], in0=SS[:, 1, :], scalar=-3.0e38,
                                                         in1=EX[:], op0=ALU.is_equal, op1=ALU.mult,
                                                         accum_out=ls[:, n % 2:n % 2 + 1]).then_inc(p_ready, 1)
                                return
                            if masked:
                                dve.wait_ge(exp_done, g + (n - 1 if n else 0) + ONE)
                                settle(dve)
                                link(dve.tensor_tensor_reduce(out=SS[:, n % 2, :], in0=psS[:, 0:K],
                                                              in1=maskf[:, j, :], scale=1.0, scalar=NEG * 4,
                                                              op0=ALU.add, op1=ALU.max, accum_out=m))
                                dve.tensor_scalar(m, m, -1.0, None, ALU.mult).then_inc(max_ready, 1)
                            else:
                                dve.wait_ge(exp_done, g + (n - 1 if n else 0) + ONE)
                                dve.tensor_reduce(m, psS[:, 0:K], X, ALU.max, negate=True).then_inc(max_ready, 1)

                        def copies(n):
                            for q in range(4):
                                w = len(KC) - 12 if q == 3 else 4
                                p = KC[-1][1] if q == 3 else 128
                                dve.wait_ge(turned, (g + n) * 4 + (q + 1) + ONE)
                                dve.tensor_copy(PT[0:p, n % 2, 4 * q:4 * q + w, :],
                                                psT[0:p, q % 2, 0:w * 128].rearrange("p (k t) -> p k t", t=128)
                                                ).then_inc(pt_ready, 1)
                            dve.wait_ge(p_ready, g + (n + 1) + ONE)
                            dve.wait_ge(us_ready, g + (n - 1 if n else 0) + ONE)
                            dve.reciprocal(li[:, n % 2:n % 2 + 1], ls[:, n % 2:n % 2 + 1]).then_inc(li_ready, 1)

                        def copy_ut(n):
                            dve.wait_ge(ut_turned, g + (n + 1) + ONE)
                            dve.tensor_copy(UT[:, n, :], psZ[:, 0:128]).then_inc(ut_ready, 1)

                        for n in range(TB + 2):
                            if n < TB:
                                maxima(n)
                            if 1 <= n <= TB:
                                copies(n - 1)
                            if n >= 2:
                                copy_ut(n - 2)
                        dve.wait_ge(y_ready, b + 1 + ONE)
                        r = slice(j * S, j * S + S)
                        xt = c.x[r, ds(i, 1), :].rearrange("p a d -> p (a d)")
                        link(dve.tensor_tensor(xt, xt, psZ[r, 128:256], ALU.add))
                        dve.tensor_tensor(xt, xt, c.bias_row[r, :], ALU.add).then_inc(x_done, 1)
                        assert link.n == LINKS_XA[bool(masked) + 2 * bool(topk)], link.n
                dve.wait_ge(x_done, B + ONE)


LINKS_XA = [1, 11, 1 + 8 * 9]


def zero_bias(c):
    nc = c.nc
    z = c.sem("bias_zero")
    with nc.Block() as block:
        @block.gpsimd
        def _(pool):
            pool.memset(c.bias_row[:], 0.0).then_inc(z, 1)
            pool.wait_ge(z, 1 + ONE)


def wide_cross_attention(c, wq, wk, wv, wo, bo, scale, masked):
    with ExitStack() as st:
        M = c.sb(st, "M", [128, H, D])
        N = c.sb(st, "N", [128, H, D])
        with ExitStack() as s2:
            w = [c.sb(s2, f"w{n}", [128, 8, 128]) for n in range(4)]
            wT = [c.sb(s2, f"wT{n}", [128, 8, 128]) for n in range(3)]
            loads = [(w[n][:].rearrange("p a b -> p (a b)"), a) for n, a in enumerate((wq, wk, wv))]
            loads.append((w[3][:], wo.rearrange("(a p) d -> p a d", p=128)))
            if bo is not None:
                loads.append((c.bias_row[:], row_bcast(bo)))
            load_all(c, loads)
            if bo is None:
                zero_bias(c)
            turn_all(c, [(wT[n][:, a, :], w[n][:, a, :]) for n in range(3) for a in range(8)])

            def half(t, h):
                return t[(h % 2) * 64:(h % 2) * 64 + 64, h // 2, :]

            multiply_all(c, [(M[:, h, :], [(half(wT[0], h), half(wT[1], h))]) for h in range(H)]
                         + [(N[:, h, :], [(half(wT[2], h), half(w[3], h))]) for h in range(H)])
        cross_attention(c, M, N, scale, masked=masked)


def stage_l1_xattn(c):
    d = c.dram
    layernorm(c)
    wide_cross_attention(c, d["L1_xattn_Wq"], d["L1_xattn_Wk"], d["L1_xattn_Wv"], d["L1_xattn_Wo"],
                         d["L1_xattn_bo"], 0.125, True)


def stage_l2_xattn(c):
    d = c.dram
    layernorm(c)
    wide_cross_attention(c, d["L2_xattn_w_q"], d["L2_xattn_w_k"], d["L2_xattn_w_v"], d["L2_xattn_w_o"],
                         None, 0.125, False)


def stage_l3_xattn(c):
    nc, d = c.nc, c.dram
    layernorm(c)
    with ExitStack() as st:
        N = c.sb(st, "N3", [128, H, D])
        QT = c.sb(st, "QT", [128, B * S])
        WT = c.sb(st, "WT", [128, 3, D])
        bias = c.sb(st, "biases", [128, 3])
        with ExitStack() as s2:
            W = c.sb(s2, "W", [128, 4, D])
            WvN = c.sb(s2, "WvN", [128, D])
            bo = c.sb(s2, "bo", [128, D])
            bv_row = c.sb(s2, "bv_row", [128, 128])
            load_all(c, [(W[:, 0, :], d["L3_xattn_Wq"]), (W[:, 1, :], d["L3_xattn_Wk"]),
                         (W[:, 2, :], d["L3_xattn_Wo"]), (WvN[:], d["L3_xattn_Wv"]),
                         (bo[:], row_bcast(d["L3_xattn_bo"]))]
                     + [(bias[:, n:n + 1], d[f"L3_xattn_{v}"].rearrange("(p a) -> p a", a=1))
                        for n, v in enumerate(("bq", "bk", "bv"))])
            turn_all(c, [(WT[:, n, :], W[:, n, :]) for n in range(3)])
            head_blocks(c, s2, WvN[:], WT[:, 2, :], N)
            spread_bias(c, bias[:, 2:3], WT[:, 2, :], bo)
            project(c, QT, WT[:, 0, :], c.xnT, bias[:, 0:1], 8.0 ** -0.5)
        cross_attention(c, None, N, None, topk=(QT, WT[:, 1, :], bias[:, 1:2]))


def spread_bias(c, col, w, bo):
    nc = c.nc
    with ExitStack() as st:
        cols = c.sb(st, "bias_cols", [128, 128])
        pb = c.ps(st, "bias_ps", [128, D])
        made, summed, done = c.sem("cols_made"), c.sem("bias_summed"), c.sem("bias_done")
        with nc.Block() as block:
            @block.vector
            def _(dve):
                dve.tensor_scalar(cols[:], c.ones[:], col, None, ALU.mult).then_inc(made, 1)
                dve.wait_ge(summed, 1 + ONE)
                if bo is None:
                    dve.tensor_copy(c.bias_row[:], pb[:]).then_inc(done, 1)
                else:
                    dve.tensor_tensor(c.bias_row[:], pb[:], bo[:], ALU.add).then_inc(done, 1)
                dve.wait_ge(done, 1 + ONE)

            @block.tensor
            def _(pe):
                pe.wait_ge(made, 1 + ONE)
                pe.matmul(pb[:], cols[:], w, start=True, stop=True).then_inc(summed, 1)


def project(c, out, w, src, bias, scale):
    nc = c.nc
    with ExitStack() as st:
        pp = c.ps(st, "proj", [128, B * S])
        summed, done = c.sem("proj_summed"), c.sem("proj_done")
        with nc.Block() as block:
            @block.tensor
            def _(pe):
                for n in range(0, B * S, 512):
                    pe.matmul(pp[:, n:n + 512], w, src[:, n:n + 512], start=True, stop=True).then_inc(summed, 1)

            @block.vector
            def _(dve):
                dve.wait_ge(summed, B * S // 512 + ONE)
                if bias is None:
                    dve.tensor_scalar(out[:], pp[:], scale, None, ALU.mult).then_inc(done, 1)
                else:
                    dve.tensor_scalar(out[:], pp[:], bias, scale, ALU.add, ALU.mult).then_inc(done, 1)
                dve.wait_ge(done, 1 + ONE)


def attention_masks(c, st, kind):
    nc = c.nc
    mask = c.sb(st, "mask", [128, 1, S])
    flag = c.sb(st, "flag", [128, 1])
    order = c.sem("mask_order")
    with nc.Block() as block:
        @block.gpsimd
        def _(pool):
            link = Link(pool, order)
            link(pool.memset(mask[:], 0.0))
            link(pool.memset(flag[:], 1.0))
            for b in range(2):
                m = mask[b * S:b * S + S, 0, :]
                link(pool.affine_select(out=m, in_=m, compare_op=ALU.is_ge, fill=NEG, base=0,
                                        pattern=[[-1, S]], channel_multiplier=1))
                if kind == "h":
                    for k in range(0, S, 16):
                        mk = mask[b * S:b * S + S, 0, k:k + 16]
                        link(pool.affine_select(out=mk, in_=mk, compare_op=ALU.is_ge, fill=NEG, base=k + 15,
                                                pattern=[[0, 16]], channel_multiplier=-1))
                    f = flag[b * S:b * S + S, :]
                    link(pool.affine_select(out=f, in_=f, compare_op=ALU.is_ge, fill=0.0, base=-S // 2,
                                            pattern=[[0, 1]], channel_multiplier=1))
            if kind == "h":
                for e in range(0, 128, 2):
                    link(pool.affine_select(out=flag[:], in_=flag[:], compare_op=ALU.not_equal, fill=0.0,
                                            base=-e, pattern=[[0, 1]], channel_multiplier=1))
    return mask, flag


LINKS_SA = {"l0": 11, "l1": 7, "l2": 5, "h": 17}


def small_attention(c, kind, W, Wq=None, bq=None, Wk=None, bk=None, M=None, scale=1.0, bv_row=None, Wf=None):
    nc = c.nc
    V = 32 if kind == "l1" else D
    with ExitStack() as st:
        mask, flag = attention_masks(c, st, kind) if kind != "l2" else (None, None)
        xs = c.sb(st, "xs", [128, 128])
        qT = c.sb(st, "qT", [128, 128])
        kT = c.sb(st, "kT", [128, 128])
        Kb = c.sb(st, "Kb", [128, 2, H, S])
        Sm = c.sb(st, "Sm", [128, H, S])
        mx = c.sb(st, "mx", [128, H, 1])
        sm = c.sb(st, "sm", [128, H, 1])
        Pn = c.sb(st, "Pn", [128, H, S])
        PT = c.sb(st, "PT", [128, 8, 128])
        VW = c.sb(st, "VW", [128, 2, 8, 2 if kind == "l1" else 1, V])
        if kind == "l0":
            Ksq = c.sb(st, "Ksq", [128, 2, H, S])
            hmx = c.sb(st, "hmx", [128, H, S])
            qsq = c.sb(st, "qsq", [128, 128])
            qm2 = c.sb(st, "qm2", [128, 128])
        if kind == "l1":
            G = c.sb(st, "G", [128, 512])
            GT = c.sb(st, "GT", [128, 4, 128])
        if kind == "h":
            qh = c.sb(st, "qh", [128, H, 128])
            qc = c.sb(st, "qc", [128, H, 64, 2])
            xc = c.sb(st, "xc", [128, 2, 16])
            A1 = c.sb(st, "A1", [128, H, 16])
            mx1 = c.sb(st, "mx1", [128, H, 1])
            sm1 = c.sb(st, "sm1", [128, H, 1])
        psS = c.ps(st, "psS", [128, 2, 512])
        psD = c.ps(st, "psD", [128, 2, 512])
        psW = c.ps(st, "psW", [128, 2048])
        order, xs_ready, proj_ready, qk_ready = (c.sem(n) for n in ("order", "xs_ready", "proj_ready", "qk_ready"))
        kb_ready, s_ready, sq_ready = c.sem("kb_ready"), c.sem("s_ready"), c.sem("sq_ready")
        sub_ready, e_ready, pn_ready = c.sem("sub_ready"), c.sem("e_ready"), c.sem("pn_ready")
        v_ready, vw_ready, turned, pt_ready = (c.sem(n) for n in ("v_ready", "vw_ready", "turned", "pt_ready"))
        o_ready, g_ready, g_turned, gt_ready = (c.sem(n) for n in ("o_ready", "g_ready", "g_turned", "gt_ready"))
        x_done, pool_order, y_ready, o_added = (c.sem(n) for n in ("x_done", "pool_order", "y_ready", "o_added"))
        heads = 1 if kind == "l1" else H
        W2 = W.rearrange("p (a b) v -> p b a v", b=2)

        if kind in ("l0", "l1"):
            zeroed = c.sem("zeroed")
            with nc.Block() as block:
                @block.vector
                def _(dve):
                    if kind == "l1":
                        dve.memset(VW[:], 0.0).then_inc(zeroed, 1)
                    else:
                        dve.tensor_copy(hmx[:], bc(c.headmask[:].rearrange("p (h a) -> p h a", a=1), [128, H, S])
                                        ).then_inc(zeroed, 1)
                    dve.wait_ge(zeroed, 1 + ONE)

        with nc.Block() as block:
            @block.vector
            def _(dve):
                with dve.Fori(0, NT) as p:
                    link = Link(dve, order, p * LINKS_SA[kind])
                    dve.tensor_copy(xs[:], c.xnT[:, ds(p * 128, 128)]).then_inc(xs_ready, 1)
                    dve.wait_ge(xs_ready, p + 1 + ONE)
                    settle(dve)
                    if kind == "l0":
                        dve.wait_ge(proj_ready, p + 1 + ONE)
                        link(dve.tensor_scalar(qT[:], psW[:, 0:128], bq, None, ALU.add))
                        link(dve.tensor_tensor(qsq[:], qT[:], qT[:], ALU.mult))
                        link(dve.tensor_scalar(qm2[:], qT[:], -2.0, None, ALU.mult))
                        dve.tensor_scalar(kT[:], psW[:, 512:640], bk, None, ALU.add).then_inc(qk_ready, 1)
                    elif kind == "l1":
                        dve.wait_ge(proj_ready, p + 1 + ONE)
                        link(dve.tensor_copy(qT[:], xs[:]))
                        dve.tensor_scalar(kT[:], psW[:, 512:640], bk, None, ALU.add).then_inc(qk_ready, 1)
                    elif kind == "l2":
                        link(dve.tensor_scalar(qT[:], xs[:], scale, None, ALU.mult))
                        dve.tensor_copy(kT[:], xs[:]).then_inc(qk_ready, 1)
                    else:
                        for b in range(2):
                            pair = xs[:, b * S:b * S + 32].rearrange("p (a b) -> p a b", b=2)
                            link(dve.tensor_tensor(xc[:, b, :], pair[:, :, 0], pair[:, :, 1], ALU.add))
                        link(dve.tensor_scalar(xc[:], xc[:], 0.5, None, ALU.mult))
                        dve.wait_ge(proj_ready, p + 1 + ONE)
                        link(dve.tensor_scalar(qh[:].rearrange("p h t -> p (h t)"), psW[:], scale, None, ALU.mult))
                        pair = qh[:].rearrange("p h (a b) -> p h a b", b=2)
                        link(dve.tensor_tensor(qc[:, :, :, 0], pair[:, :, :, 0], pair[:, :, :, 1], ALU.add))
                        link(dve.tensor_scalar(qc[:, :, :, 0], qc[:, :, :, 0], 0.5, None, ALU.mult))
                        dve.tensor_copy(qc[:, :, :, 1], qc[:, :, :, 0]).then_inc(qk_ready, 1)

                    dve.wait_ge(s_ready, p + 1 + ONE)
                    scores = psS[:].rearrange("p a (h k) -> p (a h) k", k=S)
                    if kind == "l0":
                        link(dve.tensor_scalar(Sm[:].rearrange("p h k -> p (h k)"),
                                               psD[:].rearrange("p a b -> p (a b)"), 1e-6, None, ALU.add))
                        link(dve.reciprocal(Sm[:], Sm[:]))
                        dve.wait_ge(sq_ready, p + 1 + ONE)
                        link(dve.tensor_tensor(Sm[:], Sm[:], Pn[:], ALU.mult))
                        scores = Sm[:]
                    if kind != "l2":
                        link(dve.tensor_tensor(Sm[:], scores, bc(mask[:], [128, H, S]), ALU.add))
                        scores = Sm[:]
                    link(dve.reduce_max(mx[:, :, 0], scores, axis=X))
                    dve.tensor_tensor(Sm[:], scores, bc(mx[:], [128, H, S]), ALU.subtract).then_inc(sub_ready, 1)
                    if kind == "h":
                        s1 = psD[:, 0, 0:256].rearrange("p (h k) -> p h k", k=16)
                        link(dve.reduce_max(mx1[:, :, 0], s1, axis=X))
                        dve.tensor_tensor(A1[:], s1, bc(mx1[:], [128, H, 16]), ALU.subtract).then_inc(sub_ready, 1)
                    dve.wait_ge(e_ready, (p + 1) * (2 if kind == "h" else 1) + ONE)
                    link(dve.reduce_sum(sm[:, :, 0], Pn[:], axis=X))
                    if kind == "h":
                        link(dve.reduce_sum(sm1[:, :, 0], A1[:], axis=X))
                        link(dve.tensor_scalar(sm1[:], sm1[:], flag[:], 1e-8, ALU.mult, ALU.add))
                        link(dve.tensor_tensor(sm[:], sm[:], sm1[:], ALU.add))
                        pairs = Pn[:, :, 0:32].rearrange("p h (a b) -> p h a b", b=2)
                        for e in range(2):
                            link(dve.scalar_tensor_tensor(out=pairs[:, :, :, e], in0=A1[:], scalar=flag[:],
                                                          in1=pairs[:, :, :, e], op0=ALU.mult, op1=ALU.add))
                    link(dve.reciprocal(sm[:, :, 0], sm[:, :, 0]))
                    dve.tensor_tensor(Pn[:], Pn[:], bc(sm[:], [128, H, S]), ALU.mult).then_inc(pn_ready, 1)
                    dve.wait_ge(turned, p + 1 + ONE)
                    dve.tensor_copy(PT[:].rearrange("p a t -> p (a t)"), psW[:, 0:1024]).then_inc(pt_ready, 1)
                    dve.wait_ge(o_ready, p + 1 + ONE)
                    xt = c.x[:, ds(p, 1), :].rearrange("p a d -> p (a d)")
                    if kind == "l1":
                        dve.tensor_tensor(G[:], psS[:, 0, :], bv_row, ALU.add).then_inc(o_added, 1)
                        dve.wait_ge(g_turned, p + 1 + ONE)
                        dve.tensor_copy(GT[:].rearrange("p a t -> p (a t)"), psW[:, 0:512]).then_inc(gt_ready, 1)
                        dve.wait_ge(y_ready, p + 1 + ONE)
                        link(dve.tensor_tensor(xt, xt, psS[:, 1, 0:128], ALU.add))
                        link(dve.tensor_tensor(xt, xt, c.xn[:, ds(p, 1), :].rearrange("p a d -> p (a d)"), ALU.add))
                    else:
                        link(dve.tensor_tensor(xt, xt, psS[:, 0, 0:128], ALU.add))
                    dve.tensor_tensor(xt, xt, c.bias_row[:], ALU.add).then_inc(x_done, 1)
                    assert link.n == LINKS_SA[kind], (kind, link.n)
                dve.wait_ge(x_done, NT + ONE)

            @block.gpsimd
            def _(pool):
                if kind == "h":
                    return
                with pool.Fori(0, NT) as p:
                    pool.wait_ge(qk_ready, p + 1 + ONE)
                    for b in range(2):
                        pool.tensor_tensor(
                            Kb[:, b], bc(kT[:, b * S:b * S + S].rearrange("p (a s) -> p a s", a=1), [128, H, S]),
                            bc(c.headmask[:].rearrange("p (h a) -> p h a", a=1), [128, H, S]), ALU.mult
                            ).then_inc(pool_order, 1)
                    if kind == "l0":
                        pool.wait_ge(pool_order, p * 2 + 2 + ONE)
                        pool.tensor_tensor(Ksq[:], Kb[:], Kb[:], ALU.mult).then_inc(kb_ready, 1)

            @block.scalar
            def _(act):
                with act.Fori(0, NT) as p:
                    for b in range(2):
                        act.wait_ge(v_ready, p * 2 + b + 1 + ONE)
                        if kind == "l1":
                            for e in range(2):
                                r = slice(e * 64, e * 64 + 64)
                                last = act.activation(VW[r, b, :, e, :],
                                                      psW[r, 1024:1280].rearrange("p (a v) -> p a v", v=V), ACT.Copy)
                        else:
                            last = act.activation(VW[:, b].rearrange("p a c v -> p (a c v)"), psW[:, 1024:2048],
                                                  ACT.Copy)
                        last.then_inc(vw_ready, 1)
                    if kind == "l0":
                        act.wait_ge(s_ready, p + 1 + ONE)
                        act.activation(Pn[:].rearrange("p h k -> p (h k)"), psS[:].rearrange("p a b -> p (a b)"),
                                       ACT.Square).then_inc(sq_ready, 1)
                    act.wait_ge(sub_ready, p * (2 if kind == "h" else 1) + 1 + ONE)
                    act.activation(Pn[:], Sm[:], ACT.Exp).then_inc(e_ready, 1)
                    if kind == "h":
                        act.wait_ge(sub_ready, p * 2 + 2 + ONE)
                        act.activation(A1[:], A1[:], ACT.Exp).then_inc(e_ready, 1)
                    if kind == "l1":
                        act.wait_ge(o_added, p + 1 + ONE)
                        act.activation(G[:], G[:], ACT.Gelu).then_inc(g_ready, 1)

            @block.tensor
            def _(pe):
                with pe.Fori(0, NT) as p:
                    pe.wait_ge(xs_ready, p + 1 + ONE)
                    if kind == "l0":
                        pe.matmul(psW[:, 0:128], Wq, xs[:], start=True, stop=True)
                    if kind in ("l0", "l1"):
                        pe.matmul(psW[:, 512:640], Wk, xs[:], start=True, stop=True).then_inc(proj_ready, 1)
                    if kind == "h":
                        for h in range(H):
                            last = pe.matmul(psW[:, h * 128:h * 128 + 128], M[:, h, :], xs[:], start=True, stop=True)
                        last.then_inc(proj_ready, 1)
                    pe.wait_ge(qk_ready, p + 1 + ONE)
                    if kind != "h":
                        pe.wait_ge(pool_order, p * 2 + 2 + ONE)
                    if kind == "l0":
                        pe.wait_ge(kb_ready, p + 1 + ONE)
                    pe.wait_ge(x_done, p + ONE)
                    for b in range(2):
                        r = slice(b * S, b * S + S)
                        if kind == "h":
                            for h in range(H):
                                pe.matmul(psS[r, h // 8, (h % 8) * S:(h % 8) * S + S], qh[:, h, r], xs[:, r],
                                          start=True, stop=True)
                                last = pe.matmul(psD[r, 0, h * 16:h * 16 + 16],
                                                 qc[:].rearrange("p h a b -> p h (a b)")[:, h, r],
                                                 xc[:, b, :], start=True, stop=True)
                            continue
                        for n in range(2):
                            hs = slice(8 * n, 8 * n + 8)
                            last = pe.matmul(psS[r, n, :], qT[:, r], Kb[:, b, hs, :], start=True, stop=True)
                            if kind == "l0":
                                pe.matmul(psD[r, n, :], c.ones[:, 0:S], Ksq[:, b, hs, :], start=True, stop=False)
                                pe.matmul(psD[r, n, :], qsq[:, r], hmx[:, hs, :], start=False, stop=False)
                                last = pe.matmul(psD[r, n, :], qm2[:, r], Kb[:, b, hs, :], start=False, stop=True)
                    last.then_inc(s_ready, 1)
                    for b in range(2):
                        pe.wait_ge(vw_ready, p * 2 + b + ONE)
                        for e in range(2):
                            for n in range(0, 8 * V, 512):
                                w = min(512, 8 * V)
                                hs = slice(n // V, (n + w) // V)
                                last = pe.matmul(psW[e * 64:e * 64 + 64, 1024 + n:1024 + n + w],
                                                 xs[:, b * S:b * S + S], W2[:, e, hs, :], start=True, stop=True)
                        last.then_inc(v_ready, 1)
                    pe.wait_ge(pn_ready, p + 1 + ONE)
                    for a in range(8):
                        last = pe.transpose(psW[:, a * 128:a * 128 + 128],
                                            Pn[:, 2 * a:2 * a + 2, :].rearrange("p h k -> p (h k)"), c.ident[:])
                    last.then_inc(turned, 1)
                    pe.wait_ge(pt_ready, p + 1 + ONE)
                    pe.wait_ge(vw_ready, p * 2 + 2 + ONE)
                    for b in range(2):
                        r = slice(b * S, b * S + S)
                        for a in range(8):
                            if kind == "l1":
                                last = pe.matmul(psS[r, 0, a * 64:a * 64 + 64], PT[:, a, r],
                                                 VW[:, b, a].rearrange("p c v -> p (c v)"), start=True, stop=True)
                            else:
                                last = pe.matmul(psS[r, 0, 0:128], PT[:, a, r], VW[:, b, a, 0, :],
                                                 start=(a == 0), stop=(a == 7))
                    last.then_inc(o_ready, 1)
                    if kind == "l1":
                        pe.wait_ge(g_ready, p + 1 + ONE)
                        for a in range(4):
                            last = pe.transpose(psW[:, a * 128:a * 128 + 128], G[:, a * 128:a * 128 + 128], c.ident[:])
                        last.then_inc(g_turned, 1)
                        pe.wait_ge(gt_ready, p + 1 + ONE)
                        for a in range(4):
                            last = pe.matmul(psS[:, 1, 0:128], GT[:, a, :], Wf[:, a, :], start=(a == 0), stop=(a == 3))
                        last.then_inc(y_ready, 1)


def stage_l0_attn(c):
    d = c.dram
    layernorm(c)
    with ExitStack() as st:
        W = c.sb(st, "W", [128, H, D])
        Wqkv = c.sb(st, "Wqkv", [128, 3, D])
        bias = c.sb(st, "bias", [128, 3])
        with ExitStack() as s2:
            Wo = c.sb(s2, "Wo", [128, D])
            bo = c.sb(s2, "bo", [128, D])
            WvT = c.sb(s2, "WvT", [128, D])
            load_all(c, [(Wqkv[:].rearrange("p a d -> p (a d)"), d["L0_attn_w_qkv"]), (Wo[:], d["L0_attn_w_out"]),
                         (bo[:], row_bcast(d["L0_attn_b_out"]))]
                     + [(bias[:, n:n + 1], d["L0_attn_b_qkv"][n * D:n * D + D].rearrange("(p a) -> p a", a=1))
                        for n in range(3)])
            turn_all(c, [(WvT[:], Wqkv[:, 2, :])])
            head_blocks(c, s2, WvT[:], Wo[:], W)
            spread_bias(c, bias[:, 2:3], Wo[:], bo)
        small_attention(c, "l0", W[:], Wq=Wqkv[:, 0, :], bq=bias[:, 0:1], Wk=Wqkv[:, 1, :], bk=bias[:, 1:2])


def stage_l1_attn(c):
    d = c.dram
    layernorm(c)
    with ExitStack() as st:
        W = c.sb(st, "W", [128, H, 32])
        Wk = c.sb(st, "Wk", [128, D])
        bk = c.sb(st, "bk", [128, 1])
        bv = c.sb(st, "bv", [128, 512])
        Wf = c.sb(st, "Wf", [128, 4, D])
        load_all(c, [(W[:].rearrange("p h v -> p (h v)"), d["L1_attn_Wv"]), (Wk[:], d["L1_attn_Wk"]),
                     (bk[:], d["L1_attn_bk"].rearrange("(p a) -> p a", a=1)), (bv[:], row_bcast(d["L1_attn_bv"])),
                     (Wf[:], d["L1_attn_Wf"].rearrange("(a p) d -> p a d", p=128)),
                     (c.bias_row[:], row_bcast(d["L1_attn_bf"]))])
        small_attention(c, "l1", W[:], Wk=Wk[:], bk=bk[:], bv_row=bv[:], Wf=Wf)


def stage_l2_attn(c):
    d = c.dram
    layernorm(c)
    with ExitStack() as st:
        W = c.sb(st, "W", [128, H, D])
        load_all(c, [(W[:], d["L2_attn_weight"].rearrange("(h p) d -> p h d", p=128))])
        zero_bias(c)
        small_attention(c, "l2", W[:], scale=8.0 ** -0.5)


def stage_l3_attn(c):
    d = c.dram
    layernorm(c)
    with ExitStack() as st:
        M = c.sb(st, "M", [128, H, D])
        W = c.sb(st, "W", [128, H, D])
        with ExitStack() as s2:
            w = c.sb(s2, "w", [128, 3, 8, D])
            wo = c.sb(s2, "wo", [128, 8, 128])
            woT = c.sb(s2, "woT", [128, 8, 128])
            load_all(c, [(w[:].rearrange("p q a d -> p (q a) d"),
                          d["L3_attn_w_qkv"].rearrange("(a p) d -> p a d", p=128)),
                         (wo[:].rearrange("p a b -> p (a b)"), d["L3_attn_w_out"]),
                         (c.bias_row[:], row_bcast(d["L3_attn_b_out"]))])
            turn_all(c, [(woT[:, a, :], wo[:, a, :]) for a in range(8)])

            def half(t, h):
                return t[(h % 2) * 64:(h % 2) * 64 + 64, h // 2, :]

            multiply_all(c, [(M[:, h, :], [(half(w[:, 0], h), half(w[:, 1], h))]) for h in range(H)]
                         + [(W[:, h, :], [(half(w[:, 2], h), half(woT, h))]) for h in range(H)])
        small_attention(c, "h", W[:], M=M, scale=0.125)


def route(c, st, Wr, br, weights, cap=None):
    nc = c.nc
    coef = c.sb(st, "coef", [128, NT, E])
    with ExitStack() as s:
        p = c.sb(s, "p", [128, NT, E])
        rest = c.sb(s, "rest", [128, NT, E])
        first = c.sb(s, "first", [128, 2, NT, E])
        rank = c.sb(s, "rank", [128, NT, E])
        m = c.sb(s, "m", [128, 2, NT, 1])
        r = c.sb(s, "r", [128, NT, 1])
        tri = c.sb(s, "tri", [128, 128])
        off = c.sb(s, "off", [128, 2, NT + 1, E])
        ps = c.ps(s, "logits", [128, NT * E])
        pc = c.ps(s, "counts", [128, 4, NT * E])
        made, order, logits, sub, expd = (c.sem(n) for n in ("made", "order", "logits", "sub", "expd"))
        picked, counted, done = c.sem("picked"), c.sem("counted"), c.sem("done")
        with nc.Block() as block:
            @block.gpsimd
            def _(pool):
                link = Link(pool, made)
                link(pool.iota(rank[:], pattern=[[0, NT], [-1, E]], base=E, channel_multiplier=0,
                               allow_small_or_imprecise_dtypes=True))
                link(pool.memset(tri[:], 1.0))
                link(pool.affine_select(out=tri[:], in_=tri[:], compare_op=ALU.is_ge, fill=0.0, base=0,
                                        pattern=[[1, 128]], channel_multiplier=-1))

            @block.tensor
            def _(pe):
                for t in range(NT):
                    last = pe.matmul(ps[:, t * E:t * E + E], c.xnT[:, t * 128:t * 128 + 128], Wr,
                                     start=True, stop=True)
                last.then_inc(logits, 1)
                if cap:
                    pe.wait_ge(picked, 1 + ONE)
                    pe.wait_ge(made, 3 + ONE)
                    for k in range(2):
                        f = first[:, k].rearrange("p t e -> p (t e)")
                        pe.matmul(pc[:, k, :], tri[:], f, start=True, stop=True)
                        last = pe.matmul(pc[:, 2 + k, :], c.ones[:], f, start=True, stop=True)
                    last.then_inc(counted, 1)

            @block.scalar
            def _(act):
                act.wait_ge(sub, 1 + ONE)
                act.activation(p[:], p[:], ACT.Exp).then_inc(expd, 1)

            @block.vector
            def _(dve):
                link = Link(dve, order)
                dve.wait_ge(logits, 1 + ONE)
                link(dve.tensor_copy(p[:].rearrange("p t e -> p (t e)"), ps[:]))
                if br is not None:
                    link(dve.tensor_tensor(p[:], p[:], bc(br, [128, NT, E]), ALU.add))
                link(dve.reduce_max(r[:, :, 0], p[:], axis=X))
                dve.tensor_tensor(p[:], p[:], bc(r[:], [128, NT, E]), ALU.subtract).then_inc(sub, 1)
                dve.wait_ge(expd, 1 + ONE)
                link(dve.reduce_sum(r[:, :, 0], p[:], axis=X))
                link(dve.reciprocal(r[:, :, 0], r[:, :, 0]))
                link(dve.tensor_tensor(p[:], p[:], bc(r[:], [128, NT, E]), ALU.mult))
                link(dve.tensor_copy(rest[:], p[:]))
                dve.wait_ge(made, 3 + ONE)
                for k in range(2):
                    f = first[:, k]
                    link(dve.reduce_max(m[:, k, :, 0], rest[:], axis=X))
                    link(dve.tensor_tensor(f, rest[:], bc(m[:, k], [128, NT, E]), ALU.is_equal))
                    link(dve.tensor_tensor(f, f, rank[:], ALU.mult))
                    link(dve.reduce_max(r[:, :, 0], f, axis=X))
                    link(dve.tensor_tensor(f, f, bc(r[:], [128, NT, E]), ALU.is_equal))
                    if k == 0:
                        link(dve.scalar_tensor_tensor(out=rest[:], in0=f, scalar=-2.0, in1=rest[:],
                                                      op0=ALU.mult, op1=ALU.add))
                if cap:
                    link(dve.tensor_tensor(r[:], m[:, 0], m[:, 1], ALU.add))
                    link(dve.reciprocal(r[:, :, 0], r[:, :, 0]))
                    link(dve.tensor_tensor(p[:], p[:], bc(r[:], [128, NT, E]), ALU.mult))
                    dve.memset(off[:, 0, 0, :], 0.0).then_inc(picked, 1)
                    dve.wait_ge(counted, 1 + ONE)
                    for k in range(2):
                        if k:
                            link(dve.tensor_copy(off[:, 1, 0, :], off[:, 0, NT, :]))
                        for t in range(NT):
                            link(dve.tensor_tensor(off[:, k, t + 1, :], off[:, k, t, :],
                                                   pc[:, 2 + k, t * E:t * E + E], ALU.add))
                        link(dve.tensor_tensor(rest[:].rearrange("p t e -> p (t e)"),
                                               off[:, k, 0:NT, :].rearrange("p t e -> p (t e)"),
                                               pc[:, k, :], ALU.add))
                        link(dve.tensor_scalar(rest[:], rest[:], float(cap), None, ALU.is_le))
                        link(dve.tensor_tensor(first[:, k], first[:, k], rest[:], ALU.mult))
                link(dve.tensor_tensor(coef[:], first[:, 0], first[:, 1], ALU.add))
                if weights != "one":
                    link(dve.tensor_tensor(coef[:], coef[:], p[:], ALU.mult))
    return coef


def add_expert_bias(c, coef, b):
    nc = c.nc
    with ExitStack() as st:
        cT = c.sb(st, "coefT", [E, NT, 128])
        pb = c.ps(st, "pb", [128, NT, 128])
        summed, added = c.sem("bias_summed"), c.sem("bias_added")
        turn_all(c, [(cT[:, t, :], coef[:, t, :]) for t in range(NT)])
        with nc.Block() as block:
            @block.tensor
            def _(pe):
                for t in range(NT):
                    last = pe.matmul(pb[:, t, :], cT[:, t, :], b, start=True, stop=True)
                last.then_inc(summed, 1)

            @block.vector
            def _(dve):
                dve.wait_ge(summed, 1 + ONE)
                dve.tensor_tensor(c.x[:], c.x[:], pb[:], ALU.add).then_inc(added, 1)
                dve.wait_ge(added, 1 + ONE)


def experts(c, coef, w1, w2, C, func, b1=None):
    nc = c.nc
    turn = b1 is not None
    with ExitStack() as st:
        w1n = c.sb(st, "w1n", [128, 2, C, 128])
        w2n = c.sb(st, "w2n", [128, 2, C, 128])
        w1T = c.sb(st, "w1T", [128, 2, C, 128]) if turn else w1n
        hT = c.sb(st, "hT", [128, 2, C, 512])
        ce = c.sb(st, "ce", [128, 2, NT])
        be = c.sb(st, "be", [128, 2, C])
        psH = c.ps(st, "psH", [128, C, 512])
        psY = c.ps(st, "psY", [128, 2, 512])
        psX = c.ps(st, "psX", [128, 512])
        loaded = [c.sem("w_loaded0"), c.sem("w_loaded1")]
        w1_turned, w1_ready, coef_ready = c.sem("w1_turned"), c.sem("w1_ready"), c.sem("coef_ready")
        h_ready, h_done, y_ready, y_used = (c.sem(n) for n in ("h_ready", "h_done", "y_ready", "y_used"))
        with nc.Block() as block:
            def load(sp, e, j):
                sp.dma_start(w1n[:, j], w1[ds(e, 1)].rearrange("e (c p) d -> p (e c) d", p=128)
                             ).then_inc(loaded[j], 16)
                sp.dma_start(w2n[:, j], w2[ds(e, 1)].rearrange("e (c p) d -> p (e c) d", p=128)
                             ).then_inc(loaded[j], 16)

            @block.sync
            def _(sp):
                load(sp, 0, 0)
                load(sp, 1, 1)
                with sp.Fori(0, E // 2 - 1) as i:
                    for j in range(2):
                        sp.wait_ge(y_ready, i * 4 + (2 * j + 2) + ONE)
                        settle(sp)
                        load(sp, i * 2 + (2 + j), j)

            @block.tensor
            def _(pe):
                with pe.Fori(0, E // 2) as i:
                    def up(k):
                        j, half = k // 2, k % 2
                        if half == 0:
                            pe.wait_ge(loaded[j], (i + 1) * 32 + ONE)
                            if turn:
                                for q in range(C):
                                    last = pe.transpose(psX[:, q * 128:q * 128 + 128], w1n[:, j, q, :], c.ident[:])
                                last.then_inc(w1_turned, 1)
                                pe.wait_ge(w1_ready, i * 2 + (j + 1) + ONE)
                        pe.wait_ge(h_done, (i * 4 + k) * C + ONE)
                        for q in range(C):
                            pe.matmul(psH[:, q, :], w1T[:, j, q, :], c.xnT[:, half * 512:half * 512 + 512],
                                      start=True, stop=True).then_inc(h_ready, 1)

                    def down(k):
                        j = k // 2
                        pe.wait_ge(h_done, (i * 4 + k + 1) * C + ONE)
                        pe.wait_ge(y_used, i * 4 + (k - 1 if k else 0) + ONE)
                        for t in range(4):
                            for q in range(C):
                                last = pe.matmul(psY[:, k % 2, t * 128:t * 128 + 128],
                                                 hT[:, k % 2, q, t * 128:t * 128 + 128], w2n[:, j, q, :],
                                                 start=(q == 0), stop=(q == C - 1))
                        last.then_inc(y_ready, 1)

                    for k in range(5):
                        if k < 4:
                            up(k)
                        if k:
                            down(k - 1)

            @block.scalar
            def _(act):
                with act.Fori(0, E // 2) as i:
                    for k in range(4):
                        j = k // 2
                        if k % 2 == 0:
                            act.wait_ge(coef_ready, i * 2 + (j + 1) + ONE)
                        act.wait_ge(y_ready, i * 4 + (k - 1 if k else 0) + ONE)
                        for q in range(C):
                            act.wait_ge(h_ready, (i * 4 + k) * C + (q + 1) + ONE)
                            act.activation(hT[:, k % 2, q, :], psH[:, q, :], func,
                                           bias=be[:, j, q:q + 1] if turn else 0.0).then_inc(h_done, 1)

            @block.vector
            def _(dve):
                with dve.Fori(0, E // 2) as i:
                    def prepare(j):
                        dve.wait_ge(y_used, i * 4 + ONE)
                        dve.wait_ge(h_done, i * (4 * C) + ONE)
                        if turn:
                            dve.tensor_copy(be[:, j, :], b1[:, ds(i * 2 + j, 1), :].rearrange("p a q -> p (a q)"))
                        dve.tensor_copy(ce[:, j, :], coef[:, :, ds(i * 2 + j, 1)].rearrange("p t a -> p (t a)")
                                        ).then_inc(coef_ready, 1)
                        if turn:
                            dve.wait_ge(w1_turned, i * 2 + (j + 1) + ONE)
                            dve.tensor_copy(w1T[:, j].rearrange("p q d -> p (q d)"), psX[:, 0:C * 128]
                                            ).then_inc(w1_ready, 1)

                    def add(k):
                        j, half = k // 2, k % 2
                        dve.wait_ge(coef_ready, i * 2 + (j + 1) + ONE)
                        dve.wait_ge(y_used, i * 4 + k + ONE)
                        dve.wait_ge(y_ready, i * 4 + (k + 1) + ONE)
                        for t in range(4):
                            tt = half * 4 + t
                            last = dve.scalar_tensor_tensor(
                                out=c.x[:, tt, :], in0=psY[:, k % 2, t * 128:t * 128 + 128],
                                scalar=ce[:, j, tt:tt + 1], in1=c.x[:, tt, :], op0=ALU.mult, op1=ALU.add)
                        last.then_inc(y_used, 1)

                    prepare(0)
                    add(0)
                    prepare(1)
                    for k in range(1, 4):
                        add(k)
                dve.wait_ge(y_used, 2 * E + ONE)


def stage_l1_ffn(c):
    d = c.dram
    layernorm(c)
    with ExitStack() as st:
        b1 = c.sb(st, "b1", [128, E, 4])
        b2 = c.sb(st, "b2", [E, D])
        Wr = c.sb(st, "Wr", [128, E])
        with ExitStack() as s2:
            g = c.sb(s2, "g", [E, D])
            b1n = c.sb(s2, "b1n", [32, 128])
            load_all(c, [(g[:], d["L1_ffn_gate_w"]), (b1n[:], d["L1_ffn_fc1_b"].rearrange("e a (q p) -> (e a q) p", p=128)),
                         (b2[:], d["L1_ffn_fc2_b"].rearrange("e a d -> (e a) d"))])
            turn_all(c, [(Wr[:], g[:]), (b1[:].rearrange("p e q -> p (e q)"), b1n[:])])
        cap = 2 * ((B * S + E - 1) // E)
        coef = route(c, st, Wr[:], None, "share", cap)
        add_expert_bias(c, coef, b2[:])
        experts(c, coef, d["L1_ffn_fc1_w"], d["L1_ffn_fc2_w"], 4, ACT.Relu, b1=b1)


def stage_l2_ffn(c):
    nc, d = c.nc, c.dram
    layernorm(c)
    with ExitStack() as st:
        Wr = c.sb(st, "Wr", [128, E])
        br = c.sb(st, "br", [128, 1, E])
        be = c.sb(st, "be", [E, D])
        g = c.sb(st, "g", [E, D])
        We = c.sb(st, "We", [128, E, D])
        WeT = c.sb(st, "WeT", [128, E, D])
        load_all(c, [(g[:], d["L2_ffn_w_router"]), (br[:, 0, :], row_bcast(d["L2_ffn_b_router"])),
                     (be[:], d["L2_ffn_b_experts"]), (We[:], d["L2_ffn_w_experts"].rearrange("e o d -> o e d"))])
        turn_all(c, [(Wr[:], g[:])] + [(WeT[:, e, :], We[:, e, :]) for e in range(E)])
        coef = route(c, st, Wr[:], br[:], "one")
        add_expert_bias(c, coef, be[:])
        ps = c.ps(st, "psE", [128, 2, E * D])
        made, used = c.sem("made"), c.sem("used")
        flat = WeT[:].rearrange("p e d -> p (e d)")
        with nc.Block() as block:
            @block.tensor
            def _(pe):
                for t in range(NT):
                    if t >= 2:
                        pe.wait_ge(used, E * (t - 1) + ONE)
                    for n in range(0, E * D, 512):
                        last = pe.matmul(ps[:, t % 2, n:n + 512], c.xnT[:, t * 128:t * 128 + 128],
                                         flat[:, n:n + 512], start=True, stop=True)
                    last.then_inc(made, 1)

            @block.vector
            def _(dve):
                for t in range(NT):
                    dve.wait_ge(made, t + 1 + ONE)
                    for e in range(E):
                        dve.scalar_tensor_tensor(out=c.x[:, t, :], in0=ps[:, t % 2, e * D:e * D + D],
                                                 scalar=coef[:, t, e:e + 1], in1=c.x[:, t, :],
                                                 op0=ALU.mult, op1=ALU.add).then_inc(used, 1)
                        dve.wait_ge(used, E * t + e + 1 + ONE)


def stage_l3_ffn(c):
    nc, d = c.nc, c.dram
    layernorm(c)
    with ExitStack() as st:
        Wr = c.sb(st, "Wr", [128, E])
        load_all(c, [(Wr[:], d["L3_ffn_router_w"])])
        coef = route(c, st, Wr[:], None, "prob")
        experts(c, coef, d["L3_ffn_w1"], d["L3_ffn_w2"], 1, ACT.Silu)
        gu = c.sb(st, "gu", [128, 2, 128])
        down = c.sb(st, "down", [128, D])
        gw = c.sb(st, "gw", [128, 1])
        gate = c.sb(st, "gate", [128, B * S])
        sg = c.sb(st, "sg", [128, NT])
        psG = c.ps(st, "psG", [128, B * S])
        psUp = c.ps(st, "psUp", [128, B * S])
        psY = c.ps(st, "psY", [128, NT, D])
        psg = c.ps(st, "psg", [128, NT])
        made, gated, ready, summed, done = (c.sem(n) for n in ("made", "gated", "ready", "summed", "done"))
        load_all(c, [(gu[:].rearrange("p a f -> p (a f)"), d["L3_ffn_shared_gate_up"]),
                     (down[:], d["L3_ffn_shared_down"]), (gw[:], d["L3_ffn_shared_gate_w"])])
        with nc.Block() as block:
            @block.tensor
            def _(pe):
                for n in range(0, B * S, 512):
                    pe.matmul(psG[:, n:n + 512], gu[:, 0, :], c.xnT[:, n:n + 512], start=True, stop=True)
                    pe.matmul(psUp[:, n:n + 512], gu[:, 1, :], c.xnT[:, n:n + 512], start=True, stop=True)
                for t in range(NT):
                    last = pe.matmul(psg[:, t:t + 1], c.xnT[:, t * 128:t * 128 + 128], gw[:], start=True, stop=True)
                last.then_inc(made, 1)
                pe.wait_ge(ready, 1 + ONE)
                for t in range(NT):
                    last = pe.matmul(psY[:, t, :], gate[:, t * 128:t * 128 + 128], down[:], start=True, stop=True)
                last.then_inc(summed, 1)

            @block.scalar
            def _(act):
                act.wait_ge(made, 1 + ONE)
                act.activation(gate[:], psG[:], ACT.Silu).then_inc(gated, 1)
                act.activation(sg[:], psg[:], ACT.Sigmoid).then_inc(gated, 1)

            @block.vector
            def _(dve):
                dve.wait_ge(gated, 2 + ONE)
                dve.tensor_tensor(gate[:], gate[:], psUp[:], ALU.mult).then_inc(ready, 1)
                dve.wait_ge(summed, 1 + ONE)
                for t in range(NT):
                    last = dve.scalar_tensor_tensor(out=c.x[:, t, :], in0=psY[:, t, :], scalar=sg[:, t:t + 1],
                                                    in1=c.x[:, t, :], op0=ALU.mult, op1=ALU.add)
                last.then_inc(done, 1)
                dve.wait_ge(done, 1 + ONE)


def quantize(dve, link, v, a, q, s, r):
    shape = list(v.shape)
    link(dve.tensor_reduce(s[:, :, 0], v, X, ALU.max, apply_absolute_value=True))
    link(dve.tensor_scalar(s, s, 1.0 / 6.0, 1e-12, ALU.mult, ALU.max))
    link(dve.reciprocal(r, s))
    link(dve.tensor_tensor(v, v, bc(r, shape), ALU.mult))
    link(dve.scalar_tensor_tensor(out=a, in0=v, scalar=-1.0, in1=v, op0=ALU.mult, op1=ALU.max))
    link(dve.tensor_scalar(q, a, 5.0, 2.0, ALU.is_gt, ALU.mult))
    for mid in (3.5, 2.5):
        link(dve.scalar_tensor_tensor(out=q, in0=a, scalar=mid, in1=q, op0=ALU.is_gt, op1=ALU.add))
    link(dve.tensor_scalar(q, q, 2.0, None, ALU.mult))
    for mid in (1.75, 1.25, 0.75, 0.25):
        link(dve.scalar_tensor_tensor(out=q, in0=a, scalar=mid, in1=q, op0=ALU.is_gt, op1=ALU.add))
    link(dve.tensor_scalar(v, v, 0.0, -0.5, ALU.is_ge, ALU.add))
    link(dve.tensor_tensor(v, v, q, ALU.mult))
    link(dve.tensor_tensor(v, v, bc(s, shape), ALU.mult))


def stage_l0_ffn(c):
    nc, d = c.nc, c.dram
    I = 352
    IC = [(0, 128), (128, 128), (256, 96)]
    layernorm(c)
    with ExitStack() as st:
        wT = c.sb(st, "wT", [128, 2, I])
        wdT = c.sb(st, "wdT", [128, 3, D])
        h = c.sb(st, "h", [128, NT, I])
        u = c.sb(st, "u", [128, NT, I])
        a = c.sb(st, "a", [128, NT * I // 16, 16])
        q = c.sb(st, "q", [128, NT * I // 16, 16])
        s = c.sb(st, "s", [128, NT * I // 16, 1])
        r = c.sb(st, "r", [128, NT * I // 16, 1])
        xqT = c.sb(st, "xqT", [128, NT, 128])
        hT = c.sb(st, "hT", [128, 3, NT, 128])
        w = c.sb(st, "w", [128, 2, 3, D])
        wd = c.sb(st, "wd", [128, I])
        wl = [(w[0:n, g, k, :], d[name][o:o + n, :]) for g, name in enumerate(("L0_ffn_w_gate", "L0_ffn_w_up"))
              for k, (o, n) in enumerate(IC)]
        load_all(c, wl + [(wd[:], d["L0_ffn_w_down"])])

        def quantize_all(parts):
            order = c.sem("quant_order")
            with nc.Block() as block:
                @block.vector
                def _(dve):
                    link = Link(dve, order)
                    for v in parts:
                        p, n = v.shape[0], v.shape[1]
                        quantize(dve, link, v, a[0:p, 0:n, :], q[0:p, 0:n, :], s[0:p, 0:n, :], r[0:p, 0:n, :])

        quantize_all([c.xn[:].rearrange("p t (n b) -> p (t n) b", b=16), wd[:].rearrange("p (n b) -> p n b", b=16)]
                     + [v.rearrange("p (n b) -> p n b", b=16) for v, _ in wl])
        turn_all(c, [(xqT[:, t, :], c.xn[:, t, :]) for t in range(NT)]
                 + [(wT[:, g, o:o + n], w[0:n, g, k, :]) for g in range(2) for k, (o, n) in enumerate(IC)]
                 + [(wdT[0:n, k, :], wd[:, o:o + n]) for k, (o, n) in enumerate(IC)])
        with ExitStack() as s2:
            pg = c.ps(s2, "pg", [128, 2, 512])
            pu = c.ps(s2, "pu", [128, 2, 512])
            made, silu, used = c.sem("made"), c.sem("silu"), c.sem("used")
            with nc.Block() as block:
                @block.tensor
                def _(pe):
                    for t in range(NT):
                        if t >= 2:
                            pe.wait_ge(used, t - 1 + ONE)
                        pe.matmul(pg[:, t % 2, 0:I], xqT[:, t, :], wT[:, 0, :], start=True, stop=True)
                        pe.matmul(pu[:, t % 2, 0:I], xqT[:, t, :], wT[:, 1, :], start=True, stop=True
                                  ).then_inc(made, 1)

                @block.scalar
                def _(act):
                    for t in range(NT):
                        act.wait_ge(made, t + 1 + ONE)
                        act.activation(u[:, t, :], pg[:, t % 2, 0:I], ACT.Silu).then_inc(silu, 1)

                @block.vector
                def _(dve):
                    for t in range(NT):
                        dve.wait_ge(silu, t + 1 + ONE)
                        dve.tensor_tensor(h[:, t, :], u[:, t, :], pu[:, t % 2, 0:I], ALU.mult).then_inc(used, 1)
                    dve.wait_ge(used, NT + ONE)
        quantize_all([h[:].rearrange("p t (n b) -> p (t n) b", b=16)])
        turn_all(c, [(hT[0:n, k, t, :], h[:, t, o:o + n]) for k, (o, n) in enumerate(IC) for t in range(NT)])
        py = c.ps(st, "py", [128, NT, D])
        summed, added = c.sem("summed"), c.sem("added")
        with nc.Block() as block:
            @block.tensor
            def _(pe):
                for t in range(NT):
                    for k, (o, n) in enumerate(IC):
                        last = pe.matmul(py[:, t, :], hT[0:n, k, t, :], wdT[0:n, k, :], start=(k == 0), stop=(k == 2))
                last.then_inc(summed, 1)

            @block.vector
            def _(dve):
                dve.wait_ge(summed, 1 + ONE)
                dve.tensor_tensor(c.x[:], c.x[:], py[:], ALU.add).then_inc(added, 1)
                dve.wait_ge(added, 1 + ONE)


BIG = 1.0e30


def stage_l0_xattn(c):
    nc = c.nc
    layernorm(c)
    dist = nc.dram_tensor("dist_scratch", [NT, 128, K], F32, kind="Internal").ap()
    cost = nc.dram_tensor("cost_scratch", [B, S + 1, K], F32, kind="Internal").ap()
    step = nc.dram_tensor("step_scratch", [B, S, K], F32, kind="Internal").ap()
    hi_dram = nc.dram_tensor("hi_scratch", [B * S], F32, kind="Internal").ap()
    lo_dram = nc.dram_tensor("lo_scratch", [B * S], F32, kind="Internal").ap()
    distances(c, dist)
    accumulate_costs(c, dist.rearrange("t (b s) k -> (t b) s k", b=2), cost)
    with ExitStack() as st:
        iota1 = c.sb(st, "iota1", [128, K])
        lows = c.sb(st, "lows", [128, NT, K])
        choose_steps(c, cost, step, iota1, lows)
        trace_back(c, step, iota1, hi_dram)
        look_up_lows(c, iota1, lows, hi_dram, lo_dram)
    add_aligned(c, hi_dram, lo_dram)


def distances(c, dist):
    nc = c.nc
    with ExitStack() as st:
        ctxT = c.sb(st, "ctxT", [128, 2, K])
        ctxsq = c.sb(st, "ctxsq", [128, 2, K])
        xm2 = c.sb(st, "xm2", [128, 128])
        dd = c.sb(st, "dd", [128, 2, K])
        sq = c.sb(st, "sq", [128, NT, D])
        bb = c.sb(st, "bb", [128, NT])
        bcur = c.sb(st, "bcur", [128, 1])
        psD = c.ps(st, "psD", [128, 2048])
        loaded = [c.sem("loaded0"), c.sem("loaded1")]
        order, xm2_ready, sq_ready, made, clamped = (c.sem(n) for n in ("order", "xm2", "sq", "made", "clamped"))
        rooted, stored = c.sem("rooted"), c.sem("stored")
        with nc.Block() as block:
            @block.sync
            def _(sp):
                for j in range(2):
                    sp.dma_start(ctxT[:, j, :], c.ctxT[j]).then_inc(loaded[j], 16)
                with sp.Fori(0, NT - 1) as i:
                    sp.wait_ge(made, i + 1 + ONE)
                    settle(sp)
                    for j in range(2):
                        sp.dma_start(ctxT[:, j, :], c.ctxT[ds(i * 2 + (2 + j), 1)].rearrange("b p k -> p (b k)")
                                     ).then_inc(loaded[j], 16)

            @block.tensor
            def _(pe):
                with pe.Fori(0, NT) as i:
                    pe.wait_ge(xm2_ready, i + 1 + ONE)
                    pe.wait_ge(sq_ready, i * 2 + 2 + ONE)
                    for j in range(2):
                        pe.wait_ge(loaded[j], i * 16 + 16 + ONE)
                    for j in range(2):
                        r = slice(j * S, j * S + S)
                        for o, w in KB:
                            pe.matmul(psD[r, o:o + w], xm2[:, r], ctxT[:, j, o:o + w], start=True, stop=False)
                            last = pe.matmul(psD[r, o:o + w], c.ones[:, 0:S], ctxsq[:, j, o:o + w],
                                             start=False, stop=True)
                    last.then_inc(made, 1)

            @block.vector
            def _(dve):
                link = Link(dve, order)
                link(dve.tensor_tensor(sq[:], c.xn[:], c.xn[:], ALU.mult))
                link(dve.reduce_sum(bb[:], sq[:], axis=X))
                with dve.Fori(0, NT) as i:
                    link = Link(dve, order, i + 2)
                    dve.tensor_scalar(xm2[:], c.xnT[:, ds(i * 128, 128)], -2.0, None, ALU.mult).then_inc(xm2_ready, 1)
                    link(dve.tensor_copy(bcur[:], bb[:, ds(i, 1)]))
                    dve.wait_ge(rooted, i + ONE)
                    dve.wait_ge(made, i + 1 + ONE)
                    dve.tensor_scalar(dd[:, 0, :], psD[:, 0:K], bcur[:], 0.0, ALU.add, ALU.max).then_inc(clamped, 1)
                    dve.wait_ge(clamped, i + 1 + ONE)
                    settle(dve)

            @block.scalar
            def _(act):
                with act.Fori(0, NT) as i:
                    act.wait_ge(made, i + ONE)
                    for j in range(2):
                        act.wait_ge(loaded[j], i * 16 + 16 + ONE)
                        act.activation(ctxsq[:, j, :], ctxT[:, j, :], ACT.Square).then_inc(sq_ready, 1)
                    act.wait_ge(clamped, i + 1 + ONE)
                    act.wait_ge(stored, i * 16 + ONE)
                    act.activation(dd[:, 1, :], dd[:, 0, :], ACT.Sqrt).then_inc(rooted, 1)
                    act.wait_ge(rooted, i + 1 + ONE)
                    act.dma_start(dist[ds(i, 1)].rearrange("t p k -> p (t k)"), dd[:, 1, :]).then_inc(stored, 16)
                act.wait_ge(stored, 16 * NT + ONE)


def accumulate_costs(c, dist, cost):
    nc = c.nc
    G = 4
    with ExitStack() as st:
        dcol = c.sb(st, "dcol", [B, 2, G, K])
        rcol = c.sb(st, "rcol", [B, 2, G, K + 1])
        m = c.sb(st, "m", [B, K])
        loaded = [c.sem("loaded0"), c.sem("loaded1")]
        stored = [c.sem("stored0"), c.sem("stored1")]
        order, filled, edge = c.sem("order"), c.sem("filled"), c.sem("edge_stored")
        scanned = c.sem("scanned")
        with nc.Block() as block:
            def load(sp, g, j):
                sp.dma_start(dcol[:, j], dist[:, ds(g * G, G), :]).then_inc(loaded[j], 16)

            @block.sync
            def _(sp):
                load(sp, 0, 0)
                load(sp, 1, 1)
                with sp.Fori(0, S // G // 2 - 1) as i:
                    for j in range(2):
                        sp.wait_ge(scanned, (i * 2 + (j + 1)) * G + ONE)
                        settle(sp)
                        load(sp, i * 2 + (2 + j), j)

            @block.vector
            def _(dve):
                dve.memset(rcol[:], BIG).then_inc(filled, 1)
                dve.wait_ge(filled, 1 + ONE)
                dve.memset(rcol[:, 1, G - 1, 0:1], 0.0).then_inc(filled, 1)
                dve.wait_ge(filled, 2 + ONE)
                dve.wait_ge(edge, 16 + ONE)
                with dve.Fori(0, S // G // 2) as i:
                    link = Link(dve, order, i * (2 * G + 1))
                    for j in range(2):
                        dve.wait_ge(loaded[j], i * 16 + 16 + ONE)
                        dve.wait_ge(stored[j], i * 16 + ONE)
                        for k in range(G):
                            before = rcol[:, j, k - 1] if k else rcol[:, 1 - j, G - 1]
                            link(dve.tensor_tensor(m[:], before[:, 0:K], before[:, 1:K + 1], ALU.min))
                            if j == 0 and k == 0:
                                link(dve.memset(rcol[:, 1, G - 1, 0:1], BIG))
                            dve.tensor_tensor_scan(rcol[:, j, k, 1:K + 1], m[:], dcol[:, j, k, :], BIG,
                                                   ALU.min, ALU.add).then_inc(scanned, 1)
                            dve.wait_ge(scanned, (i * 2 + j) * G + (k + 1) + ONE)
                            settle(dve)

            @block.scalar
            def _(act):
                act.wait_ge(filled, 2 + ONE)
                act.dma_start(cost[:, 0, :], rcol[:, 0, 0, 1:K + 1]).then_inc(edge, 16)
                act.wait_ge(edge, 16 + ONE)
                with act.Fori(0, S // G // 2) as i:
                    for j in range(2):
                        act.wait_ge(scanned, (i * 2 + (j + 1)) * G + ONE)
                        settle(act)
                        act.dma_start(cost[:, ds((i * 2 + j) * G + 1, G), :], rcol[:, j, :, 1:K + 1]
                                      ).then_inc(stored[j], 16)
                for j in range(2):
                    act.wait_ge(stored[j], 16 * (S // G // 2) + ONE)


def choose_steps(c, cost, step, iota1, lows):
    nc = c.nc
    with ExitStack() as st:
        cur = c.sb(st, "cur", [128, K + 1])
        left = c.sb(st, "left", [128, K + 1])
        a = c.sb(st, "a", [128, K])
        leave = c.sb(st, "leave", [128, K])
        diag = c.sb(st, "diag", [128, K])
        lcur = c.sb(st, "lcur", [128, K])
        nxt = c.sb(st, "nxt", [128, 2, K])
        zero = c.sb(st, "zero", [128, K])
        loaded, order, used, ready, stored = (c.sem(n) for n in ("loaded", "order", "used", "ready", "stored"))
        made, filled = c.sem("iota_made"), c.sem("filled")
        LINKS = 9
        with nc.Block() as block:
            def load(sp, t):
                for b in range(2):
                    r = slice(b * S, b * S + S)
                    sp.dma_start(cur[r, 1:K + 1], cost[ds(t * 2 + b, 1), 1:S + 1, :].rearrange("b s k -> (b s) k")
                                 ).then_inc(loaded, 16)
                    sp.dma_start(left[r, 1:K + 1], cost[ds(t * 2 + b, 1), 0:S, :].rearrange("b s k -> (b s) k")
                                 ).then_inc(loaded, 16)

            @block.sync
            def _(sp):
                load(sp, 0)
                with sp.Fori(0, NT - 1) as i:
                    sp.wait_ge(used, i + 1 + ONE)
                    settle(sp)
                    load(sp, i + 1)

            @block.gpsimd
            def _(pool):
                pool.iota(iota1[:], pattern=[[1, K]], base=1, channel_multiplier=0,
                          allow_small_or_imprecise_dtypes=True).then_inc(made, 1)

            @block.vector
            def _(dve):
                dve.memset(cur[:, 0:1], BIG).then_inc(filled, 1)
                dve.memset(left[:, 0:1], BIG).then_inc(filled, 1)
                dve.memset(zero[:], 0.0).then_inc(filled, 1)
                dve.wait_ge(filled, 3 + ONE)
                dve.wait_ge(made, 1 + ONE)
                with dve.Fori(0, NT) as t:
                    link = Link(dve, order, t * LINKS)
                    dve.wait_ge(loaded, t * 64 + 64 + ONE)
                    dve.wait_ge(ready, t + ONE)
                    cu, cl, cd = cur[:, 0:K], left[:, 1:K + 1], left[:, 0:K]
                    link(dve.tensor_tensor(a[:], cu, cl, ALU.min))
                    link(dve.tensor_tensor(diag[:], cd, a[:], ALU.is_le))
                    link(dve.tensor_tensor(a[:], cu, cl, ALU.is_gt))
                    link(dve.tensor_tensor(leave[:], cu, cd, ALU.is_ge))
                    dve.tensor_tensor(leave[:], leave[:], a[:], ALU.max).then_inc(used, 1)
                    dve.wait_ge(used, t + 1 + ONE)
                    settle(dve)
                    link(dve.tensor_tensor(a[:], iota1[:], leave[:], ALU.mult))
                    link(dve.tensor_tensor_scan(lcur[:], a[:], zero[:], 0.0, ALU.max, ALU.add))
                    link(dve.tensor_copy(lows[:, ds(t, 1), :].rearrange("p a k -> p (a k)"), lcur[:]))
                    link(dve.tensor_tensor(a[:], a[:], diag[:], ALU.subtract))
                    link(dve.tensor_tensor(a[:], a[:], leave[:], ALU.mult))
                    dve.wait_ge(stored, t * 16 + ONE)
                    settle(dve)
                    dve.tensor_tensor_scan(nxt[:, 0, :], a[:], zero[:], 0.0, ALU.max, ALU.add).then_inc(ready, 1)
                    assert link.n == LINKS, link.n

            @block.scalar
            def _(act):
                with act.Fori(0, NT) as t:
                    act.wait_ge(ready, t + 1 + ONE)
                    settle(act)
                    act.dma_start(step.rearrange("(t b) s k -> t (b s) k", b=2)[ds(t, 1)].rearrange(
                        "t p k -> p (t k)"), nxt[:, 0, :]).then_inc(stored, 16)
                act.wait_ge(stored, 16 * NT + ONE)


def trace_back(c, step, iota1, hi_dram):
    nc = c.nc
    G = 4
    with ExitStack() as st:
        col = c.sb(st, "col", [B, 2, G, K])
        junk = c.sb(st, "junk", [B, K])
        hi = c.sb(st, "hi", [B, S + 1])
        loaded = [c.sem("loaded0"), c.sem("loaded1")]
        found, stored, filled = c.sem("found"), c.sem("hi_stored"), c.sem("filled")
        with nc.Block() as block:
            def load(sp, g, j):
                sp.dma_start(col[:, j], step[:, ds(g * (-G) + (S - G), G), :]).then_inc(loaded[j], 16)

            @block.sync
            def _(sp):
                load(sp, 0, 0)
                load(sp, 1, 1)
                with sp.Fori(0, S // G // 2 - 1) as i:
                    for j in range(2):
                        sp.wait_ge(found, (i * 2 + (j + 1)) * G + ONE)
                        settle(sp)
                        load(sp, i * 2 + (2 + j), j)
                sp.wait_ge(found, S + ONE)
                sp.dma_start(hi_dram.rearrange("(b s) -> b s", b=B), hi[:, 1:S + 1]).then_inc(stored, 16)
                sp.wait_ge(stored, 16 + ONE)

            @block.vector
            def _(dve):
                dve.memset(hi[:, S:S + 1], float(K)).then_inc(filled, 1)
                dve.wait_ge(filled, 1 + ONE)
                with dve.Fori(0, S // G // 2) as i:
                    for j in range(2):
                        dve.wait_ge(loaded[j], i * 16 + 16 + ONE)
                        for k in range(G):
                            n = i * (-2 * G) + (S - j * G - k)
                            dve.scalar_tensor_tensor(out=junk[:], in0=iota1[0:B, :], scalar=hi[:, ds(n, 1)],
                                                     in1=col[:, j, G - 1 - k, :], op0=ALU.is_equal, op1=ALU.mult,
                                                     accum_out=hi[:, ds(n - 1, 1)]).then_inc(found, 1)
                            dve.wait_ge(found, (i * 2 + j) * G + (k + 1) + ONE)
                            settle(dve)


def look_up_lows(c, iota1, lows, hi_dram, lo_dram):
    nc = c.nc
    with ExitStack() as st:
        hi = c.sb(st, "hi", [128, NT])
        lo = c.sb(st, "lo", [128, NT])
        junk = c.sb(st, "junk", [128, K])
        loaded, order, stored = c.sem("loaded"), c.sem("order"), c.sem("stored")
        with nc.Block() as block:
            @block.sync
            def _(sp):
                with nc.allow_non_contiguous_dma(reason="1024 single numbers"):
                    sp.dma_start(hi[:], hi_dram.rearrange("(t p) -> p t", p=128)).then_inc(loaded, 16)
                    sp.wait_ge(order, NT + ONE)
                    sp.dma_start(lo_dram.rearrange("(t p) -> p t", p=128), lo[:]).then_inc(stored, 16)
                    sp.wait_ge(stored, 16 + ONE)

            @block.vector
            def _(dve):
                link = Link(dve, order)
                dve.wait_ge(loaded, 16 + ONE)
                for t in range(NT):
                    link(dve.scalar_tensor_tensor(out=junk[:], in0=iota1[:], scalar=hi[:, t:t + 1],
                                                  in1=lows[:, t, :], op0=ALU.is_equal, op1=ALU.mult,
                                                  accum_out=lo[:, t:t + 1]))


def add_aligned(c, hi_dram, lo_dram):
    nc = c.nc
    with ExitStack() as st:
        hi = c.sb(st, "hi", [128, B * S])
        lo = c.sb(st, "lo", [128, B * S])
        tmp = c.sb(st, "tmp", [128, B * S])
        row1 = c.sb(st, "row1", [128, len(KC)])
        inside = c.sb(st, "inside", [128, len(KC), B * S])
        ctxN = c.sb(st, "ctxN", [128, 2, len(KC), D])
        sumT = c.sb(st, "sumT", [128, B * S])
        psA = c.ps(st, "psA", [128, 2, 512])
        psX = c.ps(st, "psX", [128, NT, 128])
        ends, made, order = c.sem("ends"), c.sem("made"), c.sem("order")
        loaded = [c.sem("loaded0"), c.sem("loaded1")]
        summed, copied, turned, done = (c.sem(n) for n in ("summed", "copied", "turned", "done"))
        with nc.Block() as block:
            def load(sp, b, j):
                n = K // 128
                sp.dma_start(ctxN[:, j, 0:n, :], c.dram["ctx_1024"][ds(b, 1), 0:n * 128, :].rearrange(
                    "b (c p) d -> p (b c) d", p=128)).then_inc(loaded[j], 16)
                sp.dma_start(ctxN[0:K - n * 128, j, n, :], c.dram["ctx_1024"][ds(b, 1), n * 128:K, :].rearrange(
                    "b p d -> p (b d)")).then_inc(loaded[j], 16)

            @block.sync
            def _(sp):
                sp.dma_start(hi[:], row_bcast(hi_dram)).then_inc(ends, 16)
                sp.dma_start(lo[:], row_bcast(lo_dram)).then_inc(ends, 16)
                load(sp, 0, 0)
                load(sp, 1, 1)
                with sp.Fori(0, NT - 1) as i:
                    for j in range(2):
                        sp.wait_ge(summed, i * 2 + (j + 1) + ONE)
                        settle(sp)
                        load(sp, i * 2 + (2 + j), j)

            @block.gpsimd
            def _(pool):
                pool.iota(row1[:], pattern=[[128, len(KC)]], base=1, channel_multiplier=1,
                          allow_small_or_imprecise_dtypes=True).then_inc(made, 1)

            @block.vector
            def _(dve):
                link = Link(dve, order)
                dve.wait_ge(made, 1 + ONE)
                dve.wait_ge(ends, 32 + ONE)
                for k in range(len(KC)):
                    link(dve.tensor_scalar(tmp[:], lo[:], row1[:, k:k + 1], None, ALU.is_le))
                    link(dve.scalar_tensor_tensor(out=inside[:, k, :], in0=hi[:], scalar=row1[:, k:k + 1],
                                                  in1=tmp[:], op0=ALU.is_ge, op1=ALU.mult))
                with dve.Fori(0, NT) as i:
                    for j in range(2):
                        dve.wait_ge(summed, i * 2 + (j + 1) + ONE)
                        dve.tensor_copy(sumT[:, ds(i * 128 + j * S, S)], psA[:, j, 0:S]).then_inc(copied, 1)
                dve.wait_ge(turned, 1 + ONE)
                dve.tensor_tensor(c.x[:], c.x[:], psX[:], ALU.add).then_inc(done, 1)
                dve.wait_ge(done, 1 + ONE)

            @block.tensor
            def _(pe):
                pe.wait_ge(order, 2 * len(KC) + ONE)
                with pe.Fori(0, NT) as i:
                    for j in range(2):
                        pe.wait_ge(loaded[j], i * 32 + 32 + ONE)
                        pe.wait_ge(copied, i * 2 + ONE)
                        for k, (o, w) in enumerate(KC):
                            last = pe.matmul(psA[:, j, 0:S], ctxN[0:w, j, k, :],
                                             inside[0:w, k, ds(i * 128 + j * S, S)],
                                             start=(k == 0), stop=(k == len(KC) - 1))
                        last.then_inc(summed, 1)
                pe.wait_ge(copied, 2 * NT + ONE)
                for t in range(NT):
                    last = pe.transpose(psX[:, t, :], sumT[:, t * 128:t * 128 + 128], c.ident[:])
                last.then_inc(turned, 1)


STAGES = [stage_l0_xattn, stage_l0_attn, stage_l0_ffn, stage_l1_xattn, stage_l1_attn, stage_l1_ffn, stage_l2_xattn,
          stage_l2_attn, stage_l2_ffn, stage_l3_xattn, stage_l3_attn, stage_l3_ffn]


def perceiver(nc, dram, out):
    with ExitStack() as ctx:
        c = Core(nc, ctx, dram)
        c.ctxT = nc.dram_tensor("ctxT_scratch", [B, 128, K], F32, kind="Internal").ap()
        constants(c)
        if FIRST_STAGE in (0, 3, 6, 9) or LAST_STAGE > FIRST_STAGE:
            transpose_context(c)
        for stage in STAGES[FIRST_STAGE:LAST_STAGE + 1]:
            stage(c)
            c.end_stage()
        stored = c.sem("out_stored")
        with nc.Block() as block:
            @block.sync
            def _(sp):
                sp.dma_start(out.rearrange("(t b) s d -> (b s) t d", b=2), c.x[:]).then_inc(stored, 16)
                sp.wait_ge(stored, 16 + ONE)


def kernel(**inputs):
    import numpy as np
    import concourse.bacc as bacc
    from concourse.bass_utils import run_bass_kernel_spmd

    nc = bacc.Bacc("TRN2", target_bir_lowering=False, num_devices=1)
    arrays, dram = {}, {}
    for name, value in inputs.items():
        a = np.ascontiguousarray(value)
        if a.dtype == np.bool_:
            a = a.view(np.uint8)
        arrays[f"in_{name}"] = a
        dram[name] = nc.dram_tensor(f"in_{name}", a.shape, mybir.dt.from_np(a.dtype), kind="ExternalInput").ap()
    out = nc.dram_tensor("out", [B, S, D], F32, kind="ExternalOutput").ap()
    perceiver(nc, dram, out)
    result = run_bass_kernel_spmd(nc, [arrays], core_ids=[0])
    return result.results[0]["out"]
```

```python
from contextlib import ExitStack

import concourse.bass as bass
from concourse import mybir

FIRST_STAGE, LAST_STAGE = 0, 11

ALU = mybir.AluOpType
ACT = mybir.ActivationFunctionType
F32 = mybir.dt.float32
U8 = mybir.dt.uint8
X = mybir.AxisListType.X
ds = bass.ds

B, S, D = 16, 64, 128
NT = B * S // 128
K = 1601
KC = [(c * 128, min(128, K - c * 128)) for c in range((K + 127) // 128)]
KB = [(c * 512, min(512, K - c * 512)) for c in range((K + 511) // 512)]
H = 16
E = 8
NEG = -1.0e30
LN_EPS = 1e-5
ONE = 1
SEMS = 100


def settle(eng):
    eng.nop(nofuse=True)


class Link:

    def __init__(self, eng, sem, base=0):
        self.eng, self.sem, self.base, self.n = eng, sem, base, 0

    def __call__(self, ins):
        self.n += 1
        ins.then_inc(self.sem, 1)
        self.eng.wait_ge(self.sem, self.base + self.n + ONE)
        if not isinstance(self.base, int):
            settle(self.eng)
        return ins


class Core:

    def __init__(self, nc, ctx, dram):
        self.nc, self.ctx, self.dram, self.n = nc, ctx, dram, 0
        self.pool = [nc.alloc_semaphore(f"stage_sem_{n}") for n in range(SEMS)]
        self.used = 0
        self.credit(self.pool)
        self.x = self.keep("x", [128, NT, D])
        self.xn = self.keep("xn", [128, NT, D])
        self.xnT = self.keep("xnT", [128, NT * 128])
        self.ident = self.keep("ident", [128, 128])
        self.ones = self.keep("ones", [128, 128])
        self.headmask = self.keep("headmask", [128, H])
        self.bias_row = self.keep("bias_row", [128, D])

    def keep(self, name, shape, dt=F32):
        return self.ctx.enter_context(self.nc.sbuf_tensor(name, shape, dt))

    def sem(self, name):
        self.used += 1
        return self.pool[self.used - 1]

    def credit(self, sems):
        for sem in sems:
            self.nc.gpsimd.sem_inc(sem, ONE)
        self.nc.all_engine_barrier()

    def end_stage(self):
        used = self.pool[:self.used]
        for sem in used:
            self.nc.gpsimd.sem_clear(sem)
        self.credit(used)
        self.used = 0

    def sb(self, st, name, shape, dt=F32):
        self.n += 1
        return st.enter_context(self.nc.sbuf_tensor(f"{name}_{self.n}", shape, dt))

    def ps(self, st, name, shape, dt=F32):
        self.n += 1
        return st.enter_context(self.nc.psum_tensor(f"{name}_{self.n}", shape, dt))


def row_bcast(vec, n=128):
    return vec.rearrange("(a d) -> a d", a=1).to_broadcast([n, vec.shape[0]])


def bc(ap, shape):
    return ap.to_broadcast(shape)


def constants(c):
    nc = c.nc
    loaded, made, filled = c.sem("x_loaded"), c.sem("const_made"), c.sem("const_filled")
    with nc.Block() as block:
        @block.sync
        def _(sp):
            sp.dma_start(c.x[:], c.dram["x"].rearrange("(t b) s d -> (b s) t d", b=2)).then_inc(loaded, 16)
            sp.wait_ge(loaded, 16 + ONE)

        @block.gpsimd
        def _(pool):
            pool.memset(c.ident[:], 0.0).then_inc(filled, 1)
            pool.memset(c.ones[:], 1.0).then_inc(filled, 1)
            pool.memset(c.headmask[:], 1.0).then_inc(filled, 1)
            pool.wait_ge(filled, 3 + ONE)
            pool.affine_select(out=c.ident[:], in_=c.ident[:], compare_op=ALU.not_equal, fill=1.0, base=0,
                               pattern=[[-1, 128]], channel_multiplier=1).then_inc(made, 1)
            pool.affine_select(out=c.headmask[:], in_=c.headmask[:], compare_op=ALU.is_ge, fill=0.0, base=0,
                               pattern=[[-8, H]], channel_multiplier=1).then_inc(made, 1)
            pool.wait_ge(made, 2 + ONE)
            pool.affine_select(out=c.headmask[:], in_=c.headmask[:], compare_op=ALU.is_ge, fill=0.0, base=7,
                               pattern=[[8, H]], channel_multiplier=-1).then_inc(made, 1)
            pool.wait_ge(made, 3 + ONE)


def transpose_context(c):
    nc = c.nc
    with ExitStack() as st:
        nat = c.sb(st, "ctx_nat", [128, 2, len(KC), D])
        trn = c.sb(st, "ctx_trn", [128, 2, K])
        pt = [c.ps(st, f"ctx_pt{g}", [128, 512]) for g in range(4)]
        loaded = [c.sem("nat_loaded0"), c.sem("nat_loaded1")]
        turned, copied = c.sem("ctx_turned"), c.sem("ctx_copied")
        stored = [c.sem("trn_stored0"), c.sem("trn_stored1")]
        ctx = c.dram["ctx_1024"]
        with nc.Block() as block:
            def load(sp, b, j):
                n = K // 128
                sp.dma_start(nat[:, j, 0:n, :], ctx[b:b + 1 if isinstance(b, int) else None] if 0 else
                             ctx[ds(b, 1), 0:n * 128, :].rearrange("b (c p) d -> p (b c) d", p=128)
                             ).then_inc(loaded[j], 16)
                sp.dma_start(nat[0:K - n * 128, j, n, :],
                             ctx[ds(b, 1), n * 128:K, :].rearrange("b p d -> p (b d)")).then_inc(loaded[j], 16)

            @block.sync
            def _(sp):
                load(sp, 0, 0)
                load(sp, 1, 1)
                with sp.Fori(0, B // 2 - 1) as i:
                    for j in range(2):
                        sp.wait_ge(turned, (i * 2 + j + 1) * 4 + ONE)
                        settle(sp)
                        load(sp, i * 2 + (2 + j), j)

            @block.tensor
            def _(pe):
                with pe.Fori(0, B // 2) as i:
                    for j in range(2):
                        pe.wait_ge(loaded[j], (i + 1) * 32 + ONE)
                        for g in range(4):
                            pe.wait_ge(copied, (i * 2 + j) * 4 + ONE)
                            for k in range(4 * g, min(4 * g + 4, len(KC))):
                                n = KC[k][1]
                                last = pe.transpose(pt[g][:, (k % 4) * 128:(k % 4) * 128 + n],
                                                    nat[0:n, j, k, :], c.ident[0:n, 0:n])
                            last.then_inc(turned, 1)

            @block.vector
            def _(dve):
                with dve.Fori(0, B // 2) as i:
                    for j in range(2):
                        dve.wait_ge(stored[j], i * 16 + ONE)
                        for g in range(4):
                            o, n = KB[g]
                            dve.wait_ge(turned, (i * 2 + j) * 4 + g + 1 + ONE)
                            dve.tensor_copy(trn[:, j, o:o + n], pt[g][:, 0:n]).then_inc(copied, 1)

            @block.scalar
            def _(act):
                with act.Fori(0, B // 2) as i:
                    for j in range(2):
                        act.wait_ge(copied, (i * 2 + j + 1) * 4 + ONE)
                        act.dma_start(c.ctxT[ds(i * 2 + j, 1)].rearrange("b p k -> p (b k)"),
                                      trn[:, j, :]).then_inc(stored[j], 16)
                for j in range(2):
                    act.wait_ge(stored[j], 16 * (B // 2) + ONE)


def layernorm(c):
    nc = c.nc
    with ExitStack() as st:
        mean = c.sb(st, "ln_mean", [128, NT, 1])
        var = c.sb(st, "ln_var", [128, NT, 1])
        std = c.sb(st, "ln_std", [128, NT, 1])
        inv = c.sb(st, "ln_inv", [128, NT, 1])
        sq = c.sb(st, "ln_sq", [128, NT, D])
        pt = c.ps(st, "ln_pt", [128, NT * 128])
        order, var_ready, std_ready = c.sem("ln_order"), c.sem("ln_var_ready"), c.sem("ln_std_ready")
        xn_ready, turned, done = c.sem("xn_ready"), c.sem("xn_turned"), c.sem("xnT_done")
        with nc.Block() as block:
            @block.vector
            def _(dve):
                link = Link(dve, order)
                link(dve.reduce_sum(mean[:, :, 0], c.x[:], axis=X))
                link(dve.tensor_scalar(mean[:, :, 0], mean[:, :, 0], 1.0 / D, None, ALU.mult))
                link(dve.tensor_tensor(c.xn[:], c.x[:], bc(mean[:], [128, NT, D]), ALU.subtract))
                link(dve.tensor_tensor(sq[:], c.xn[:], c.xn[:], ALU.mult))
                link(dve.reduce_sum(var[:, :, 0], sq[:], axis=X))
                dve.tensor_scalar(var[:, :, 0], var[:, :, 0], 1.0 / D, LN_EPS, ALU.mult, ALU.add
                                  ).then_inc(var_ready, 1)
                dve.wait_ge(std_ready, 1 + ONE)
                link(dve.reciprocal(inv[:, :, 0], std[:, :, 0]))
                dve.tensor_tensor(c.xn[:], c.xn[:], bc(inv[:], [128, NT, D]), ALU.mult).then_inc(xn_ready, 1)
                for h in range(2):
                    dve.wait_ge(turned, h + 1 + ONE)
                    dve.tensor_copy(c.xnT[:, h * 512:h * 512 + 512], pt[:, h * 512:h * 512 + 512]
                                    ).then_inc(done, 1)
                dve.wait_ge(done, 2 + ONE)

            @block.scalar
            def _(act):
                act.wait_ge(var_ready, 1 + ONE)
                act.activation(std[:, :, 0], var[:, :, 0], ACT.Sqrt).then_inc(std_ready, 1)

            @block.tensor
            def _(pe):
                pe.wait_ge(xn_ready, 1 + ONE)
                for t in range(NT):
                    last = pe.transpose(pt[:, t * 128:t * 128 + 128], c.xn[:, t, :], c.ident[:])
                    if t % 4 == 3:
                        last.then_inc(turned, 1)


def load_all(c, pairs):
    nc = c.nc
    loaded = c.sem("loaded")
    with nc.Block() as block:
        @block.sync
        def _(sp):
            for out, src in pairs:
                sp.dma_start(out, src).then_inc(loaded, 16)
            sp.wait_ge(loaded, 16 * len(pairs) + ONE)


def turn_all(c, jobs):
    nc = c.nc
    with ExitStack() as st:
        pt = [c.ps(st, f"turn{j}", [128, 512]) for j in range(2)]
        turned, copied = c.sem("turned"), c.sem("turn_copied")
        with nc.Block() as block:
            @block.tensor
            def _(pe):
                for n, (out, src) in enumerate(jobs):
                    if n >= 2:
                        pe.wait_ge(copied, n - 1 + ONE)
                    p, f = src.shape
                    pe.transpose(pt[n % 2][0:f, 0:p], src, c.ident[0:p, 0:p]).then_inc(turned, 1)

            @block.vector
            def _(dve):
                for n, (out, src) in enumerate(jobs):
                    p, f = src.shape
                    dve.wait_ge(turned, n + 1 + ONE)
                    dve.tensor_copy(out, pt[n % 2][0:f, 0:p]).then_inc(copied, 1)
                dve.wait_ge(copied, len(jobs) + ONE)


def multiply_all(c, jobs):
    nc = c.nc
    with ExitStack() as st:
        pm = [c.ps(st, f"mul{j}", [128, 512]) for j in range(2)]
        summed, copied = c.sem("summed"), c.sem("sum_copied")
        with nc.Block() as block:
            @block.tensor
            def _(pe):
                for n, (out, terms) in enumerate(jobs):
                    if n >= 2:
                        pe.wait_ge(copied, n - 1 + ONE)
                    p, f = out.shape
                    for k, (lhsT, rhs) in enumerate(terms):
                        last = pe.matmul(pm[n % 2][0:p, 0:f], lhsT, rhs, start=(k == 0),
                                         stop=(k == len(terms) - 1))
                    last.then_inc(summed, 1)

            @block.vector
            def _(dve):
                for n, (out, terms) in enumerate(jobs):
                    p, f = out.shape
                    dve.wait_ge(summed, n + 1 + ONE)
                    dve.tensor_copy(out, pm[n % 2][0:p, 0:f]).then_inc(copied, 1)
                dve.wait_ge(copied, len(jobs) + ONE)


def head_blocks(c, st, lhsT, rhs, out):
    nc = c.nc
    spread = c.sb(st, "spread", [128, H, D])
    spread_done = c.sem("spread_done")
    with nc.Block() as block:
        @block.vector
        def _(dve):
            for h in range(H):
                dve.tensor_scalar(spread[:, h, :], rhs, c.headmask[:, h:h + 1], None, ALU.mult
                                  ).then_inc(spread_done, 1)
            dve.wait_ge(spread_done, H + ONE)
    flat_in = spread[:].rearrange("p h d -> p (h d)")
    flat_out = out.rearrange("p h d -> p (h d)")
    multiply_all(c, [(flat_out[:, n:n + 512], [(lhsT, flat_in[:, n:n + 512])]) for n in range(0, H * D, 512)])


def cross_attention(c, M, N, scale, masked=False, topk=None):
    nc = c.nc
    TB = H // 2
    T = 2 * TB
    AHEAD = 2 if topk else 1
    NI = B // 2
    VW = D + 1 if topk else D
    with ExitStack() as st:
        ctxT = c.sb(st, "ctxT", [128, 2, K])
        ctxN = c.sb(st, "ctxN", [128, 2, len(KC), D + 4])
        stat = c.sb(st, "stat", [128, 2, H, S])
        P = c.sb(st, "P", [128, 2, K])
        PT = c.sb(st, "PT", [128, 2, len(KC), 128])
        UT = c.sb(st, "UT", [128, 2, TB, 128])
        U = c.sb(st, "U", [128, 2, 128])
        mx = c.sb(st, "mx", [128, 2])
        ls = c.sb(st, "ls", [128, 2])
        li = c.sb(st, "li", [128, 2])
        if masked or topk:
            SS = c.sb(st, "SS", [128, 2, K])
        if masked:
            mask8 = c.sb(st, "mask8", [128, 2, K], U8)
            maskf = c.sb(st, "maskf", [128, 2, K])
        if topk:
            KT = c.sb(st, "KT", [128, 2, K])
            top = c.sb(st, "top", [128, 4, 8])
            rest = c.sb(st, "rest", [128, 2, K])
            EX = c.sb(st, "EX", [128, K])
            ER = c.sb(st, "ER", [128, K])
        psS = c.ps(st, "psS", [128, 2048])
        psT = c.ps(st, "psT", [128, 2, 512])
        psU = c.ps(st, "psU", [128, 512])
        psZ = c.ps(st, "psZ", [128, 512])

        loaded = [c.sem("ctx_loaded0"), c.sem("ctx_loaded1")]
        mask_ready, ones_ready = c.sem("mask_ready"), c.sem("ones_ready")
        qp_ready, stat_ready, kt_ready = c.sem("qp_ready"), c.sem("stat_ready"), c.sem("kt_ready")
        scores_ready, max_ready, exp_done = c.sem("scores_ready"), c.sem("max_ready"), c.sem("exp_done")
        copied, rest_ready, rest_exp = c.sem("copied"), c.sem("rest_ready"), c.sem("rest_exp")
        p_ready = c.sem("p_ready") if topk else exp_done
        score_free = copied if topk else max_ready if masked else exp_done
        turned, pt_front, pt_back = c.sem("turned"), c.sem("pt_front"), c.sem("pt_back")
        u_ready, li_ready, us_ready = c.sem("u_ready"), c.sem("li_ready"), c.sem("us_ready")
        ut_turned, ut_ready = c.sem("ut_turned"), c.sem("ut_ready")
        y_ready, x_done, order = c.sem("y_ready"), c.sem("x_done"), c.sem("order")
        LOADS = 16 * (4 if masked else 3)
        LINKS = 2 + T * (7 if topk else 1 if masked else 0)

        if topk:
            with nc.Block() as block:
                @block.gpsimd
                def _(pool):
                    for j in range(2):
                        pool.memset(ctxN[:, j, :, D:D + 1], 1.0).then_inc(ones_ready, 1)
                    pool.wait_ge(ones_ready, 2 + ONE)

        def copy_weights(eng, copy, g, n, q):
            w = len(KC) - 12 if q == 3 else 4
            p = KC[-1][1] if q == 3 else 128
            eng.wait_ge(turned, g * 4 + (q + 1) + ONE)
            copy(PT[0:p, n % 2, 4 * q:4 * q + w, :],
                 psT[0:p, q % 2, 0:w * 128].rearrange("p (k t) -> p k t", t=128)
                 ).then_inc(pt_front if q < 2 else pt_back, 1)

        with nc.Block() as block:
            def load(sp, b, j):
                n = K // 128
                sp.dma_start(ctxT[:, j, :], c.ctxT[ds(b, 1)].rearrange("b p k -> p (b k)")).then_inc(loaded[j], 16)
                sp.dma_start(ctxN[:, j, 0:n, 0:D], c.dram["ctx_1024"][ds(b, 1), 0:n * 128, :].rearrange(
                    "b (c p) d -> p (b c) d", p=128)).then_inc(loaded[j], 16)
                sp.dma_start(ctxN[0:K - n * 128, j, n, 0:D], c.dram["ctx_1024"][ds(b, 1), n * 128:K, :].rearrange(
                    "b p d -> p (b d)")).then_inc(loaded[j], 16)
                if masked:
                    sp.dma_start(mask8[:, j, :], c.dram["mask_BxS2_bf1"][ds(b, 1)].to_broadcast([128, K])
                                 ).then_inc(loaded[j], 16)

            @block.sync
            def _(sp):
                load(sp, 0, 0)
                load(sp, 1, 1)
                with sp.Fori(0, NI - 1) as i:
                    for j in range(2):
                        sp.wait_ge(u_ready, i * T + TB * (j + 1) + ONE)
                        settle(sp)
                        if masked:
                            sp.wait_ge(mask_ready, i * 2 + (j + 1) + ONE)
                            settle(sp)
                        load(sp, i * 2 + (2 + j), j)

            @block.tensor
            def _(pe):
                def scores(i, t):
                    j, n = t // TB % 2, t % TB
                    if n == 0:
                        pe.wait_ge(stat_ready, i * 2 + (t // TB + 1) + ONE)
                    pe.wait_ge(score_free, i * T + t + ONE)
                    src = KT[:, j, :] if topk else ctxT[:, j, :]
                    for o, w in KB:
                        last = pe.matmul(psS[:, o:o + w], stat[:, j, 2 * n:2 * n + 2, :], src[:, o:o + w],
                                         start=True, stop=True)
                    last.then_inc(scores_ready, 1)

                def project(loads, b, j, g, ahead):
                    pe.wait_ge(loaded[j], loads * LOADS + ONE)
                    if topk:
                        pe.wait_ge(score_free, g + ahead + ONE)
                        for o, w in KB:
                            last = pe.matmul(psS[:, o:o + w], topk[1], ctxT[:, j, o:o + w], start=True, stop=True)
                        last.then_inc(qp_ready, 1)
                        pe.wait_ge(kt_ready, b + 1 + ONE)
                    else:
                        pe.wait_ge(pt_back, g * 2 + ONE)
                        for h in range(H):
                            last = pe.matmul(psT[:, h // 8, (h % 8) * S:(h % 8) * S + S], M[:, h, :],
                                             c.xnT[:, ds(b * S, S)], start=True, stop=True)
                        last.then_inc(qp_ready, 1)

                def turn(g, t, q, first):
                    if q >= 2:
                        pe.wait_ge(pt_front, g * 2 + (q - 1) + ONE)
                    elif not (first and t == 0):
                        pe.wait_ge(pt_back, g * 2 - (1 - q) + ONE)
                    for k in range(4 * q, min(4 * q + 4, len(KC))):
                        o, w = KC[k]
                        last = pe.transpose(psT[0:w, q % 2, (k % 4) * 128:(k % 4) * 128 + 128],
                                            P[:, t % 2, o:o + w], c.ident[:])
                    last.then_inc(turned, 1)

                def values(g, t, q):
                    if q == 0:
                        pe.wait_ge(us_ready, g + ONE)
                    if q < 2:
                        pe.wait_ge(pt_front, g * 2 + (q + 1) + ONE)
                    else:
                        pe.wait_ge(pt_back, g * 2 + (q - 1) + ONE)
                    for k in range(4 * q, min(4 * q + 4, len(KC))):
                        w = KC[k][1]
                        last = pe.matmul(psU[:, 0:VW], PT[0:w, t % 2, k, :], ctxN[0:w, t // TB, k, 0:VW],
                                         start=(k == 0), stop=(k == len(KC) - 1))
                    if q == 3:
                        last.then_inc(u_ready, 1)

                def turn_u(g, t):
                    pe.wait_ge(us_ready, g + 1 + ONE)
                    pe.wait_ge(ut_ready, g + ONE)
                    pe.transpose(psZ[:, 0:128], U[:, t % 2, :], c.ident[:]).then_inc(ut_turned, 1)

                def sums(j, g):
                    pe.wait_ge(ut_ready, g + ONE)
                    for h in range(H):
                        last = pe.matmul(psZ[j * S:j * S + S, 128:256], UT[:, j, h // 2, (h % 2) * S:(h % 2) * S + S],
                                         N[:, h, :], start=(h == 0), stop=(h == H - 1))
                    last.then_inc(y_ready, 1)

                def iteration(i, first, final):
                    g = i * T
                    for t in range(T):
                        if t == 4:
                            project(i + 1, i * 2 + 1, 1, g + t, AHEAD)
                        if t == 12 and not final:
                            project(i + 2, i * 2 + 2, 0, g + t, AHEAD)
                        more = t + AHEAD < T or not final
                        early = topk or t == 4 or (t == 12 and not final)
                        if more and early:
                            scores(i, t + AHEAD)
                            if not topk:
                                pe.wait_ge(stat_ready, i * 2 + (2 if t == 4 else 3) + ONE)
                        pe.wait_ge(p_ready, g + t + 1 + ONE)
                        turn(g + t, t, 0, first)
                        turn(g + t, t, 1, first)
                        if more and not early:
                            scores(i, t + AHEAD)
                        done = t in (1, 9) and not (first and t == 1)
                        if done:
                            sums(int(t == 1), g + (t - 1))
                        turn(g + t, t, 2, first)
                        values(g + t, t, 0)
                        turn(g + t, t, 3, first)
                        for q in range(1, 4):
                            values(g + t, t, q)
                        if done:
                            pe.wait_ge(x_done, i * 2 + int(t == 9) + ONE)
                        if t:
                            turn_u(g + (t - 1), t - 1)
                        elif not first:
                            turn_u(g - 1, T - 1)

                project(1, 0, 0, 0, 0)
                for t in range(AHEAD):
                    scores(0, t)
                iteration(0, True, False)
                with pe.Fori(1, NI - 1) as i:
                    iteration(i, False, False)
                iteration(NI - 1, False, True)
                turn_u(NI * T - 1, T - 1)
                sums(1, NI * T)

            @block.scalar
            def _(act):
                def stationary(b, j):
                    act.wait_ge(qp_ready, b + 1 + ONE)
                    if topk:
                        act.activation(KT[:, j, :], psS[:, 0:K], ACT.Identity, bias=topk[2]).then_inc(kt_ready, 1)
                    else:
                        act.activation(stat[:, j].rearrange("p h s -> p (h s)"),
                                       psT[:].rearrange("p a b -> p (a b)"), ACT.Copy, scale=scale
                                       ).then_inc(stat_ready, 1)

                def exps(g, t, first=False):
                    k = t % 2
                    act.wait_ge(max_ready, g + 1 + ONE)
                    if not first:
                        act.wait_ge(u_ready, g - 1 + ONE)
                    act.activation(P[:, k, :], SS[:, k, :] if masked else psS[:, 0:K], ACT.Exp,
                                   bias=mx[:, k:k + 1], accum_out=ls[:, k:k + 1]).then_inc(exp_done, 1)

                def copy_scores(g, t, first=False):
                    act.wait_ge(scores_ready, g + 1 + ONE)
                    if not first:
                        act.wait_ge(rest_ready, g - 1 + ONE)
                        act.wait_ge(exp_done, g - 1 + ONE)
                    act.activation(SS[:, t % 2, :], psS[:, 0:K], ACT.Copy).then_inc(copied, 1)

                def exps_topk(g, t):
                    k = t % 2
                    act.wait_ge(max_ready, g + 1 + ONE)
                    act.wait_ge(p_ready, g + ONE)
                    act.activation(EX[:], SS[:, k, :], ACT.Exp, bias=mx[:, k:k + 1]).then_inc(exp_done, 1)
                    act.wait_ge(rest_ready, g + 1 + ONE)
                    act.activation(ER[:], rest[:, k, :], ACT.Exp, bias=mx[:, k:k + 1]).then_inc(rest_exp, 1)

                def norm(g, t):
                    act.wait_ge(u_ready, g + 1 + ONE)
                    act.wait_ge(li_ready, g + 1 + ONE)
                    act.wait_ge(ut_turned, (g if t == 0 else g - 1) + ONE)
                    act.activation(U[:, t % 2, :], psU[:, 0:128], ACT.Copy,
                                   scale=li[:, t % 2:t % 2 + 1]).then_inc(us_ready, 1)

                def copy(out, src):
                    return act.activation(out, src, ACT.Copy)

                def iteration(i, first, final):
                    g = i * T
                    for t in range(T):
                        more = t + AHEAD < T or not final
                        if topk:
                            exps_topk(g + t, t)
                            if t:
                                norm(g + (t - 1), t - 1)
                            elif not first:
                                norm(g - 1, T - 1)
                        if t == 4:
                            stationary(i * 2 + 1, 1)
                        if t == 12 and not final:
                            stationary(i * 2 + 2, 0)
                        if topk:
                            if more:
                                copy_scores(g + (t + AHEAD), t + AHEAD)
                            copy_weights(act, copy, g + t, t, 0)
                            copy_weights(act, copy, g + t, t, 1)
                        copy_weights(act, copy, g + t, t, 2)
                        copy_weights(act, copy, g + t, t, 3)
                        if not topk:
                            if more:
                                exps(g + (t + AHEAD), t + AHEAD)
                            norm(g + t, t)

                stationary(0, 0)
                for t in range(AHEAD):
                    if topk:
                        copy_scores(t, t, first=True)
                    else:
                        exps(t, t, first=True)
                iteration(0, True, False)
                with act.Fori(1, NI - 1) as i:
                    iteration(i, False, False)
                iteration(NI - 1, False, True)
                if topk:
                    norm(NI * T - 1, T - 1)

            @block.gpsimd
            def _(pool):
                if masked:
                    def convert(i, b, j, first):
                        pool.wait_ge(loaded[j], (i + 1) * LOADS + ONE)
                        if not first:
                            pool.wait_ge(max_ready, i * T + (j * TB - TB) + ONE)
                        settle(pool)
                        pool.tensor_scalar(maskf[:, j, :], mask8[:, j, :], -1.0, -NEG, ALU.add, ALU.mult
                                           ).then_inc(mask_ready, 1)

                    for j in range(2):
                        convert(0, j, j, True)
                    with pool.Fori(1, NI) as i:
                        for j in range(2):
                            convert(i, i * 2 + j, j, False)
                if topk:
                    def spread(b, j):
                        pool.wait_ge(qp_ready, b + 1 + ONE)
                        pool.tensor_tensor(
                            stat[:, j],
                            bc(topk[0][:, ds(b * S, S)].rearrange("p (a s) -> p a s", a=1), [128, H, S]),
                            bc(c.headmask[:].rearrange("p (h a) -> p h a", a=1), [128, H, S]), ALU.mult
                            ).then_inc(stat_ready, 1)

                    def weights(g, t, first=False):
                        pool.wait_ge(rest_exp, g + 1 + ONE)
                        pool.wait_ge(u_ready, (g if t == 0 else g - 1) + ONE)
                        pool.tensor_tensor(P[:, t % 2, :], EX[:], ER[:], ALU.subtract).then_inc(p_ready, 1)

                    def iteration(i, final):
                        for t in range(T):
                            weights(i * T + t, t)
                            if t == 3:
                                spread(i * 2 + 1, 1)
                            if t == 11 and not final:
                                spread(i * 2 + 2, 0)

                    spread(0, 0)
                    with pool.Fori(0, NI - 1) as i:
                        iteration(i, False)
                    iteration(NI - 1, True)

            @block.vector
            def _(dve):
                def maxima(g, t, link, first=False, between=None):
                    k = t % 2
                    m = mx[:, k:k + 1]
                    if not first:
                        dve.wait_ge(exp_done, g - 1 + ONE)
                    if masked:
                        b = t // TB
                        dve.wait_ge(mask_ready, link.batch + b + 1 + ONE)
                    if topk:
                        if not first:
                            dve.wait_ge(rest_exp, g - 1 + ONE)
                        dve.wait_ge(copied, g + 1 + ONE)
                        settle(dve)
                        link(dve.max(top[:, 0, :], SS[:, k, :]))
                        dve.tensor_scalar(m, top[:, 0, 0:1], -1.0, None, ALU.mult).then_inc(max_ready, 1)
                        if between:
                            between()
                        link(dve.match_replace(rest[:, k, :], top[:, 0, :], SS[:, k, :], -3.0e38))
                        for r in range(1, 4):
                            link(dve.max(top[:, r, :], rest[:, k, :]))
                            last = dve.match_replace(rest[:, k, :], top[:, r, :], rest[:, k, :], -3.0e38)
                            if r < 3:
                                link(last)
                        last.then_inc(rest_ready, 1)
                        return
                    dve.wait_ge(scores_ready, g + 1 + ONE)
                    if masked:
                        settle(dve)
                        link(dve.tensor_tensor_reduce(out=SS[:, k, :], in0=psS[:, 0:K],
                                                      in1=maskf[:, t // TB % 2, :], scale=1.0, scalar=NEG * 4,
                                                      op0=ALU.add, op1=ALU.max, accum_out=m))
                        dve.tensor_scalar(m, m, -1.0, None, ALU.mult).then_inc(max_ready, 1)
                    else:
                        dve.tensor_reduce(m, psS[:, 0:K], X, ALU.max, negate=True).then_inc(max_ready, 1)

                def inverse(g, t):
                    k = t % 2
                    dve.wait_ge(us_ready, (g if t == 0 else g - 1) + ONE)
                    if topk:
                        dve.wait_ge(u_ready, g + 1 + ONE)
                        src = psU[:, D:D + 1]
                    else:
                        dve.wait_ge(exp_done, g + 1 + ONE)
                        src = ls[:, k:k + 1]
                    dve.reciprocal(li[:, k:k + 1], src).then_inc(li_ready, 1)

                def copy_ut(g, t):
                    dve.wait_ge(ut_turned, g + 1 + ONE)
                    dve.tensor_copy(UT[:, t // TB, t % TB, :], psZ[:, 0:128]).then_inc(ut_ready, 1)

                def add(i, b, j, link):
                    dve.wait_ge(y_ready, b + 1 + ONE)
                    r = slice(j * S, j * S + S)
                    xt = c.x[r, i, :] if isinstance(i, int) else c.x[r, ds(i, 1), :].rearrange("p a d -> p (a d)")
                    link(dve.tensor_tensor(xt, xt, psZ[r, 128:256], ALU.add))
                    dve.tensor_tensor(xt, xt, c.bias_row[r, :], ALU.add).then_inc(x_done, 1)

                def finish(i, t, link, first):
                    g = i * T
                    inverse(g + t, t)
                    if t == 9:
                        add(i, i * 2, 0, link)
                    if t == 1 and not first:
                        add(i - 1, i * 2 - 1, 1, link)
                    if t:
                        copy_ut(g + (t - 1), t - 1)
                    elif not first:
                        copy_ut(g - 1, T - 1)

                def iteration(i, first, final):
                    g = i * T
                    link = Link(dve, order, HEAD if first else i * LINKS + (HEAD - 1))
                    link.batch = i * 2
                    for t in range(T):
                        more = t + (2 if topk else 1) < T or not final
                        if topk and more:
                            maxima(g + (t + 2), t + 2, link, between=lambda: finish(i, t, link, first))
                        if not topk:
                            copy_weights(dve, dve.tensor_copy, g + t, t, 0)
                            copy_weights(dve, dve.tensor_copy, g + t, t, 1)
                            if more:
                                maxima(g + (t + 1), t + 1, link)
                        if not (topk and more):
                            finish(i, t, link, first)
                    assert final or link.n == LINKS - first, link.n
                    return link

                head = Link(dve, order)
                head.batch = 0
                maxima(0, 0, head, first=True)
                if topk:
                    maxima(1, 1, head, first=True)
                HEAD = head.n
                iteration(0, True, False)
                with dve.Fori(1, NI - 1) as i:
                    iteration(i, False, False)
                link = iteration(NI - 1, False, True)
                copy_ut(NI * T - 1, T - 1)
                add(NI - 1, B - 1, 1, link)
                dve.wait_ge(x_done, B + ONE)


def zero_bias(c):
    nc = c.nc
    z = c.sem("bias_zero")
    with nc.Block() as block:
        @block.gpsimd
        def _(pool):
            pool.memset(c.bias_row[:], 0.0).then_inc(z, 1)
            pool.wait_ge(z, 1 + ONE)


def wide_cross_attention(c, wq, wk, wv, wo, bo, scale, masked):
    with ExitStack() as st:
        M = c.sb(st, "M", [128, H, D])
        N = c.sb(st, "N", [128, H, D])
        with ExitStack() as s2:
            w = [c.sb(s2, f"w{n}", [128, 8, 128]) for n in range(4)]
            wT = [c.sb(s2, f"wT{n}", [128, 8, 128]) for n in range(3)]
            loads = [(w[n][:].rearrange("p a b -> p (a b)"), a) for n, a in enumerate((wq, wk, wv))]
            loads.append((w[3][:], wo.rearrange("(a p) d -> p a d", p=128)))
            if bo is not None:
                loads.append((c.bias_row[:], row_bcast(bo)))
            load_all(c, loads)
            if bo is None:
                zero_bias(c)
            turn_all(c, [(wT[n][:, a, :], w[n][:, a, :]) for n in range(3) for a in range(8)])

            def half(t, h):
                return t[(h % 2) * 64:(h % 2) * 64 + 64, h // 2, :]

            multiply_all(c, [(M[:, h, :], [(half(wT[0], h), half(wT[1], h))]) for h in range(H)]
                         + [(N[:, h, :], [(half(wT[2], h), half(w[3], h))]) for h in range(H)])
        cross_attention(c, M, N, scale, masked=masked)


def stage_l1_xattn(c):
    d = c.dram
    layernorm(c)
    wide_cross_attention(c, d["L1_xattn_Wq"], d["L1_xattn_Wk"], d["L1_xattn_Wv"], d["L1_xattn_Wo"],
                         d["L1_xattn_bo"], 0.125, True)


def stage_l2_xattn(c):
    d = c.dram
    layernorm(c)
    wide_cross_attention(c, d["L2_xattn_w_q"], d["L2_xattn_w_k"], d["L2_xattn_w_v"], d["L2_xattn_w_o"],
                         None, 0.125, False)


def stage_l3_xattn(c):
    nc, d = c.nc, c.dram
    layernorm(c)
    with ExitStack() as st:
        N = c.sb(st, "N3", [128, H, D])
        QT = c.sb(st, "QT", [128, B * S])
        WT = c.sb(st, "WT", [128, 3, D])
        bias = c.sb(st, "biases", [128, 3])
        with ExitStack() as s2:
            W = c.sb(s2, "W", [128, 4, D])
            WvN = c.sb(s2, "WvN", [128, D])
            bo = c.sb(s2, "bo", [128, D])
            bv_row = c.sb(s2, "bv_row", [128, 128])
            load_all(c, [(W[:, 0, :], d["L3_xattn_Wq"]), (W[:, 1, :], d["L3_xattn_Wk"]),
                         (W[:, 2, :], d["L3_xattn_Wo"]), (WvN[:], d["L3_xattn_Wv"]),
                         (bo[:], row_bcast(d["L3_xattn_bo"]))]
                     + [(bias[:, n:n + 1], d[f"L3_xattn_{v}"].rearrange("(p a) -> p a", a=1))
                        for n, v in enumerate(("bq", "bk", "bv"))])
            turn_all(c, [(WT[:, n, :], W[:, n, :]) for n in range(3)])
            head_blocks(c, s2, WvN[:], WT[:, 2, :], N)
            spread_bias(c, bias[:, 2:3], WT[:, 2, :], bo)
            project(c, QT, WT[:, 0, :], c.xnT, bias[:, 0:1], 8.0 ** -0.5)
        cross_attention(c, None, N, None, topk=(QT, WT[:, 1, :], bias[:, 1:2]))


def spread_bias(c, col, w, bo):
    nc = c.nc
    with ExitStack() as st:
        cols = c.sb(st, "bias_cols", [128, 128])
        pb = c.ps(st, "bias_ps", [128, D])
        made, summed, done = c.sem("cols_made"), c.sem("bias_summed"), c.sem("bias_done")
        with nc.Block() as block:
            @block.vector
            def _(dve):
                dve.tensor_scalar(cols[:], c.ones[:], col, None, ALU.mult).then_inc(made, 1)
                dve.wait_ge(summed, 1 + ONE)
                if bo is None:
                    dve.tensor_copy(c.bias_row[:], pb[:]).then_inc(done, 1)
                else:
                    dve.tensor_tensor(c.bias_row[:], pb[:], bo[:], ALU.add).then_inc(done, 1)
                dve.wait_ge(done, 1 + ONE)

            @block.tensor
            def _(pe):
                pe.wait_ge(made, 1 + ONE)
                pe.matmul(pb[:], cols[:], w, start=True, stop=True).then_inc(summed, 1)


def project(c, out, w, src, bias, scale):
    nc = c.nc
    with ExitStack() as st:
        pp = c.ps(st, "proj", [128, B * S])
        summed, done = c.sem("proj_summed"), c.sem("proj_done")
        with nc.Block() as block:
            @block.tensor
            def _(pe):
                for n in range(0, B * S, 512):
                    pe.matmul(pp[:, n:n + 512], w, src[:, n:n + 512], start=True, stop=True).then_inc(summed, 1)

            @block.vector
            def _(dve):
                dve.wait_ge(summed, B * S // 512 + ONE)
                if bias is None:
                    dve.tensor_scalar(out[:], pp[:], scale, None, ALU.mult).then_inc(done, 1)
                else:
                    dve.tensor_scalar(out[:], pp[:], bias, scale, ALU.add, ALU.mult).then_inc(done, 1)
                dve.wait_ge(done, 1 + ONE)


def attention_masks(c, st, kind):
    nc = c.nc
    mask = c.sb(st, "mask", [128, 1, S])
    flag = c.sb(st, "flag", [128, 1])
    order = c.sem("mask_order")
    with nc.Block() as block:
        @block.gpsimd
        def _(pool):
            link = Link(pool, order)
            link(pool.memset(mask[:], 0.0))
            link(pool.memset(flag[:], 1.0))
            for b in range(2):
                m = mask[b * S:b * S + S, 0, :]
                link(pool.affine_select(out=m, in_=m, compare_op=ALU.is_ge, fill=NEG, base=0,
                                        pattern=[[-1, S]], channel_multiplier=1))
                if kind == "h":
                    for k in range(0, S, 16):
                        mk = mask[b * S:b * S + S, 0, k:k + 16]
                        link(pool.affine_select(out=mk, in_=mk, compare_op=ALU.is_ge, fill=NEG, base=k + 15,
                                                pattern=[[0, 16]], channel_multiplier=-1))
                    f = flag[b * S:b * S + S, :]
                    link(pool.affine_select(out=f, in_=f, compare_op=ALU.is_ge, fill=0.0, base=-S // 2,
                                            pattern=[[0, 1]], channel_multiplier=1))
            if kind == "h":
                for e in range(0, 128, 2):
                    link(pool.affine_select(out=flag[:], in_=flag[:], compare_op=ALU.not_equal, fill=0.0,
                                            base=-e, pattern=[[0, 1]], channel_multiplier=1))
    return mask, flag


LINKS_SA = {"l0": 11, "l1": 7, "l2": 5, "h": 17}


def small_attention(c, kind, W, Wq=None, bq=None, Wk=None, bk=None, M=None, scale=1.0, bv_row=None, Wf=None):
    nc = c.nc
    V = 32 if kind == "l1" else D
    with ExitStack() as st:
        mask, flag = attention_masks(c, st, kind) if kind != "l2" else (None, None)
        xs = c.sb(st, "xs", [128, 128])
        qT = c.sb(st, "qT", [128, 128])
        kT = c.sb(st, "kT", [128, 128])
        Kb = c.sb(st, "Kb", [128, 2, H, S])
        Sm = c.sb(st, "Sm", [128, H, S])
        mx = c.sb(st, "mx", [128, H, 1])
        sm = c.sb(st, "sm", [128, H, 1])
        Pn = c.sb(st, "Pn", [128, H, S])
        PT = c.sb(st, "PT", [128, 8, 128])
        VW = c.sb(st, "VW", [128, 2, 8, 2 if kind == "l1" else 1, V])
        if kind == "l0":
            Ksq = c.sb(st, "Ksq", [128, 2, H, S])
            hmx = c.sb(st, "hmx", [128, H, S])
            qsq = c.sb(st, "qsq", [128, 128])
            qm2 = c.sb(st, "qm2", [128, 128])
        if kind == "l1":
            G = c.sb(st, "G", [128, 512])
            GT = c.sb(st, "GT", [128, 4, 128])
        if kind == "h":
            qh = c.sb(st, "qh", [128, H, 128])
            qc = c.sb(st, "qc", [128, H, 64, 2])
            xc = c.sb(st, "xc", [128, 2, 16])
            A1 = c.sb(st, "A1", [128, H, 16])
            mx1 = c.sb(st, "mx1", [128, H, 1])
            sm1 = c.sb(st, "sm1", [128, H, 1])
        psS = c.ps(st, "psS", [128, 2, 512])
        psD = c.ps(st, "psD", [128, 2, 512])
        psW = c.ps(st, "psW", [128, 2048])
        order, xs_ready, proj_ready, qk_ready = (c.sem(n) for n in ("order", "xs_ready", "proj_ready", "qk_ready"))
        kb_ready, s_ready, sq_ready = c.sem("kb_ready"), c.sem("s_ready"), c.sem("sq_ready")
        sub_ready, e_ready, pn_ready = c.sem("sub_ready"), c.sem("e_ready"), c.sem("pn_ready")
        v_ready, vw_ready, turned, pt_ready = (c.sem(n) for n in ("v_ready", "vw_ready", "turned", "pt_ready"))
        o_ready, g_ready, g_turned, gt_ready = (c.sem(n) for n in ("o_ready", "g_ready", "g_turned", "gt_ready"))
        x_done, pool_order, y_ready, o_added = (c.sem(n) for n in ("x_done", "pool_order", "y_ready", "o_added"))
        heads = 1 if kind == "l1" else H
        W2 = W.rearrange("p (a b) v -> p b a v", b=2)

        if kind in ("l0", "l1"):
            zeroed = c.sem("zeroed")
            with nc.Block() as block:
                @block.vector
                def _(dve):
                    if kind == "l1":
                        dve.memset(VW[:], 0.0).then_inc(zeroed, 1)
                    else:
                        dve.tensor_copy(hmx[:], bc(c.headmask[:].rearrange("p (h a) -> p h a", a=1), [128, H, S])
                                        ).then_inc(zeroed, 1)
                    dve.wait_ge(zeroed, 1 + ONE)

        with nc.Block() as block:
            @block.vector
            def _(dve):
                with dve.Fori(0, NT) as p:
                    link = Link(dve, order, p * LINKS_SA[kind])
                    dve.tensor_copy(xs[:], c.xnT[:, ds(p * 128, 128)]).then_inc(xs_ready, 1)
                    dve.wait_ge(xs_ready, p + 1 + ONE)
                    settle(dve)
                    if kind == "l0":
                        dve.wait_ge(proj_ready, p + 1 + ONE)
                        link(dve.tensor_scalar(qT[:], psW[:, 0:128], bq, None, ALU.add))
                        link(dve.tensor_tensor(qsq[:], qT[:], qT[:], ALU.mult))
                        link(dve.tensor_scalar(qm2[:], qT[:], -2.0, None, ALU.mult))
                        dve.tensor_scalar(kT[:], psW[:, 512:640], bk, None, ALU.add).then_inc(qk_ready, 1)
                    elif kind == "l1":
                        dve.wait_ge(proj_ready, p + 1 + ONE)
                        link(dve.tensor_copy(qT[:], xs[:]))
                        dve.tensor_scalar(kT[:], psW[:, 512:640], bk, None, ALU.add).then_inc(qk_ready, 1)
                    elif kind == "l2":
                        link(dve.tensor_scalar(qT[:], xs[:], scale, None, ALU.mult))
                        dve.tensor_copy(kT[:], xs[:]).then_inc(qk_ready, 1)
                    else:
                        for b in range(2):
                            pair = xs[:, b * S:b * S + 32].rearrange("p (a b) -> p a b", b=2)
                            link(dve.tensor_tensor(xc[:, b, :], pair[:, :, 0], pair[:, :, 1], ALU.add))
                        link(dve.tensor_scalar(xc[:], xc[:], 0.5, None, ALU.mult))
                        dve.wait_ge(proj_ready, p + 1 + ONE)
                        link(dve.tensor_scalar(qh[:].rearrange("p h t -> p (h t)"), psW[:], scale, None, ALU.mult))
                        pair = qh[:].rearrange("p h (a b) -> p h a b", b=2)
                        link(dve.tensor_tensor(qc[:, :, :, 0], pair[:, :, :, 0], pair[:, :, :, 1], ALU.add))
                        link(dve.tensor_scalar(qc[:, :, :, 0], qc[:, :, :, 0], 0.5, None, ALU.mult))
                        dve.tensor_copy(qc[:, :, :, 1], qc[:, :, :, 0]).then_inc(qk_ready, 1)

                    dve.wait_ge(s_ready, p + 1 + ONE)
                    scores = psS[:].rearrange("p a (h k) -> p (a h) k", k=S)
                    if kind == "l0":
                        link(dve.tensor_scalar(Sm[:].rearrange("p h k -> p (h k)"),
                                               psD[:].rearrange("p a b -> p (a b)"), 1e-6, None, ALU.add))
                        link(dve.reciprocal(Sm[:], Sm[:]))
                        dve.wait_ge(sq_ready, p + 1 + ONE)
                        link(dve.tensor_tensor(Sm[:], Sm[:], Pn[:], ALU.mult))
                        scores = Sm[:]
                    if kind != "l2":
                        link(dve.tensor_tensor(Sm[:], scores, bc(mask[:], [128, H, S]), ALU.add))
                        scores = Sm[:]
                    link(dve.reduce_max(mx[:, :, 0], scores, axis=X))
                    dve.tensor_tensor(Sm[:], scores, bc(mx[:], [128, H, S]), ALU.subtract).then_inc(sub_ready, 1)
                    if kind == "h":
                        s1 = psD[:, 0, 0:256].rearrange("p (h k) -> p h k", k=16)
                        link(dve.reduce_max(mx1[:, :, 0], s1, axis=X))
                        dve.tensor_tensor(A1[:], s1, bc(mx1[:], [128, H, 16]), ALU.subtract).then_inc(sub_ready, 1)
                    dve.wait_ge(e_ready, (p + 1) * (2 if kind == "h" else 1) + ONE)
                    link(dve.reduce_sum(sm[:, :, 0], Pn[:], axis=X))
                    if kind == "h":
                        link(dve.reduce_sum(sm1[:, :, 0], A1[:], axis=X))
                        link(dve.tensor_scalar(sm1[:], sm1[:], flag[:], 1e-8, ALU.mult, ALU.add))
                        link(dve.tensor_tensor(sm[:], sm[:], sm1[:], ALU.add))
                        pairs = Pn[:, :, 0:32].rearrange("p h (a b) -> p h a b", b=2)
                        for e in range(2):
                            link(dve.scalar_tensor_tensor(out=pairs[:, :, :, e], in0=A1[:], scalar=flag[:],
                                                          in1=pairs[:, :, :, e], op0=ALU.mult, op1=ALU.add))
                    link(dve.reciprocal(sm[:, :, 0], sm[:, :, 0]))
                    dve.tensor_tensor(Pn[:], Pn[:], bc(sm[:], [128, H, S]), ALU.mult).then_inc(pn_ready, 1)
                    dve.wait_ge(turned, p + 1 + ONE)
                    dve.tensor_copy(PT[:].rearrange("p a t -> p (a t)"), psW[:, 0:1024]).then_inc(pt_ready, 1)
                    dve.wait_ge(o_ready, p + 1 + ONE)
                    xt = c.x[:, ds(p, 1), :].rearrange("p a d -> p (a d)")
                    if kind == "l1":
                        dve.tensor_tensor(G[:], psS[:, 0, :], bv_row, ALU.add).then_inc(o_added, 1)
                        dve.wait_ge(g_turned, p + 1 + ONE)
                        dve.tensor_copy(GT[:].rearrange("p a t -> p (a t)"), psW[:, 0:512]).then_inc(gt_ready, 1)
                        dve.wait_ge(y_ready, p + 1 + ONE)
                        link(dve.tensor_tensor(xt, xt, psS[:, 1, 0:128], ALU.add))
                        link(dve.tensor_tensor(xt, xt, c.xn[:, ds(p, 1), :].rearrange("p a d -> p (a d)"), ALU.add))
                    else:
                        link(dve.tensor_tensor(xt, xt, psS[:, 0, 0:128], ALU.add))
                    dve.tensor_tensor(xt, xt, c.bias_row[:], ALU.add).then_inc(x_done, 1)
                    assert link.n == LINKS_SA[kind], (kind, link.n)
                dve.wait_ge(x_done, NT + ONE)

            @block.gpsimd
            def _(pool):
                if kind == "h":
                    return
                with pool.Fori(0, NT) as p:
                    pool.wait_ge(qk_ready, p + 1 + ONE)
                    for b in range(2):
                        pool.tensor_tensor(
                            Kb[:, b], bc(kT[:, b * S:b * S + S].rearrange("p (a s) -> p a s", a=1), [128, H, S]),
                            bc(c.headmask[:].rearrange("p (h a) -> p h a", a=1), [128, H, S]), ALU.mult
                            ).then_inc(pool_order, 1)
                    if kind == "l0":
                        pool.wait_ge(pool_order, p * 2 + 2 + ONE)
                        pool.tensor_tensor(Ksq[:], Kb[:], Kb[:], ALU.mult).then_inc(kb_ready, 1)

            @block.scalar
            def _(act):
                with act.Fori(0, NT) as p:
                    for b in range(2):
                        act.wait_ge(v_ready, p * 2 + b + 1 + ONE)
                        if kind == "l1":
                            for e in range(2):
                                r = slice(e * 64, e * 64 + 64)
                                last = act.activation(VW[r, b, :, e, :],
                                                      psW[r, 1024:1280].rearrange("p (a v) -> p a v", v=V), ACT.Copy)
                        else:
                            last = act.activation(VW[:, b].rearrange("p a c v -> p (a c v)"), psW[:, 1024:2048],
                                                  ACT.Copy)
                        last.then_inc(vw_ready, 1)
                    if kind == "l0":
                        act.wait_ge(s_ready, p + 1 + ONE)
                        act.activation(Pn[:].rearrange("p h k -> p (h k)"), psS[:].rearrange("p a b -> p (a b)"),
                                       ACT.Square).then_inc(sq_ready, 1)
                    act.wait_ge(sub_ready, p * (2 if kind == "h" else 1) + 1 + ONE)
                    act.activation(Pn[:], Sm[:], ACT.Exp).then_inc(e_ready, 1)
                    if kind == "h":
                        act.wait_ge(sub_ready, p * 2 + 2 + ONE)
                        act.activation(A1[:], A1[:], ACT.Exp).then_inc(e_ready, 1)
                    if kind == "l1":
                        act.wait_ge(o_added, p + 1 + ONE)
                        act.activation(G[:], G[:], ACT.Gelu).then_inc(g_ready, 1)

            @block.tensor
            def _(pe):
                with pe.Fori(0, NT) as p:
                    pe.wait_ge(xs_ready, p + 1 + ONE)
                    if kind == "l0":
                        pe.matmul(psW[:, 0:128], Wq, xs[:], start=True, stop=True)
                    if kind in ("l0", "l1"):
                        pe.matmul(psW[:, 512:640], Wk, xs[:], start=True, stop=True).then_inc(proj_ready, 1)
                    if kind == "h":
                        for h in range(H):
                            last = pe.matmul(psW[:, h * 128:h * 128 + 128], M[:, h, :], xs[:], start=True, stop=True)
                        last.then_inc(proj_ready, 1)
                    pe.wait_ge(qk_ready, p + 1 + ONE)
                    if kind != "h":
                        pe.wait_ge(pool_order, p * 2 + 2 + ONE)
                    if kind == "l0":
                        pe.wait_ge(kb_ready, p + 1 + ONE)
                    pe.wait_ge(x_done, p + ONE)
                    for b in range(2):
                        r = slice(b * S, b * S + S)
                        if kind == "h":
                            for h in range(H):
                                pe.matmul(psS[r, h // 8, (h % 8) * S:(h % 8) * S + S], qh[:, h, r], xs[:, r],
                                          start=True, stop=True)
                                last = pe.matmul(psD[r, 0, h * 16:h * 16 + 16],
                                                 qc[:].rearrange("p h a b -> p h (a b)")[:, h, r],
                                                 xc[:, b, :], start=True, stop=True)
                            continue
                        for n in range(2):
                            hs = slice(8 * n, 8 * n + 8)
                            last = pe.matmul(psS[r, n, :], qT[:, r], Kb[:, b, hs, :], start=True, stop=True)
                            if kind == "l0":
                                pe.matmul(psD[r, n, :], c.ones[:, 0:S], Ksq[:, b, hs, :], start=True, stop=False)
                                pe.matmul(psD[r, n, :], qsq[:, r], hmx[:, hs, :], start=False, stop=False)
                                last = pe.matmul(psD[r, n, :], qm2[:, r], Kb[:, b, hs, :], start=False, stop=True)
                    last.then_inc(s_ready, 1)
                    for b in range(2):
                        pe.wait_ge(vw_ready, p * 2 + b + ONE)
                        for e in range(2):
                            for n in range(0, 8 * V, 512):
                                w = min(512, 8 * V)
                                hs = slice(n // V, (n + w) // V)
                                last = pe.matmul(psW[e * 64:e * 64 + 64, 1024 + n:1024 + n + w],
                                                 xs[:, b * S:b * S + S], W2[:, e, hs, :], start=True, stop=True)
                        last.then_inc(v_ready, 1)
                    pe.wait_ge(pn_ready, p + 1 + ONE)
                    for a in range(8):
                        last = pe.transpose(psW[:, a * 128:a * 128 + 128],
                                            Pn[:, 2 * a:2 * a + 2, :].rearrange("p h k -> p (h k)"), c.ident[:])
                    last.then_inc(turned, 1)
                    pe.wait_ge(pt_ready, p + 1 + ONE)
                    pe.wait_ge(vw_ready, p * 2 + 2 + ONE)
                    for b in range(2):
                        r = slice(b * S, b * S + S)
                        for a in range(8):
                            if kind == "l1":
                                last = pe.matmul(psS[r, 0, a * 64:a * 64 + 64], PT[:, a, r],
                                                 VW[:, b, a].rearrange("p c v -> p (c v)"), start=True, stop=True)
                            else:
                                last = pe.matmul(psS[r, 0, 0:128], PT[:, a, r], VW[:, b, a, 0, :],
                                                 start=(a == 0), stop=(a == 7))
                    last.then_inc(o_ready, 1)
                    if kind == "l1":
                        pe.wait_ge(g_ready, p + 1 + ONE)
                        for a in range(4):
                            last = pe.transpose(psW[:, a * 128:a * 128 + 128], G[:, a * 128:a * 128 + 128], c.ident[:])
                        last.then_inc(g_turned, 1)
                        pe.wait_ge(gt_ready, p + 1 + ONE)
                        for a in range(4):
                            last = pe.matmul(psS[:, 1, 0:128], GT[:, a, :], Wf[:, a, :], start=(a == 0), stop=(a == 3))
                        last.then_inc(y_ready, 1)


def stage_l0_attn(c):
    d = c.dram
    layernorm(c)
    with ExitStack() as st:
        W = c.sb(st, "W", [128, H, D])
        Wqkv = c.sb(st, "Wqkv", [128, 3, D])
        bias = c.sb(st, "bias", [128, 3])
        with ExitStack() as s2:
            Wo = c.sb(s2, "Wo", [128, D])
            bo = c.sb(s2, "bo", [128, D])
            WvT = c.sb(s2, "WvT", [128, D])
            load_all(c, [(Wqkv[:].rearrange("p a d -> p (a d)"), d["L0_attn_w_qkv"]), (Wo[:], d["L0_attn_w_out"]),
                         (bo[:], row_bcast(d["L0_attn_b_out"]))]
                     + [(bias[:, n:n + 1], d["L0_attn_b_qkv"][n * D:n * D + D].rearrange("(p a) -> p a", a=1))
                        for n in range(3)])
            turn_all(c, [(WvT[:], Wqkv[:, 2, :])])
            head_blocks(c, s2, WvT[:], Wo[:], W)
            spread_bias(c, bias[:, 2:3], Wo[:], bo)
        small_attention(c, "l0", W[:], Wq=Wqkv[:, 0, :], bq=bias[:, 0:1], Wk=Wqkv[:, 1, :], bk=bias[:, 1:2])


def stage_l1_attn(c):
    d = c.dram
    layernorm(c)
    with ExitStack() as st:
        W = c.sb(st, "W", [128, H, 32])
        Wk = c.sb(st, "Wk", [128, D])
        bk = c.sb(st, "bk", [128, 1])
        bv = c.sb(st, "bv", [128, 512])
        Wf = c.sb(st, "Wf", [128, 4, D])
        load_all(c, [(W[:].rearrange("p h v -> p (h v)"), d["L1_attn_Wv"]), (Wk[:], d["L1_attn_Wk"]),
                     (bk[:], d["L1_attn_bk"].rearrange("(p a) -> p a", a=1)), (bv[:], row_bcast(d["L1_attn_bv"])),
                     (Wf[:], d["L1_attn_Wf"].rearrange("(a p) d -> p a d", p=128)),
                     (c.bias_row[:], row_bcast(d["L1_attn_bf"]))])
        small_attention(c, "l1", W[:], Wk=Wk[:], bk=bk[:], bv_row=bv[:], Wf=Wf)


def stage_l2_attn(c):
    d = c.dram
    layernorm(c)
    with ExitStack() as st:
        W = c.sb(st, "W", [128, H, D])
        load_all(c, [(W[:], d["L2_attn_weight"].rearrange("(h p) d -> p h d", p=128))])
        zero_bias(c)
        small_attention(c, "l2", W[:], scale=8.0 ** -0.5)


def stage_l3_attn(c):
    d = c.dram
    layernorm(c)
    with ExitStack() as st:
        M = c.sb(st, "M", [128, H, D])
        W = c.sb(st, "W", [128, H, D])
        with ExitStack() as s2:
            w = c.sb(s2, "w", [128, 3, 8, D])
            wo = c.sb(s2, "wo", [128, 8, 128])
            woT = c.sb(s2, "woT", [128, 8, 128])
            load_all(c, [(w[:].rearrange("p q a d -> p (q a) d"),
                          d["L3_attn_w_qkv"].rearrange("(a p) d -> p a d", p=128)),
                         (wo[:].rearrange("p a b -> p (a b)"), d["L3_attn_w_out"]),
                         (c.bias_row[:], row_bcast(d["L3_attn_b_out"]))])
            turn_all(c, [(woT[:, a, :], wo[:, a, :]) for a in range(8)])

            def half(t, h):
                return t[(h % 2) * 64:(h % 2) * 64 + 64, h // 2, :]

            multiply_all(c, [(M[:, h, :], [(half(w[:, 0], h), half(w[:, 1], h))]) for h in range(H)]
                         + [(W[:, h, :], [(half(w[:, 2], h), half(woT, h))]) for h in range(H)])
        small_attention(c, "h", W[:], M=M, scale=0.125)


def route(c, st, Wr, br, weights, cap=None):
    nc = c.nc
    coef = c.sb(st, "coef", [128, NT, E])
    with ExitStack() as s:
        p = c.sb(s, "p", [128, NT, E])
        rest = c.sb(s, "rest", [128, NT, E])
        first = c.sb(s, "first", [128, 2, NT, E])
        rank = c.sb(s, "rank", [128, NT, E])
        m = c.sb(s, "m", [128, 2, NT, 1])
        r = c.sb(s, "r", [128, NT, 1])
        tri = c.sb(s, "tri", [128, 128])
        off = c.sb(s, "off", [128, 2, NT + 1, E])
        ps = c.ps(s, "logits", [128, NT * E])
        pc = c.ps(s, "counts", [128, 4, NT * E])
        made, order, logits, sub, expd = (c.sem(n) for n in ("made", "order", "logits", "sub", "expd"))
        picked, counted, done = c.sem("picked"), c.sem("counted"), c.sem("done")
        with nc.Block() as block:
            @block.gpsimd
            def _(pool):
                link = Link(pool, made)
                link(pool.iota(rank[:], pattern=[[0, NT], [-1, E]], base=E, channel_multiplier=0,
                               allow_small_or_imprecise_dtypes=True))
                link(pool.memset(tri[:], 1.0))
                link(pool.affine_select(out=tri[:], in_=tri[:], compare_op=ALU.is_ge, fill=0.0, base=0,
                                        pattern=[[1, 128]], channel_multiplier=-1))

            @block.tensor
            def _(pe):
                for t in range(NT):
                    last = pe.matmul(ps[:, t * E:t * E + E], c.xnT[:, t * 128:t * 128 + 128], Wr,
                                     start=True, stop=True)
                last.then_inc(logits, 1)
                if cap:
                    pe.wait_ge(picked, 1 + ONE)
                    pe.wait_ge(made, 3 + ONE)
                    for k in range(2):
                        f = first[:, k].rearrange("p t e -> p (t e)")
                        pe.matmul(pc[:, k, :], tri[:], f, start=True, stop=True)
                        last = pe.matmul(pc[:, 2 + k, :], c.ones[:], f, start=True, stop=True)
                    last.then_inc(counted, 1)

            @block.scalar
            def _(act):
                act.wait_ge(sub, 1 + ONE)
                act.activation(p[:], p[:], ACT.Exp).then_inc(expd, 1)

            @block.vector
            def _(dve):
                link = Link(dve, order)
                dve.wait_ge(logits, 1 + ONE)
                link(dve.tensor_copy(p[:].rearrange("p t e -> p (t e)"), ps[:]))
                if br is not None:
                    link(dve.tensor_tensor(p[:], p[:], bc(br, [128, NT, E]), ALU.add))
                link(dve.reduce_max(r[:, :, 0], p[:], axis=X))
                dve.tensor_tensor(p[:], p[:], bc(r[:], [128, NT, E]), ALU.subtract).then_inc(sub, 1)
                dve.wait_ge(expd, 1 + ONE)
                link(dve.reduce_sum(r[:, :, 0], p[:], axis=X))
                link(dve.reciprocal(r[:, :, 0], r[:, :, 0]))
                link(dve.tensor_tensor(p[:], p[:], bc(r[:], [128, NT, E]), ALU.mult))
                link(dve.tensor_copy(rest[:], p[:]))
                dve.wait_ge(made, 3 + ONE)
                for k in range(2):
                    f = first[:, k]
                    link(dve.reduce_max(m[:, k, :, 0], rest[:], axis=X))
                    link(dve.tensor_tensor(f, rest[:], bc(m[:, k], [128, NT, E]), ALU.is_equal))
                    link(dve.tensor_tensor(f, f, rank[:], ALU.mult))
                    link(dve.reduce_max(r[:, :, 0], f, axis=X))
                    link(dve.tensor_tensor(f, f, bc(r[:], [128, NT, E]), ALU.is_equal))
                    if k == 0:
                        link(dve.scalar_tensor_tensor(out=rest[:], in0=f, scalar=-2.0, in1=rest[:],
                                                      op0=ALU.mult, op1=ALU.add))
                if cap:
                    link(dve.tensor_tensor(r[:], m[:, 0], m[:, 1], ALU.add))
                    link(dve.reciprocal(r[:, :, 0], r[:, :, 0]))
                    link(dve.tensor_tensor(p[:], p[:], bc(r[:], [128, NT, E]), ALU.mult))
                    dve.memset(off[:, 0, 0, :], 0.0).then_inc(picked, 1)
                    dve.wait_ge(counted, 1 + ONE)
                    for k in range(2):
                        if k:
                            link(dve.tensor_copy(off[:, 1, 0, :], off[:, 0, NT, :]))
                        for t in range(NT):
                            link(dve.tensor_tensor(off[:, k, t + 1, :], off[:, k, t, :],
                                                   pc[:, 2 + k, t * E:t * E + E], ALU.add))
                        link(dve.tensor_tensor(rest[:].rearrange("p t e -> p (t e)"),
                                               off[:, k, 0:NT, :].rearrange("p t e -> p (t e)"),
                                               pc[:, k, :], ALU.add))
                        link(dve.tensor_scalar(rest[:], rest[:], float(cap), None, ALU.is_le))
                        link(dve.tensor_tensor(first[:, k], first[:, k], rest[:], ALU.mult))
                link(dve.tensor_tensor(coef[:], first[:, 0], first[:, 1], ALU.add))
                if weights != "one":
                    link(dve.tensor_tensor(coef[:], coef[:], p[:], ALU.mult))
    return coef


def add_expert_bias(c, coef, b):
    nc = c.nc
    with ExitStack() as st:
        cT = c.sb(st, "coefT", [E, NT, 128])
        pb = c.ps(st, "pb", [128, NT, 128])
        summed, added = c.sem("bias_summed"), c.sem("bias_added")
        turn_all(c, [(cT[:, t, :], coef[:, t, :]) for t in range(NT)])
        with nc.Block() as block:
            @block.tensor
            def _(pe):
                for t in range(NT):
                    last = pe.matmul(pb[:, t, :], cT[:, t, :], b, start=True, stop=True)
                last.then_inc(summed, 1)

            @block.vector
            def _(dve):
                dve.wait_ge(summed, 1 + ONE)
                dve.tensor_tensor(c.x[:], c.x[:], pb[:], ALU.add).then_inc(added, 1)
                dve.wait_ge(added, 1 + ONE)


def experts(c, coef, w1, w2, C, func, b1=None):
    nc = c.nc
    turn = b1 is not None
    with ExitStack() as st:
        w1n = c.sb(st, "w1n", [128, 2, C, 128])
        w2n = c.sb(st, "w2n", [128, 2, C, 128])
        w1T = c.sb(st, "w1T", [128, 2, C, 128]) if turn else w1n
        hT = c.sb(st, "hT", [128, 2, C, 512])
        ce = c.sb(st, "ce", [128, 2, NT])
        be = c.sb(st, "be", [128, 2, C])
        psH = c.ps(st, "psH", [128, C, 512])
        psY = c.ps(st, "psY", [128, 2, 512])
        psX = c.ps(st, "psX", [128, 512])
        loaded = [c.sem("w_loaded0"), c.sem("w_loaded1")]
        w1_turned, w1_ready, coef_ready = c.sem("w1_turned"), c.sem("w1_ready"), c.sem("coef_ready")
        h_ready, h_done, y_ready, y_used = (c.sem(n) for n in ("h_ready", "h_done", "y_ready", "y_used"))
        with nc.Block() as block:
            def load(sp, e, j):
                sp.dma_start(w1n[:, j], w1[ds(e, 1)].rearrange("e (c p) d -> p (e c) d", p=128)
                             ).then_inc(loaded[j], 16)
                sp.dma_start(w2n[:, j], w2[ds(e, 1)].rearrange("e (c p) d -> p (e c) d", p=128)
                             ).then_inc(loaded[j], 16)

            @block.sync
            def _(sp):
                load(sp, 0, 0)
                load(sp, 1, 1)
                with sp.Fori(0, E // 2 - 1) as i:
                    for j in range(2):
                        sp.wait_ge(y_ready, i * 4 + (2 * j + 2) + ONE)
                        settle(sp)
                        load(sp, i * 2 + (2 + j), j)

            @block.tensor
            def _(pe):
                with pe.Fori(0, E // 2) as i:
                    def up(k):
                        j, half = k // 2, k % 2
                        if half == 0:
                            pe.wait_ge(loaded[j], (i + 1) * 32 + ONE)
                            if turn:
                                for q in range(C):
                                    last = pe.transpose(psX[:, q * 128:q * 128 + 128], w1n[:, j, q, :], c.ident[:])
                                last.then_inc(w1_turned, 1)
                                pe.wait_ge(w1_ready, i * 2 + (j + 1) + ONE)
                        pe.wait_ge(h_done, (i * 4 + k) * C + ONE)
                        for q in range(C):
                            pe.matmul(psH[:, q, :], w1T[:, j, q, :], c.xnT[:, half * 512:half * 512 + 512],
                                      start=True, stop=True).then_inc(h_ready, 1)

                    def down(k):
                        j = k // 2
                        pe.wait_ge(h_done, (i * 4 + k + 1) * C + ONE)
                        pe.wait_ge(y_used, i * 4 + (k - 1 if k else 0) + ONE)
                        for t in range(4):
                            for q in range(C):
                                last = pe.matmul(psY[:, k % 2, t * 128:t * 128 + 128],
                                                 hT[:, k % 2, q, t * 128:t * 128 + 128], w2n[:, j, q, :],
                                                 start=(q == 0), stop=(q == C - 1))
                        last.then_inc(y_ready, 1)

                    for k in range(5):
                        if k < 4:
                            up(k)
                        if k:
                            down(k - 1)

            @block.scalar
            def _(act):
                with act.Fori(0, E // 2) as i:
                    for k in range(4):
                        j = k // 2
                        if k % 2 == 0:
                            act.wait_ge(coef_ready, i * 2 + (j + 1) + ONE)
                        act.wait_ge(y_ready, i * 4 + (k - 1 if k else 0) + ONE)
                        for q in range(C):
                            act.wait_ge(h_ready, (i * 4 + k) * C + (q + 1) + ONE)
                            act.activation(hT[:, k % 2, q, :], psH[:, q, :], func,
                                           bias=be[:, j, q:q + 1] if turn else 0.0).then_inc(h_done, 1)

            @block.vector
            def _(dve):
                with dve.Fori(0, E // 2) as i:
                    def prepare(j):
                        dve.wait_ge(y_used, i * 4 + ONE)
                        dve.wait_ge(h_done, i * (4 * C) + ONE)
                        if turn:
                            dve.tensor_copy(be[:, j, :], b1[:, ds(i * 2 + j, 1), :].rearrange("p a q -> p (a q)"))
                        dve.tensor_copy(ce[:, j, :], coef[:, :, ds(i * 2 + j, 1)].rearrange("p t a -> p (t a)")
                                        ).then_inc(coef_ready, 1)
                        if turn:
                            dve.wait_ge(w1_turned, i * 2 + (j + 1) + ONE)
                            dve.tensor_copy(w1T[:, j].rearrange("p q d -> p (q d)"), psX[:, 0:C * 128]
                                            ).then_inc(w1_ready, 1)

                    def add(k):
                        j, half = k // 2, k % 2
                        dve.wait_ge(coef_ready, i * 2 + (j + 1) + ONE)
                        dve.wait_ge(y_used, i * 4 + k + ONE)
                        dve.wait_ge(y_ready, i * 4 + (k + 1) + ONE)
                        for t in range(4):
                            tt = half * 4 + t
                            last = dve.scalar_tensor_tensor(
                                out=c.x[:, tt, :], in0=psY[:, k % 2, t * 128:t * 128 + 128],
                                scalar=ce[:, j, tt:tt + 1], in1=c.x[:, tt, :], op0=ALU.mult, op1=ALU.add)
                        last.then_inc(y_used, 1)

                    prepare(0)
                    add(0)
                    prepare(1)
                    for k in range(1, 4):
                        add(k)
                dve.wait_ge(y_used, 2 * E + ONE)


def stage_l1_ffn(c):
    d = c.dram
    layernorm(c)
    with ExitStack() as st:
        b1 = c.sb(st, "b1", [128, E, 4])
        b2 = c.sb(st, "b2", [E, D])
        Wr = c.sb(st, "Wr", [128, E])
        with ExitStack() as s2:
            g = c.sb(s2, "g", [E, D])
            b1n = c.sb(s2, "b1n", [32, 128])
            load_all(c, [(g[:], d["L1_ffn_gate_w"]), (b1n[:], d["L1_ffn_fc1_b"].rearrange("e a (q p) -> (e a q) p", p=128)),
                         (b2[:], d["L1_ffn_fc2_b"].rearrange("e a d -> (e a) d"))])
            turn_all(c, [(Wr[:], g[:]), (b1[:].rearrange("p e q -> p (e q)"), b1n[:])])
        cap = 2 * ((B * S + E - 1) // E)
        coef = route(c, st, Wr[:], None, "share", cap)
        add_expert_bias(c, coef, b2[:])
        experts(c, coef, d["L1_ffn_fc1_w"], d["L1_ffn_fc2_w"], 4, ACT.Relu, b1=b1)


def stage_l2_ffn(c):
    nc, d = c.nc, c.dram
    layernorm(c)
    with ExitStack() as st:
        Wr = c.sb(st, "Wr", [128, E])
        br = c.sb(st, "br", [128, 1, E])
        be = c.sb(st, "be", [E, D])
        g = c.sb(st, "g", [E, D])
        We = c.sb(st, "We", [128, E, D])
        WeT = c.sb(st, "WeT", [128, E, D])
        load_all(c, [(g[:], d["L2_ffn_w_router"]), (br[:, 0, :], row_bcast(d["L2_ffn_b_router"])),
                     (be[:], d["L2_ffn_b_experts"]), (We[:], d["L2_ffn_w_experts"].rearrange("e o d -> o e d"))])
        turn_all(c, [(Wr[:], g[:])] + [(WeT[:, e, :], We[:, e, :]) for e in range(E)])
        coef = route(c, st, Wr[:], br[:], "one")
        add_expert_bias(c, coef, be[:])
        ps = c.ps(st, "psE", [128, 2, E * D])
        made, used = c.sem("made"), c.sem("used")
        flat = WeT[:].rearrange("p e d -> p (e d)")
        with nc.Block() as block:
            @block.tensor
            def _(pe):
                for t in range(NT):
                    if t >= 2:
                        pe.wait_ge(used, E * (t - 1) + ONE)
                    for n in range(0, E * D, 512):
                        last = pe.matmul(ps[:, t % 2, n:n + 512], c.xnT[:, t * 128:t * 128 + 128],
                                         flat[:, n:n + 512], start=True, stop=True)
                    last.then_inc(made, 1)

            @block.vector
            def _(dve):
                for t in range(NT):
                    dve.wait_ge(made, t + 1 + ONE)
                    for e in range(E):
                        dve.scalar_tensor_tensor(out=c.x[:, t, :], in0=ps[:, t % 2, e * D:e * D + D],
                                                 scalar=coef[:, t, e:e + 1], in1=c.x[:, t, :],
                                                 op0=ALU.mult, op1=ALU.add).then_inc(used, 1)
                        dve.wait_ge(used, E * t + e + 1 + ONE)


def stage_l3_ffn(c):
    nc, d = c.nc, c.dram
    layernorm(c)
    with ExitStack() as st:
        Wr = c.sb(st, "Wr", [128, E])
        load_all(c, [(Wr[:], d["L3_ffn_router_w"])])
        coef = route(c, st, Wr[:], None, "prob")
        experts(c, coef, d["L3_ffn_w1"], d["L3_ffn_w2"], 1, ACT.Silu)
        gu = c.sb(st, "gu", [128, 2, 128])
        down = c.sb(st, "down", [128, D])
        gw = c.sb(st, "gw", [128, 1])
        gate = c.sb(st, "gate", [128, B * S])
        sg = c.sb(st, "sg", [128, NT])
        psG = c.ps(st, "psG", [128, B * S])
        psUp = c.ps(st, "psUp", [128, B * S])
        psY = c.ps(st, "psY", [128, NT, D])
        psg = c.ps(st, "psg", [128, NT])
        made, gated, ready, summed, done = (c.sem(n) for n in ("made", "gated", "ready", "summed", "done"))
        load_all(c, [(gu[:].rearrange("p a f -> p (a f)"), d["L3_ffn_shared_gate_up"]),
                     (down[:], d["L3_ffn_shared_down"]), (gw[:], d["L3_ffn_shared_gate_w"])])
        with nc.Block() as block:
            @block.tensor
            def _(pe):
                for n in range(0, B * S, 512):
                    pe.matmul(psG[:, n:n + 512], gu[:, 0, :], c.xnT[:, n:n + 512], start=True, stop=True)
                    pe.matmul(psUp[:, n:n + 512], gu[:, 1, :], c.xnT[:, n:n + 512], start=True, stop=True)
                for t in range(NT):
                    last = pe.matmul(psg[:, t:t + 1], c.xnT[:, t * 128:t * 128 + 128], gw[:], start=True, stop=True)
                last.then_inc(made, 1)
                pe.wait_ge(ready, 1 + ONE)
                for t in range(NT):
                    last = pe.matmul(psY[:, t, :], gate[:, t * 128:t * 128 + 128], down[:], start=True, stop=True)
                last.then_inc(summed, 1)

            @block.scalar
            def _(act):
                act.wait_ge(made, 1 + ONE)
                act.activation(gate[:], psG[:], ACT.Silu).then_inc(gated, 1)
                act.activation(sg[:], psg[:], ACT.Sigmoid).then_inc(gated, 1)

            @block.vector
            def _(dve):
                dve.wait_ge(gated, 2 + ONE)
                dve.tensor_tensor(gate[:], gate[:], psUp[:], ALU.mult).then_inc(ready, 1)
                dve.wait_ge(summed, 1 + ONE)
                for t in range(NT):
                    last = dve.scalar_tensor_tensor(out=c.x[:, t, :], in0=psY[:, t, :], scalar=sg[:, t:t + 1],
                                                    in1=c.x[:, t, :], op0=ALU.mult, op1=ALU.add)
                last.then_inc(done, 1)
                dve.wait_ge(done, 1 + ONE)


def quantize(dve, link, v, a, q, s, r):
    shape = list(v.shape)
    link(dve.tensor_reduce(s[:, :, 0], v, X, ALU.max, apply_absolute_value=True))
    link(dve.tensor_scalar(s, s, 1.0 / 6.0, 1e-12, ALU.mult, ALU.max))
    link(dve.reciprocal(r, s))
    link(dve.tensor_tensor(v, v, bc(r, shape), ALU.mult))
    link(dve.scalar_tensor_tensor(out=a, in0=v, scalar=-1.0, in1=v, op0=ALU.mult, op1=ALU.max))
    link(dve.tensor_scalar(q, a, 5.0, 2.0, ALU.is_gt, ALU.mult))
    for mid in (3.5, 2.5):
        link(dve.scalar_tensor_tensor(out=q, in0=a, scalar=mid, in1=q, op0=ALU.is_gt, op1=ALU.add))
    link(dve.tensor_scalar(q, q, 2.0, None, ALU.mult))
    for mid in (1.75, 1.25, 0.75, 0.25):
        link(dve.scalar_tensor_tensor(out=q, in0=a, scalar=mid, in1=q, op0=ALU.is_gt, op1=ALU.add))
    link(dve.tensor_scalar(v, v, 0.0, -0.5, ALU.is_ge, ALU.add))
    link(dve.tensor_tensor(v, v, q, ALU.mult))
    link(dve.tensor_tensor(v, v, bc(s, shape), ALU.mult))


def stage_l0_ffn(c):
    nc, d = c.nc, c.dram
    I = 352
    IC = [(0, 128), (128, 128), (256, 96)]
    layernorm(c)
    with ExitStack() as st:
        wT = c.sb(st, "wT", [128, 2, I])
        wdT = c.sb(st, "wdT", [128, 3, D])
        h = c.sb(st, "h", [128, NT, I])
        u = c.sb(st, "u", [128, NT, I])
        a = c.sb(st, "a", [128, NT * I // 16, 16])
        q = c.sb(st, "q", [128, NT * I // 16, 16])
        s = c.sb(st, "s", [128, NT * I // 16, 1])
        r = c.sb(st, "r", [128, NT * I // 16, 1])
        xqT = c.sb(st, "xqT", [128, NT, 128])
        hT = c.sb(st, "hT", [128, 3, NT, 128])
        w = c.sb(st, "w", [128, 2, 3, D])
        wd = c.sb(st, "wd", [128, I])
        wl = [(w[0:n, g, k, :], d[name][o:o + n, :]) for g, name in enumerate(("L0_ffn_w_gate", "L0_ffn_w_up"))
              for k, (o, n) in enumerate(IC)]
        load_all(c, wl + [(wd[:], d["L0_ffn_w_down"])])

        def quantize_all(parts):
            order = c.sem("quant_order")
            with nc.Block() as block:
                @block.vector
                def _(dve):
                    link = Link(dve, order)
                    for v in parts:
                        p, n = v.shape[0], v.shape[1]
                        quantize(dve, link, v, a[0:p, 0:n, :], q[0:p, 0:n, :], s[0:p, 0:n, :], r[0:p, 0:n, :])

        quantize_all([c.xn[:].rearrange("p t (n b) -> p (t n) b", b=16), wd[:].rearrange("p (n b) -> p n b", b=16)]
                     + [v.rearrange("p (n b) -> p n b", b=16) for v, _ in wl])
        turn_all(c, [(xqT[:, t, :], c.xn[:, t, :]) for t in range(NT)]
                 + [(wT[:, g, o:o + n], w[0:n, g, k, :]) for g in range(2) for k, (o, n) in enumerate(IC)]
                 + [(wdT[0:n, k, :], wd[:, o:o + n]) for k, (o, n) in enumerate(IC)])
        with ExitStack() as s2:
            pg = c.ps(s2, "pg", [128, 2, 512])
            pu = c.ps(s2, "pu", [128, 2, 512])
            made, silu, used = c.sem("made"), c.sem("silu"), c.sem("used")
            with nc.Block() as block:
                @block.tensor
                def _(pe):
                    for t in range(NT):
                        if t >= 2:
                            pe.wait_ge(used, t - 1 + ONE)
                        pe.matmul(pg[:, t % 2, 0:I], xqT[:, t, :], wT[:, 0, :], start=True, stop=True)
                        pe.matmul(pu[:, t % 2, 0:I], xqT[:, t, :], wT[:, 1, :], start=True, stop=True
                                  ).then_inc(made, 1)

                @block.scalar
                def _(act):
                    for t in range(NT):
                        act.wait_ge(made, t + 1 + ONE)
                        act.activation(u[:, t, :], pg[:, t % 2, 0:I], ACT.Silu).then_inc(silu, 1)

                @block.vector
                def _(dve):
                    for t in range(NT):
                        dve.wait_ge(silu, t + 1 + ONE)
                        dve.tensor_tensor(h[:, t, :], u[:, t, :], pu[:, t % 2, 0:I], ALU.mult).then_inc(used, 1)
                    dve.wait_ge(used, NT + ONE)
        quantize_all([h[:].rearrange("p t (n b) -> p (t n) b", b=16)])
        turn_all(c, [(hT[0:n, k, t, :], h[:, t, o:o + n]) for k, (o, n) in enumerate(IC) for t in range(NT)])
        py = c.ps(st, "py", [128, NT, D])
        summed, added = c.sem("summed"), c.sem("added")
        with nc.Block() as block:
            @block.tensor
            def _(pe):
                for t in range(NT):
                    for k, (o, n) in enumerate(IC):
                        last = pe.matmul(py[:, t, :], hT[0:n, k, t, :], wdT[0:n, k, :], start=(k == 0), stop=(k == 2))
                last.then_inc(summed, 1)

            @block.vector
            def _(dve):
                dve.wait_ge(summed, 1 + ONE)
                dve.tensor_tensor(c.x[:], c.x[:], py[:], ALU.add).then_inc(added, 1)
                dve.wait_ge(added, 1 + ONE)


BIG = 1.0e30


def stage_l0_xattn(c):
    nc = c.nc
    layernorm(c)
    dist = nc.dram_tensor("dist_scratch", [NT, 128, K], F32, kind="Internal").ap()
    cost = nc.dram_tensor("cost_scratch", [B, S + 1, K], F32, kind="Internal").ap()
    step = nc.dram_tensor("step_scratch", [B, S, K], F32, kind="Internal").ap()
    hi_dram = nc.dram_tensor("hi_scratch", [B * S], F32, kind="Internal").ap()
    lo_dram = nc.dram_tensor("lo_scratch", [B * S], F32, kind="Internal").ap()
    distances(c, dist)
    accumulate_costs(c, dist.rearrange("t (b s) k -> (t b) s k", b=2), cost)
    with ExitStack() as st:
        iota1 = c.sb(st, "iota1", [128, K])
        lows = c.sb(st, "lows", [128, NT, K])
        choose_steps(c, cost, step, iota1, lows)
        trace_back(c, step, iota1, hi_dram)
        look_up_lows(c, iota1, lows, hi_dram, lo_dram)
    add_aligned(c, hi_dram, lo_dram)


def distances(c, dist):
    nc = c.nc
    with ExitStack() as st:
        ctxT = c.sb(st, "ctxT", [128, 2, K])
        ctxsq = c.sb(st, "ctxsq", [128, 2, K])
        xm2 = c.sb(st, "xm2", [128, 128])
        dd = c.sb(st, "dd", [128, 2, K])
        sq = c.sb(st, "sq", [128, NT, D])
        bb = c.sb(st, "bb", [128, NT])
        bcur = c.sb(st, "bcur", [128, 1])
        psD = c.ps(st, "psD", [128, 2048])
        loaded = [c.sem("loaded0"), c.sem("loaded1")]
        order, xm2_ready, sq_ready, made, clamped = (c.sem(n) for n in ("order", "xm2", "sq", "made", "clamped"))
        rooted, stored = c.sem("rooted"), c.sem("stored")
        with nc.Block() as block:
            @block.sync
            def _(sp):
                for j in range(2):
                    sp.dma_start(ctxT[:, j, :], c.ctxT[j]).then_inc(loaded[j], 16)
                with sp.Fori(0, NT - 1) as i:
                    sp.wait_ge(made, i + 1 + ONE)
                    settle(sp)
                    for j in range(2):
                        sp.dma_start(ctxT[:, j, :], c.ctxT[ds(i * 2 + (2 + j), 1)].rearrange("b p k -> p (b k)")
                                     ).then_inc(loaded[j], 16)

            @block.tensor
            def _(pe):
                with pe.Fori(0, NT) as i:
                    pe.wait_ge(xm2_ready, i + 1 + ONE)
                    pe.wait_ge(sq_ready, i * 2 + 2 + ONE)
                    for j in range(2):
                        pe.wait_ge(loaded[j], i * 16 + 16 + ONE)
                    for j in range(2):
                        r = slice(j * S, j * S + S)
                        for o, w in KB:
                            pe.matmul(psD[r, o:o + w], xm2[:, r], ctxT[:, j, o:o + w], start=True, stop=False)
                            last = pe.matmul(psD[r, o:o + w], c.ones[:, 0:S], ctxsq[:, j, o:o + w],
                                             start=False, stop=True)
                    last.then_inc(made, 1)

            @block.vector
            def _(dve):
                link = Link(dve, order)
                link(dve.tensor_tensor(sq[:], c.xn[:], c.xn[:], ALU.mult))
                link(dve.reduce_sum(bb[:], sq[:], axis=X))
                with dve.Fori(0, NT) as i:
                    link = Link(dve, order, i + 2)
                    dve.tensor_scalar(xm2[:], c.xnT[:, ds(i * 128, 128)], -2.0, None, ALU.mult).then_inc(xm2_ready, 1)
                    link(dve.tensor_copy(bcur[:], bb[:, ds(i, 1)]))
                    dve.wait_ge(rooted, i + ONE)
                    dve.wait_ge(made, i + 1 + ONE)
                    dve.tensor_scalar(dd[:, 0, :], psD[:, 0:K], bcur[:], 0.0, ALU.add, ALU.max).then_inc(clamped, 1)
                    dve.wait_ge(clamped, i + 1 + ONE)
                    settle(dve)

            @block.scalar
            def _(act):
                with act.Fori(0, NT) as i:
                    act.wait_ge(made, i + ONE)
                    for j in range(2):
                        act.wait_ge(loaded[j], i * 16 + 16 + ONE)
                        act.activation(ctxsq[:, j, :], ctxT[:, j, :], ACT.Square).then_inc(sq_ready, 1)
                    act.wait_ge(clamped, i + 1 + ONE)
                    act.wait_ge(stored, i * 16 + ONE)
                    act.activation(dd[:, 1, :], dd[:, 0, :], ACT.Sqrt).then_inc(rooted, 1)
                    act.wait_ge(rooted, i + 1 + ONE)
                    act.dma_start(dist[ds(i, 1)].rearrange("t p k -> p (t k)"), dd[:, 1, :]).then_inc(stored, 16)
                act.wait_ge(stored, 16 * NT + ONE)


def accumulate_costs(c, dist, cost):
    nc = c.nc
    G = 4
    with ExitStack() as st:
        dcol = c.sb(st, "dcol", [B, 2, G, K])
        rcol = c.sb(st, "rcol", [B, 2, G, K + 1])
        m = c.sb(st, "m", [B, K])
        loaded = [c.sem("loaded0"), c.sem("loaded1")]
        stored = [c.sem("stored0"), c.sem("stored1")]
        order, filled, edge = c.sem("order"), c.sem("filled"), c.sem("edge_stored")
        scanned = c.sem("scanned")
        with nc.Block() as block:
            def load(sp, g, j):
                sp.dma_start(dcol[:, j], dist[:, ds(g * G, G), :]).then_inc(loaded[j], 16)

            @block.sync
            def _(sp):
                load(sp, 0, 0)
                load(sp, 1, 1)
                with sp.Fori(0, S // G // 2 - 1) as i:
                    for j in range(2):
                        sp.wait_ge(scanned, (i * 2 + (j + 1)) * G + ONE)
                        settle(sp)
                        load(sp, i * 2 + (2 + j), j)

            @block.vector
            def _(dve):
                dve.memset(rcol[:], BIG).then_inc(filled, 1)
                dve.wait_ge(filled, 1 + ONE)
                dve.memset(rcol[:, 1, G - 1, 0:1], 0.0).then_inc(filled, 1)
                dve.wait_ge(filled, 2 + ONE)
                dve.wait_ge(edge, 16 + ONE)
                with dve.Fori(0, S // G // 2) as i:
                    link = Link(dve, order, i * (2 * G + 1))
                    for j in range(2):
                        dve.wait_ge(loaded[j], i * 16 + 16 + ONE)
                        dve.wait_ge(stored[j], i * 16 + ONE)
                        for k in range(G):
                            before = rcol[:, j, k - 1] if k else rcol[:, 1 - j, G - 1]
                            link(dve.tensor_tensor(m[:], before[:, 0:K], before[:, 1:K + 1], ALU.min))
                            if j == 0 and k == 0:
                                link(dve.memset(rcol[:, 1, G - 1, 0:1], BIG))
                            dve.tensor_tensor_scan(rcol[:, j, k, 1:K + 1], m[:], dcol[:, j, k, :], BIG,
                                                   ALU.min, ALU.add).then_inc(scanned, 1)
                            dve.wait_ge(scanned, (i * 2 + j) * G + (k + 1) + ONE)
                            settle(dve)

            @block.scalar
            def _(act):
                act.wait_ge(filled, 2 + ONE)
                act.dma_start(cost[:, 0, :], rcol[:, 0, 0, 1:K + 1]).then_inc(edge, 16)
                act.wait_ge(edge, 16 + ONE)
                with act.Fori(0, S // G // 2) as i:
                    for j in range(2):
                        act.wait_ge(scanned, (i * 2 + (j + 1)) * G + ONE)
                        settle(act)
                        act.dma_start(cost[:, ds((i * 2 + j) * G + 1, G), :], rcol[:, j, :, 1:K + 1]
                                      ).then_inc(stored[j], 16)
                for j in range(2):
                    act.wait_ge(stored[j], 16 * (S // G // 2) + ONE)


def choose_steps(c, cost, step, iota1, lows):
    nc = c.nc
    with ExitStack() as st:
        cur = c.sb(st, "cur", [128, K + 1])
        left = c.sb(st, "left", [128, K + 1])
        a = c.sb(st, "a", [128, K])
        leave = c.sb(st, "leave", [128, K])
        diag = c.sb(st, "diag", [128, K])
        lcur = c.sb(st, "lcur", [128, K])
        nxt = c.sb(st, "nxt", [128, 2, K])
        zero = c.sb(st, "zero", [128, K])
        loaded, order, used, ready, stored = (c.sem(n) for n in ("loaded", "order", "used", "ready", "stored"))
        made, filled = c.sem("iota_made"), c.sem("filled")
        LINKS = 9
        with nc.Block() as block:
            def load(sp, t):
                for b in range(2):
                    r = slice(b * S, b * S + S)
                    sp.dma_start(cur[r, 1:K + 1], cost[ds(t * 2 + b, 1), 1:S + 1, :].rearrange("b s k -> (b s) k")
                                 ).then_inc(loaded, 16)
                    sp.dma_start(left[r, 1:K + 1], cost[ds(t * 2 + b, 1), 0:S, :].rearrange("b s k -> (b s) k")
                                 ).then_inc(loaded, 16)

            @block.sync
            def _(sp):
                load(sp, 0)
                with sp.Fori(0, NT - 1) as i:
                    sp.wait_ge(used, i + 1 + ONE)
                    settle(sp)
                    load(sp, i + 1)

            @block.gpsimd
            def _(pool):
                pool.iota(iota1[:], pattern=[[1, K]], base=1, channel_multiplier=0,
                          allow_small_or_imprecise_dtypes=True).then_inc(made, 1)

            @block.vector
            def _(dve):
                dve.memset(cur[:, 0:1], BIG).then_inc(filled, 1)
                dve.memset(left[:, 0:1], BIG).then_inc(filled, 1)
                dve.memset(zero[:], 0.0).then_inc(filled, 1)
                dve.wait_ge(filled, 3 + ONE)
                dve.wait_ge(made, 1 + ONE)
                with dve.Fori(0, NT) as t:
                    link = Link(dve, order, t * LINKS)
                    dve.wait_ge(loaded, t * 64 + 64 + ONE)
                    dve.wait_ge(ready, t + ONE)
                    cu, cl, cd = cur[:, 0:K], left[:, 1:K + 1], left[:, 0:K]
                    link(dve.tensor_tensor(a[:], cu, cl, ALU.min))
                    link(dve.tensor_tensor(diag[:], cd, a[:], ALU.is_le))
                    link(dve.tensor_tensor(a[:], cu, cl, ALU.is_gt))
                    link(dve.tensor_tensor(leave[:], cu, cd, ALU.is_ge))
                    dve.tensor_tensor(leave[:], leave[:], a[:], ALU.max).then_inc(used, 1)
                    dve.wait_ge(used, t + 1 + ONE)
                    settle(dve)
                    link(dve.tensor_tensor(a[:], iota1[:], leave[:], ALU.mult))
                    link(dve.tensor_tensor_scan(lcur[:], a[:], zero[:], 0.0, ALU.max, ALU.add))
                    link(dve.tensor_copy(lows[:, ds(t, 1), :].rearrange("p a k -> p (a k)"), lcur[:]))
                    link(dve.tensor_tensor(a[:], a[:], diag[:], ALU.subtract))
                    link(dve.tensor_tensor(a[:], a[:], leave[:], ALU.mult))
                    dve.wait_ge(stored, t * 16 + ONE)
                    settle(dve)
                    dve.tensor_tensor_scan(nxt[:, 0, :], a[:], zero[:], 0.0, ALU.max, ALU.add).then_inc(ready, 1)
                    assert link.n == LINKS, link.n

            @block.scalar
            def _(act):
                with act.Fori(0, NT) as t:
                    act.wait_ge(ready, t + 1 + ONE)
                    settle(act)
                    act.dma_start(step.rearrange("(t b) s k -> t (b s) k", b=2)[ds(t, 1)].rearrange(
                        "t p k -> p (t k)"), nxt[:, 0, :]).then_inc(stored, 16)
                act.wait_ge(stored, 16 * NT + ONE)


def trace_back(c, step, iota1, hi_dram):
    nc = c.nc
    G = 4
    with ExitStack() as st:
        col = c.sb(st, "col", [B, 2, G, K])
        junk = c.sb(st, "junk", [B, K])
        hi = c.sb(st, "hi", [B, S + 1])
        loaded = [c.sem("loaded0"), c.sem("loaded1")]
        found, stored, filled = c.sem("found"), c.sem("hi_stored"), c.sem("filled")
        with nc.Block() as block:
            def load(sp, g, j):
                sp.dma_start(col[:, j], step[:, ds(g * (-G) + (S - G), G), :]).then_inc(loaded[j], 16)

            @block.sync
            def _(sp):
                load(sp, 0, 0)
                load(sp, 1, 1)
                with sp.Fori(0, S // G // 2 - 1) as i:
                    for j in range(2):
                        sp.wait_ge(found, (i * 2 + (j + 1)) * G + ONE)
                        settle(sp)
                        load(sp, i * 2 + (2 + j), j)
                sp.wait_ge(found, S + ONE)
                sp.dma_start(hi_dram.rearrange("(b s) -> b s", b=B), hi[:, 1:S + 1]).then_inc(stored, 16)
                sp.wait_ge(stored, 16 + ONE)

            @block.vector
            def _(dve):
                dve.memset(hi[:, S:S + 1], float(K)).then_inc(filled, 1)
                dve.wait_ge(filled, 1 + ONE)
                with dve.Fori(0, S // G // 2) as i:
                    for j in range(2):
                        dve.wait_ge(loaded[j], i * 16 + 16 + ONE)
                        for k in range(G):
                            n = i * (-2 * G) + (S - j * G - k)
                            dve.scalar_tensor_tensor(out=junk[:], in0=iota1[0:B, :], scalar=hi[:, ds(n, 1)],
                                                     in1=col[:, j, G - 1 - k, :], op0=ALU.is_equal, op1=ALU.mult,
                                                     accum_out=hi[:, ds(n - 1, 1)]).then_inc(found, 1)
                            dve.wait_ge(found, (i * 2 + j) * G + (k + 1) + ONE)
                            settle(dve)


def look_up_lows(c, iota1, lows, hi_dram, lo_dram):
    nc = c.nc
    with ExitStack() as st:
        hi = c.sb(st, "hi", [128, NT])
        lo = c.sb(st, "lo", [128, NT])
        junk = c.sb(st, "junk", [128, K])
        loaded, order, stored = c.sem("loaded"), c.sem("order"), c.sem("stored")
        with nc.Block() as block:
            @block.sync
            def _(sp):
                with nc.allow_non_contiguous_dma(reason="1024 single numbers"):
                    sp.dma_start(hi[:], hi_dram.rearrange("(t p) -> p t", p=128)).then_inc(loaded, 16)
                    sp.wait_ge(order, NT + ONE)
                    sp.dma_start(lo_dram.rearrange("(t p) -> p t", p=128), lo[:]).then_inc(stored, 16)
                    sp.wait_ge(stored, 16 + ONE)

            @block.vector
            def _(dve):
                link = Link(dve, order)
                dve.wait_ge(loaded, 16 + ONE)
                for t in range(NT):
                    link(dve.scalar_tensor_tensor(out=junk[:], in0=iota1[:], scalar=hi[:, t:t + 1],
                                                  in1=lows[:, t, :], op0=ALU.is_equal, op1=ALU.mult,
                                                  accum_out=lo[:, t:t + 1]))


def add_aligned(c, hi_dram, lo_dram):
    nc = c.nc
    with ExitStack() as st:
        hi = c.sb(st, "hi", [128, B * S])
        lo = c.sb(st, "lo", [128, B * S])
        tmp = c.sb(st, "tmp", [128, B * S])
        row1 = c.sb(st, "row1", [128, len(KC)])
        inside = c.sb(st, "inside", [128, len(KC), B * S])
        ctxN = c.sb(st, "ctxN", [128, 2, len(KC), D])
        sumT = c.sb(st, "sumT", [128, B * S])
        psA = c.ps(st, "psA", [128, 2, 512])
        psX = c.ps(st, "psX", [128, NT, 128])
        ends, made, order = c.sem("ends"), c.sem("made"), c.sem("order")
        loaded = [c.sem("loaded0"), c.sem("loaded1")]
        summed, copied, turned, done = (c.sem(n) for n in ("summed", "copied", "turned", "done"))
        with nc.Block() as block:
            def load(sp, b, j):
                n = K // 128
                sp.dma_start(ctxN[:, j, 0:n, :], c.dram["ctx_1024"][ds(b, 1), 0:n * 128, :].rearrange(
                    "b (c p) d -> p (b c) d", p=128)).then_inc(loaded[j], 16)
                sp.dma_start(ctxN[0:K - n * 128, j, n, :], c.dram["ctx_1024"][ds(b, 1), n * 128:K, :].rearrange(
                    "b p d -> p (b d)")).then_inc(loaded[j], 16)

            @block.sync
            def _(sp):
                sp.dma_start(hi[:], row_bcast(hi_dram)).then_inc(ends, 16)
                sp.dma_start(lo[:], row_bcast(lo_dram)).then_inc(ends, 16)
                load(sp, 0, 0)
                load(sp, 1, 1)
                with sp.Fori(0, NT - 1) as i:
                    for j in range(2):
                        sp.wait_ge(summed, i * 2 + (j + 1) + ONE)
                        settle(sp)
                        load(sp, i * 2 + (2 + j), j)

            @block.gpsimd
            def _(pool):
                pool.iota(row1[:], pattern=[[128, len(KC)]], base=1, channel_multiplier=1,
                          allow_small_or_imprecise_dtypes=True).then_inc(made, 1)

            @block.vector
            def _(dve):
                link = Link(dve, order)
                dve.wait_ge(made, 1 + ONE)
                dve.wait_ge(ends, 32 + ONE)
                for k in range(len(KC)):
                    link(dve.tensor_scalar(tmp[:], lo[:], row1[:, k:k + 1], None, ALU.is_le))
                    link(dve.scalar_tensor_tensor(out=inside[:, k, :], in0=hi[:], scalar=row1[:, k:k + 1],
                                                  in1=tmp[:], op0=ALU.is_ge, op1=ALU.mult))
                with dve.Fori(0, NT) as i:
                    for j in range(2):
                        dve.wait_ge(summed, i * 2 + (j + 1) + ONE)
                        dve.tensor_copy(sumT[:, ds(i * 128 + j * S, S)], psA[:, j, 0:S]).then_inc(copied, 1)
                dve.wait_ge(turned, 1 + ONE)
                dve.tensor_tensor(c.x[:], c.x[:], psX[:], ALU.add).then_inc(done, 1)
                dve.wait_ge(done, 1 + ONE)

            @block.tensor
            def _(pe):
                pe.wait_ge(order, 2 * len(KC) + ONE)
                with pe.Fori(0, NT) as i:
                    for j in range(2):
                        pe.wait_ge(loaded[j], i * 32 + 32 + ONE)
                        pe.wait_ge(copied, i * 2 + ONE)
                        for k, (o, w) in enumerate(KC):
                            last = pe.matmul(psA[:, j, 0:S], ctxN[0:w, j, k, :],
                                             inside[0:w, k, ds(i * 128 + j * S, S)],
                                             start=(k == 0), stop=(k == len(KC) - 1))
                        last.then_inc(summed, 1)
                pe.wait_ge(copied, 2 * NT + ONE)
                for t in range(NT):
                    last = pe.transpose(psX[:, t, :], sumT[:, t * 128:t * 128 + 128], c.ident[:])
                last.then_inc(turned, 1)


STAGES = [stage_l0_xattn, stage_l0_attn, stage_l0_ffn, stage_l1_xattn, stage_l1_attn, stage_l1_ffn, stage_l2_xattn,
          stage_l2_attn, stage_l2_ffn, stage_l3_xattn, stage_l3_attn, stage_l3_ffn]


def perceiver(nc, dram, out):
    with ExitStack() as ctx:
        c = Core(nc, ctx, dram)
        c.ctxT = nc.dram_tensor("ctxT_scratch", [B, 128, K], F32, kind="Internal").ap()
        constants(c)
        if FIRST_STAGE in (0, 3, 6, 9) or LAST_STAGE > FIRST_STAGE:
            transpose_context(c)
        for stage in STAGES[FIRST_STAGE:LAST_STAGE + 1]:
            stage(c)
            c.end_stage()
        stored = c.sem("out_stored")
        with nc.Block() as block:
            @block.sync
            def _(sp):
                sp.dma_start(out.rearrange("(t b) s d -> (b s) t d", b=2), c.x[:]).then_inc(stored, 16)
                sp.wait_ge(stored, 16 + ONE)


def kernel(**inputs):
    import numpy as np
    import concourse.bacc as bacc
    from concourse.bass_utils import run_bass_kernel_spmd

    nc = bacc.Bacc("TRN2", target_bir_lowering=False, num_devices=1)
    arrays, dram = {}, {}
    for name, value in inputs.items():
        a = np.ascontiguousarray(value)
        if a.dtype == np.bool_:
            a = a.view(np.uint8)
        arrays[f"in_{name}"] = a
        dram[name] = nc.dram_tensor(f"in_{name}", a.shape, mybir.dt.from_np(a.dtype), kind="ExternalInput").ap()
    out = nc.dram_tensor("out", [B, S, D], F32, kind="ExternalOutput").ap()
    perceiver(nc, dram, out)
    result = run_bass_kernel_spmd(nc, [arrays], core_ids=[0])
    return result.results[0]["out"]
```

```python
from contextlib import ExitStack

import concourse.bass as bass
from concourse import mybir

ALU = mybir.AluOpType
ACT = mybir.ActivationFunctionType
F32 = mybir.dt.float32
F32R = mybir.dt.float32r
I32 = mybir.dt.int32
U8 = mybir.dt.uint8
X = mybir.AxisListType.X
ds = bass.ds

B, S, D = 16, 64, 128
NT = B * S // 128
K = 1601
KC = [(c * 128, min(128, K - c * 128)) for c in range((K + 127) // 128)]
KB = [(c * 512, min(512, K - c * 512)) for c in range((K + 511) // 512)]
H = 16
E = 8
NEG = -1.0e30
LN_EPS = 1e-5
HIGH = -4096
ONE = 1
SEMS = 100


def settle(eng):
    eng.nop(nofuse=True)


class Link:

    def __init__(self, eng, sem, base=0):
        self.eng, self.sem, self.base, self.n = eng, sem, base, 0

    def __call__(self, ins):
        self.n += 1
        ins.then_inc(self.sem, 1)
        self.eng.wait_ge(self.sem, self.base + self.n + ONE)
        if not isinstance(self.base, int):
            settle(self.eng)
        return ins


class Core:

    def __init__(self, nc, ctx, dram):
        self.nc, self.ctx, self.dram, self.n = nc, ctx, dram, 0
        self.pool = [nc.alloc_semaphore(f"stage_sem_{n}") for n in range(SEMS)]
        self.used = 0
        self.credit(self.pool)
        self.x = self.keep("x", [128, NT, D])
        self.xn = self.keep("xn", [128, NT, D])
        self.xnT = self.keep("xnT", [128, NT * 128])
        self.ident = self.keep("ident", [128, 128])
        self.ones = self.keep("ones", [128, 128])
        self.headmask = self.keep("headmask", [128, H])
        self.bias_row = self.keep("bias_row", [128, D])

    def keep(self, name, shape, dt=F32):
        return self.ctx.enter_context(self.nc.sbuf_tensor(name, shape, dt))

    def sem(self, name):
        self.used += 1
        return self.pool[self.used - 1]

    def credit(self, sems):
        for sem in sems:
            self.nc.gpsimd.sem_inc(sem, ONE)
        self.nc.all_engine_barrier()

    def end_stage(self):
        used = self.pool[:self.used]
        for sem in used:
            self.nc.gpsimd.sem_clear(sem)
        self.credit(used)
        self.used = 0

    def sb(self, st, name, shape, dt=F32):
        self.n += 1
        return st.enter_context(self.nc.sbuf_tensor(f"{name}_{self.n}", shape, dt))

    def ps(self, st, name, shape, dt=F32):
        self.n += 1
        return st.enter_context(self.nc.psum_tensor(f"{name}_{self.n}", shape, dt))


def row_bcast(vec, n=128):
    return vec.rearrange("(a d) -> a d", a=1).to_broadcast([n, vec.shape[0]])


def bc(ap, shape):
    return ap.to_broadcast(shape)


def constants(c):
    nc = c.nc
    loaded, made, filled = c.sem("x_loaded"), c.sem("const_made"), c.sem("const_filled")
    with nc.Block() as block:
        @block.sync
        def _(sp):
            sp.dma_start(c.x[:], c.dram["x"].rearrange("(t b) s d -> (b s) t d", b=2)).then_inc(loaded, 16)
            sp.wait_ge(loaded, 16 + ONE)

        @block.gpsimd
        def _(pool):
            pool.memset(c.ident[:], 0.0).then_inc(filled, 1)
            pool.memset(c.ones[:], 1.0).then_inc(filled, 1)
            pool.memset(c.headmask[:], 1.0).then_inc(filled, 1)
            pool.wait_ge(filled, 3 + ONE)
            pool.affine_select(out=c.ident[:], in_=c.ident[:], compare_op=ALU.not_equal, fill=1.0, base=0,
                               pattern=[[-1, 128]], channel_multiplier=1).then_inc(made, 1)
            pool.affine_select(out=c.headmask[:], in_=c.headmask[:], compare_op=ALU.is_ge, fill=0.0, base=0,
                               pattern=[[-8, H]], channel_multiplier=1).then_inc(made, 1)
            pool.wait_ge(made, 2 + ONE)
            pool.affine_select(out=c.headmask[:], in_=c.headmask[:], compare_op=ALU.is_ge, fill=0.0, base=7,
                               pattern=[[8, H]], channel_multiplier=-1).then_inc(made, 1)
            pool.wait_ge(made, 3 + ONE)


def transpose_context(c):
    nc = c.nc
    with ExitStack() as st:
        nat = c.sb(st, "ctx_nat", [128, 2, len(KC), D])
        trn = c.sb(st, "ctx_trn", [128, 2, K])
        pt = [c.ps(st, f"ctx_pt{g}", [128, 512]) for g in range(4)]
        loaded = [c.sem("nat_loaded0"), c.sem("nat_loaded1")]
        turned, copied = c.sem("ctx_turned"), c.sem("ctx_copied")
        stored = [c.sem("trn_stored0"), c.sem("trn_stored1")]
        ctx = c.dram["ctx_1024"]
        with nc.Block() as block:
            def load(sp, b, j):
                n = K // 128
                sp.dma_start(nat[:, j, 0:n, :], ctx[ds(b, 1), 0:n * 128, :].rearrange("b (c p) d -> p (b c) d", p=128)
                             ).then_inc(loaded[j], 16)
                sp.dma_start(nat[0:K - n * 128, j, n, :],
                             ctx[ds(b, 1), n * 128:K, :].rearrange("b p d -> p (b d)")).then_inc(loaded[j], 16)

            @block.sync
            def _(sp):
                load(sp, 0, 0)
                load(sp, 1, 1)
                with sp.Fori(0, B // 2 - 1) as i:
                    for j in range(2):
                        sp.wait_ge(turned, (i * 2 + j + 1) * 4 + ONE)
                        settle(sp)
                        load(sp, i * 2 + (2 + j), j)

            @block.tensor
            def _(pe):
                with pe.Fori(0, B // 2) as i:
                    for j in range(2):
                        pe.wait_ge(loaded[j], (i + 1) * 32 + ONE)
                        for g in range(4):
                            pe.wait_ge(copied, (i * 2 + j) * 4 + ONE)
                            for k in range(4 * g, min(4 * g + 4, len(KC))):
                                n = KC[k][1]
                                last = pe.transpose(pt[g][:, (k % 4) * 128:(k % 4) * 128 + n],
                                                    nat[0:n, j, k, :], c.ident[0:n, 0:n])
                            last.then_inc(turned, 1)

            @block.vector
            def _(dve):
                with dve.Fori(0, B // 2) as i:
                    for j in range(2):
                        dve.wait_ge(stored[j], i * 16 + ONE)
                        for g in range(4):
                            o, n = KB[g]
                            dve.wait_ge(turned, (i * 2 + j) * 4 + g + 1 + ONE)
                            dve.tensor_copy(trn[:, j, o:o + n], pt[g][:, 0:n]).then_inc(copied, 1)

            @block.scalar
            def _(act):
                with act.Fori(0, B // 2) as i:
                    for j in range(2):
                        act.wait_ge(copied, (i * 2 + j + 1) * 4 + ONE)
                        act.dma_start(c.ctxT[ds(i * 2 + j, 1)].rearrange("b p k -> p (b k)"),
                                      trn[:, j, :]).then_inc(stored[j], 16)
                for j in range(2):
                    act.wait_ge(stored[j], 16 * (B // 2) + ONE)


def layernorm(c):
    nc = c.nc
    with ExitStack() as st:
        mean = c.sb(st, "ln_mean", [128, NT, 1])
        var = c.sb(st, "ln_var", [128, NT, 1])
        std = c.sb(st, "ln_std", [128, NT, 1])
        inv = c.sb(st, "ln_inv", [128, NT, 1])
        sq = c.sb(st, "ln_sq", [128, NT, D])
        pt = c.ps(st, "ln_pt", [128, NT * 128])
        order, var_ready, std_ready = c.sem("ln_order"), c.sem("ln_var_ready"), c.sem("ln_std_ready")
        xn_ready, turned, done = c.sem("xn_ready"), c.sem("xn_turned"), c.sem("xnT_done")
        with nc.Block() as block:
            @block.vector
            def _(dve):
                link = Link(dve, order)
                link(dve.reduce_sum(mean[:, :, 0], c.x[:], axis=X))
                link(dve.tensor_scalar(mean[:, :, 0], mean[:, :, 0], 1.0 / D, None, ALU.mult))
                link(dve.tensor_tensor(c.xn[:], c.x[:], bc(mean[:], [128, NT, D]), ALU.subtract))
                link(dve.tensor_tensor(sq[:], c.xn[:], c.xn[:], ALU.mult))
                link(dve.reduce_sum(var[:, :, 0], sq[:], axis=X))
                dve.tensor_scalar(var[:, :, 0], var[:, :, 0], 1.0 / D, LN_EPS, ALU.mult, ALU.add
                                  ).then_inc(var_ready, 1)
                dve.wait_ge(std_ready, 1 + ONE)
                link(dve.reciprocal(inv[:, :, 0], std[:, :, 0]))
                dve.tensor_tensor(c.xn[:], c.xn[:], bc(inv[:], [128, NT, D]), ALU.mult).then_inc(xn_ready, 1)
                for h in range(2):
                    dve.wait_ge(turned, h + 1 + ONE)
                    dve.tensor_copy(c.xnT[:, h * 512:h * 512 + 512], pt[:, h * 512:h * 512 + 512]
                                    ).then_inc(done, 1)
                dve.wait_ge(done, 2 + ONE)

            @block.scalar
            def _(act):
                act.wait_ge(var_ready, 1 + ONE)
                act.activation(std[:, :, 0], var[:, :, 0], ACT.Sqrt).then_inc(std_ready, 1)

            @block.tensor
            def _(pe):
                pe.wait_ge(xn_ready, 1 + ONE)
                for t in range(NT):
                    last = pe.transpose(pt[:, t * 128:t * 128 + 128], c.xn[:, t, :], c.ident[:])
                    if t % 4 == 3:
                        last.then_inc(turned, 1)


def load_all(c, pairs):
    nc = c.nc
    loaded = c.sem("loaded")
    with nc.Block() as block:
        @block.sync
        def _(sp):
            for out, src in pairs:
                sp.dma_start(out, src).then_inc(loaded, 16)
            sp.wait_ge(loaded, 16 * len(pairs) + ONE)


def turn_all(c, jobs):
    nc = c.nc
    with ExitStack() as st:
        pt = [c.ps(st, f"turn{j}", [128, 512]) for j in range(2)]
        turned, copied = c.sem("turned"), c.sem("turn_copied")
        with nc.Block() as block:
            @block.tensor
            def _(pe):
                for n, (out, src) in enumerate(jobs):
                    if n >= 2:
                        pe.wait_ge(copied, n - 1 + ONE)
                    p, f = src.shape
                    pe.transpose(pt[n % 2][0:f, 0:p], src, c.ident[0:p, 0:p]).then_inc(turned, 1)

            @block.vector
            def _(dve):
                for n, (out, src) in enumerate(jobs):
                    p, f = src.shape
                    dve.wait_ge(turned, n + 1 + ONE)
                    dve.tensor_copy(out, pt[n % 2][0:f, 0:p]).then_inc(copied, 1)
                dve.wait_ge(copied, len(jobs) + ONE)


def multiply_all(c, jobs):
    nc = c.nc
    with ExitStack() as st:
        pm = [c.ps(st, f"mul{j}", [128, 512]) for j in range(2)]
        summed, copied = c.sem("summed"), c.sem("sum_copied")
        with nc.Block() as block:
            @block.tensor
            def _(pe):
                for n, (out, terms) in enumerate(jobs):
                    if n >= 2:
                        pe.wait_ge(copied, n - 1 + ONE)
                    p, f = out.shape
                    for k, (lhsT, rhs) in enumerate(terms):
                        last = pe.matmul(pm[n % 2][0:p, 0:f], lhsT, rhs, start=(k == 0),
                                         stop=(k == len(terms) - 1))
                    last.then_inc(summed, 1)

            @block.vector
            def _(dve):
                for n, (out, terms) in enumerate(jobs):
                    p, f = out.shape
                    dve.wait_ge(summed, n + 1 + ONE)
                    dve.tensor_copy(out, pm[n % 2][0:p, 0:f]).then_inc(copied, 1)
                dve.wait_ge(copied, len(jobs) + ONE)


def head_blocks(c, st, lhsT, rhs, out):
    nc = c.nc
    spread = c.sb(st, "spread", [128, H, D])
    spread_done = c.sem("spread_done")
    with nc.Block() as block:
        @block.vector
        def _(dve):
            for h in range(H):
                dve.tensor_scalar(spread[:, h, :], rhs, c.headmask[:, h:h + 1], None, ALU.mult
                                  ).then_inc(spread_done, 1)
            dve.wait_ge(spread_done, H + ONE)
    flat_in = spread[:].rearrange("p h d -> p (h d)")
    flat_out = out.rearrange("p h d -> p (h d)")
    multiply_all(c, [(flat_out[:, n:n + 512], [(lhsT, flat_in[:, n:n + 512])]) for n in range(0, H * D, 512)])


def cross_attention(c, M, N, scale, masked=False, topk=None):
    nc = c.nc
    TB = H // 2
    T = 2 * TB
    AHEAD = 2 if topk else 1
    NI = B // 2
    VW = D + 1 if topk else D
    with ExitStack() as st:
        ctxT = c.sb(st, "ctxT", [128, 2, K])
        ctxN = c.sb(st, "ctxN", [128, 2, len(KC), D + 4])
        stat = c.sb(st, "stat", [128, 2, H, S])
        P = c.sb(st, "P", [128, 2, K])
        PT = c.sb(st, "PT", [128, 2, len(KC), 128])
        UT = c.sb(st, "UT", [128, 2, TB, 128])
        U = c.sb(st, "U", [128, 2, 128])
        mx = c.sb(st, "mx", [128, 2])
        pmx = c.sb(st, "pmx", [128, 2, 2])
        ls = c.sb(st, "ls", [128, 2])
        li = c.sb(st, "li", [128, 2])
        if masked or topk:
            SS = c.sb(st, "SS", [128, 2, K])
        if not topk:
            ctxH, ctxL = c.sb(st, "ctxH", [128, 2, K + K % 2], F32R), c.sb(st, "ctxL", [128, 2, K + K % 2], F32R)
            ctxM, statM = c.sb(st, "ctxM", [128, K]), c.sb(st, "statM", [128, H * S])
            statH, statL = c.sb(st, "statH", [128, 2, H, S], F32R), c.sb(st, "statL", [128, 2, H, S], F32R)
        if masked:
            mask8 = c.sb(st, "mask8", [128, 2, K], U8)
            maskf = c.sb(st, "maskf", [128, 2, K])
        if topk:
            KT = c.sb(st, "KT", [128, 2, K])
            top = c.sb(st, "top", [128, 4, 8])
            rest = c.sb(st, "rest", [128, 2, K])
            EX = c.sb(st, "EX", [128, K])
            ER = c.sb(st, "ER", [128, K])
        psS = c.ps(st, "psS", [128, 2048])
        psT = c.ps(st, "psT", [128, 2, 512])
        psU = c.ps(st, "psU", [128, 512])
        psZ = c.ps(st, "psZ", [128, 512])

        loaded = [c.sem("ctx_loaded0"), c.sem("ctx_loaded1")]
        mask_ready, ones_ready = c.sem("mask_ready"), c.sem("ones_ready")
        qp_ready, stat_ready, kt_ready = c.sem("qp_ready"), c.sem("stat_ready"), c.sem("kt_ready")
        scores_ready, max_ready, exp_done = c.sem("scores_ready"), c.sem("max_ready"), c.sem("exp_done")
        copied, rest_ready, rest_exp = c.sem("copied"), c.sem("rest_ready"), c.sem("rest_exp")
        p_ready = c.sem("p_ready") if topk else exp_done
        score_free = copied if topk else max_ready if masked else exp_done
        turned, pt_front, pt_back = c.sem("turned"), c.sem("pt_front"), c.sem("pt_back")
        u_ready, li_ready, us_ready = c.sem("u_ready"), c.sem("li_ready"), c.sem("us_ready")
        ut_turned, ut_ready = c.sem("ut_turned"), c.sem("ut_ready")
        y_ready, x_done, order = c.sem("y_ready"), c.sem("x_done"), c.sem("order")
        ctx_high, ctx_cut = c.sem("ctx_high"), c.sem("ctx_cut")
        stat_high, stat_cut = c.sem("stat_high"), c.sem("stat_cut")
        front_ready, part_max = c.sem("front_ready"), c.sem("part_max")
        LOADS = 16 * (4 if masked else 3)
        LINKS = 2 + T * (7 if topk else 0)

        if not topk and K % 2:
            with nc.Block() as block:
                @block.vector
                def _(dve):
                    for half in (ctxH, ctxL):
                        dve.memset(half[:, :, K:K + 1].bitcast(F32), 0.0).then_inc(ones_ready, 1)
                    dve.wait_ge(ones_ready, 2 + ONE)
        if topk:
            with nc.Block() as block:
                @block.gpsimd
                def _(pool):
                    for j in range(2):
                        pool.memset(ctxN[:, j, :, D:D + 1], 1.0).then_inc(ones_ready, 1)
                    pool.wait_ge(ones_ready, 2 + ONE)

        def copy_weights(eng, copy, g, n, q):
            w = len(KC) - 12 if q == 3 else 4
            p = KC[-1][1] if q == 3 else 128
            eng.wait_ge(turned, g * 4 + (q + 1) + ONE)
            copy(PT[0:p, n % 2, 4 * q:4 * q + w, :],
                 psT[0:p, q % 2, 0:w * 128].rearrange("p (k t) -> p k t", t=128)
                 ).then_inc(pt_front if q < 2 else pt_back, 1)

        with nc.Block() as block:
            def load(sp, b, j):
                n = K // 128
                sp.dma_start(ctxT[:, j, :], c.ctxT[ds(b, 1)].rearrange("b p k -> p (b k)")).then_inc(loaded[j], 16)
                sp.dma_start(ctxN[:, j, 0:n, 0:D], c.dram["ctx_1024"][ds(b, 1), 0:n * 128, :].rearrange(
                    "b (c p) d -> p (b c) d", p=128)).then_inc(loaded[j], 16)
                sp.dma_start(ctxN[0:K - n * 128, j, n, 0:D], c.dram["ctx_1024"][ds(b, 1), n * 128:K, :].rearrange(
                    "b p d -> p (b d)")).then_inc(loaded[j], 16)
                if masked:
                    sp.dma_start(mask8[:, j, :], c.dram["mask_BxS2_bf1"][ds(b, 1)].to_broadcast([128, K])
                                 ).then_inc(loaded[j], 16)

            @block.sync
            def _(sp):
                load(sp, 0, 0)
                load(sp, 1, 1)
                with sp.Fori(0, NI - 1) as i:
                    for j in range(2):
                        sp.wait_ge(u_ready, i * T + TB * (j + 1) + ONE)
                        settle(sp)
                        if masked:
                            sp.wait_ge(mask_ready, i * 2 + (j + 1) + ONE)
                            settle(sp)
                        load(sp, i * 2 + (2 + j), j)

            @block.tensor
            def _(pe):
                def scores(i, t):
                    j, n = t // TB % 2, t % TB
                    if n == 0:
                        if topk:
                            pe.wait_ge(stat_ready, i * 2 + (t // TB + 1) + ONE)
                        else:
                            pe.wait_ge(stat_cut, i * 4 + 2 * (t // TB + 1) + ONE)
                            pe.wait_ge(ctx_cut, i * 4 + 2 * (t // TB + 1) + ONE)
                    pe.wait_ge(score_free, i * T + t + ONE)
                    if topk:
                        for o, w in KB:
                            last = pe.matmul(psS[:, o:o + w], stat[:, j, 2 * n:2 * n + 2, :], KT[:, j, o:o + w],
                                             start=True, stop=True)
                    else:
                        for banks in (KB[:2], KB[2:]):
                            for u, (q, k) in enumerate(((statH, ctxL), (statH, ctxH), (statL, ctxH))):
                                for o, w in banks:
                                    w += w % 2
                                    last = pe.matmul(psS[:, o:o + w], q[:, j, 2 * n:2 * n + 2, :],
                                                     k[:, j, o:o + w], start=(u == 0), stop=(u == 2))
                            if banks[0] == KB[0]:
                                last.then_inc(front_ready, 1)
                    last.then_inc(scores_ready, 1)

                def project(loads, b, j, g, ahead):
                    pe.wait_ge(loaded[j], loads * LOADS + ONE)
                    if topk:
                        pe.wait_ge(score_free, g + ahead + ONE)
                        for o, w in KB:
                            last = pe.matmul(psS[:, o:o + w], topk[1], ctxT[:, j, o:o + w], start=True, stop=True)
                        last.then_inc(qp_ready, 1)
                        pe.wait_ge(kt_ready, b + 1 + ONE)
                    else:
                        pe.wait_ge(pt_back, g * 2 + ONE)
                        for h in range(H):
                            last = pe.matmul(psT[:, h // 8, (h % 8) * S:(h % 8) * S + S], M[:, h, :],
                                             c.xnT[:, ds(b * S, S)], start=True, stop=True)
                        last.then_inc(qp_ready, 1)

                def turn(g, t, q, first):
                    if q >= 2:
                        pe.wait_ge(pt_front, g * 2 + (q - 1) + ONE)
                    elif not (first and t == 0):
                        pe.wait_ge(pt_back, g * 2 - (1 - q) + ONE)
                    for k in range(4 * q, min(4 * q + 4, len(KC))):
                        o, w = KC[k]
                        last = pe.transpose(psT[0:w, q % 2, (k % 4) * 128:(k % 4) * 128 + 128],
                                            P[:, t % 2, o:o + w], c.ident[:])
                    last.then_inc(turned, 1)

                def values(g, t, q):
                    if q == 0:
                        pe.wait_ge(us_ready, g + ONE)
                    if q < 2:
                        pe.wait_ge(pt_front, g * 2 + (q + 1) + ONE)
                    else:
                        pe.wait_ge(pt_back, g * 2 + (q - 1) + ONE)
                    for k in range(4 * q, min(4 * q + 4, len(KC))):
                        w = KC[k][1]
                        last = pe.matmul(psU[:, 0:VW], PT[0:w, t % 2, k, :], ctxN[0:w, t // TB, k, 0:VW],
                                         start=(k == 0), stop=(k == len(KC) - 1))
                    if q == 3:
                        last.then_inc(u_ready, 1)

                def turn_u(g, t):
                    pe.wait_ge(us_ready, g + 1 + ONE)
                    pe.wait_ge(ut_ready, g + ONE)
                    pe.transpose(psZ[:, 0:128], U[:, t % 2, :], c.ident[:]).then_inc(ut_turned, 1)

                def sums(j, g):
                    pe.wait_ge(ut_ready, g + ONE)
                    for h in range(H):
                        last = pe.matmul(psZ[j * S:j * S + S, 128:256], UT[:, j, h // 2, (h % 2) * S:(h % 2) * S + S],
                                         N[:, h, :], start=(h == 0), stop=(h == H - 1))
                    last.then_inc(y_ready, 1)

                def iteration(i, first, final):
                    g = i * T
                    for t in range(T):
                        if t == 4:
                            project(i + 1, i * 2 + 1, 1, g + t, AHEAD)
                        if t == 12 and not final:
                            project(i + 2, i * 2 + 2, 0, g + t, AHEAD)
                        more = t + AHEAD < T or not final
                        early = topk or t == 4 or (t == 12 and not final)
                        if more and early:
                            scores(i, t + AHEAD)
                            if not topk:
                                pe.wait_ge(stat_ready, i * 2 + (2 if t == 4 else 3) + ONE)
                        pe.wait_ge(p_ready, g + t + 1 + ONE)
                        turn(g + t, t, 0, first)
                        turn(g + t, t, 1, first)
                        if more and not early:
                            scores(i, t + AHEAD)
                        done = t in (1, 9) and not (first and t == 1)
                        if done:
                            sums(int(t == 1), g + (t - 1))
                        turn(g + t, t, 2, first)
                        values(g + t, t, 0)
                        turn(g + t, t, 3, first)
                        for q in range(1, 4):
                            values(g + t, t, q)
                        if done:
                            pe.wait_ge(x_done, i * 2 + int(t == 9) + ONE)
                        if t:
                            turn_u(g + (t - 1), t - 1)
                        elif not first:
                            turn_u(g - 1, T - 1)

                project(1, 0, 0, 0, 0)
                for t in range(AHEAD):
                    scores(0, t)
                iteration(0, True, False)
                with pe.Fori(1, NI - 1) as i:
                    iteration(i, False, False)
                iteration(NI - 1, False, True)
                turn_u(NI * T - 1, T - 1)
                sums(1, NI * T)

            @block.scalar
            def _(act):
                def stationary(b, j):
                    act.wait_ge(qp_ready, b + 1 + ONE)
                    if topk:
                        act.activation(KT[:, j, :], psS[:, 0:K], ACT.Identity, bias=topk[2]).then_inc(kt_ready, 1)
                    else:
                        act.activation(stat[:, j].rearrange("p h s -> p (h s)"),
                                       psT[:].rearrange("p a b -> p (a b)"), ACT.Copy, scale=scale
                                       ).then_inc(stat_ready, 1)

                def exps(g, t, first=False):
                    k = t % 2
                    act.wait_ge(max_ready, g + 1 + ONE)
                    if not first:
                        act.wait_ge(u_ready, g - 1 + ONE)
                    act.activation(P[:, k, :], SS[:, k, :] if masked else psS[:, 0:K], ACT.Exp,
                                   bias=mx[:, k:k + 1], accum_out=ls[:, k:k + 1]).then_inc(exp_done, 1)

                def copy_scores(g, t, first=False):
                    act.wait_ge(scores_ready, g + 1 + ONE)
                    if not first:
                        act.wait_ge(rest_ready, g - 1 + ONE)
                        act.wait_ge(exp_done, g - 1 + ONE)
                    act.activation(SS[:, t % 2, :], psS[:, 0:K], ACT.Copy).then_inc(copied, 1)

                def exps_topk(g, t):
                    k = t % 2
                    act.wait_ge(max_ready, g + 1 + ONE)
                    act.wait_ge(p_ready, g + ONE)
                    act.activation(EX[:], SS[:, k, :], ACT.Exp, bias=mx[:, k:k + 1]).then_inc(exp_done, 1)
                    act.wait_ge(rest_ready, g + 1 + ONE)
                    act.activation(ER[:], rest[:, k, :], ACT.Exp, bias=mx[:, k:k + 1]).then_inc(rest_exp, 1)

                def norm(g, t):
                    act.wait_ge(u_ready, g + 1 + ONE)
                    act.wait_ge(li_ready, g + 1 + ONE)
                    act.wait_ge(ut_turned, (g if t == 0 else g - 1) + ONE)
                    act.activation(U[:, t % 2, :], psU[:, 0:128], ACT.Copy,
                                   scale=li[:, t % 2:t % 2 + 1]).then_inc(us_ready, 1)

                def copy(out, src):
                    return act.activation(out, src, ACT.Copy)

                def iteration(i, first, final):
                    g = i * T
                    for t in range(T):
                        more = t + AHEAD < T or not final
                        if topk:
                            exps_topk(g + t, t)
                            if t:
                                norm(g + (t - 1), t - 1)
                            elif not first:
                                norm(g - 1, T - 1)
                        if t == 4:
                            stationary(i * 2 + 1, 1)
                        if t == 12 and not final:
                            stationary(i * 2 + 2, 0)
                        if topk:
                            if more:
                                copy_scores(g + (t + AHEAD), t + AHEAD)
                            copy_weights(act, copy, g + t, t, 0)
                            copy_weights(act, copy, g + t, t, 1)
                        copy_weights(act, copy, g + t, t, 2)
                        copy_weights(act, copy, g + t, t, 3)
                        if not topk:
                            if more:
                                exps(g + (t + AHEAD), t + AHEAD)
                            norm(g + t, t)

                stationary(0, 0)
                for t in range(AHEAD):
                    if topk:
                        copy_scores(t, t, first=True)
                    else:
                        exps(t, t, first=True)
                iteration(0, True, False)
                with act.Fori(1, NI - 1) as i:
                    iteration(i, False, False)
                iteration(NI - 1, False, True)
                if topk:
                    norm(NI * T - 1, T - 1)

            @block.gpsimd
            def _(pool):
                if masked:
                    def convert(i, b, j, first):
                        pool.wait_ge(loaded[j], (i + 1) * LOADS + ONE)
                        if not first:
                            pool.wait_ge(max_ready, i * T + (j * TB - TB) + ONE)
                        settle(pool)
                        pool.tensor_scalar(maskf[:, j, :], mask8[:, j, :], -1.0, -NEG, ALU.add, ALU.mult
                                           ).then_inc(mask_ready, 1)

                if not topk:
                    def lows(i, b, j):
                        pool.wait_ge(ctx_high, b + 1 + ONE)
                        settle(pool)
                        pool.tensor_copy(ctxH[:, j, 0:K], ctxM[:]).then_inc(ctx_cut, 1)
                        pool.tensor_tensor(ctxL[:, j, 0:K], ctxT[:, j, :], ctxM[:], ALU.subtract
                                           ).then_inc(ctx_cut, 1)
                        pool.wait_ge(stat_high, b + 1 + ONE)
                        settle(pool)
                        masked_stat = statM[:].rearrange("p (h s) -> p h s", s=S)
                        pool.tensor_copy(statH[:, j], masked_stat).then_inc(stat_cut, 1)
                        pool.tensor_tensor(statL[:, j], stat[:, j], masked_stat, ALU.subtract).then_inc(stat_cut, 1)

                    def batches(i, first):
                        for j in range(2):
                            if masked:
                                convert(i, i * 2 + j, j, first)
                            lows(i, i * 2 + j, j)

                    batches(0, True)
                    with pool.Fori(1, NI) as i:
                        batches(i, False)
                if topk:
                    def spread(b, j):
                        pool.wait_ge(qp_ready, b + 1 + ONE)
                        pool.tensor_tensor(
                            stat[:, j],
                            bc(topk[0][:, ds(b * S, S)].rearrange("p (a s) -> p a s", a=1), [128, H, S]),
                            bc(c.headmask[:].rearrange("p (h a) -> p h a", a=1), [128, H, S]), ALU.mult
                            ).then_inc(stat_ready, 1)

                    def weights(g, t):
                        pool.wait_ge(rest_exp, g + 1 + ONE)
                        pool.wait_ge(u_ready, (g if t == 0 else g - 1) + ONE)
                        pool.tensor_tensor(P[:, t % 2, :], EX[:], ER[:], ALU.subtract).then_inc(p_ready, 1)

                    def iteration(i, final):
                        for t in range(T):
                            weights(i * T + t, t)
                            if t == 3:
                                spread(i * 2 + 1, 1)
                            if t == 11 and not final:
                                spread(i * 2 + 2, 0)

                    spread(0, 0)
                    with pool.Fori(0, NI - 1) as i:
                        iteration(i, False)
                    iteration(NI - 1, True)

            @block.vector
            def _(dve):
                def maxima(g, t, link, first=False, between=None):
                    k = t % 2
                    m = mx[:, k:k + 1]
                    if not first:
                        dve.wait_ge(exp_done, g - 1 + ONE)
                    if masked:
                        b = t // TB
                        dve.wait_ge(mask_ready, link.batch + b + 1 + ONE)
                    if topk:
                        if not first:
                            dve.wait_ge(rest_exp, g - 1 + ONE)
                        dve.wait_ge(copied, g + 1 + ONE)
                        settle(dve)
                        link(dve.max(top[:, 0, :], SS[:, k, :]))
                        dve.tensor_scalar(m, top[:, 0, 0:1], -1.0, None, ALU.mult).then_inc(max_ready, 1)
                        if between:
                            between()
                        link(dve.match_replace(rest[:, k, :], top[:, 0, :], SS[:, k, :], -3.0e38))
                        for r in range(1, 4):
                            link(dve.max(top[:, r, :], rest[:, k, :]))
                            last = dve.match_replace(rest[:, k, :], top[:, r, :], rest[:, k, :], -3.0e38)
                            if r < 3:
                                link(last)
                        last.then_inc(rest_ready, 1)
                        return
                    for a, (lo, hi) in enumerate(((0, 1024), (1024, K))):
                        dve.wait_ge(scores_ready if a else front_ready, g + 1 + ONE)
                        pm = pmx[:, k, a:a + 1]
                        if masked:
                            settle(dve)
                            dve.tensor_tensor_reduce(out=SS[:, k, lo:hi], in0=psS[:, lo:hi],
                                                     in1=maskf[:, t // TB % 2, lo:hi], scale=1.0, scalar=NEG * 4,
                                                     op0=ALU.add, op1=ALU.max, accum_out=pm).then_inc(part_max, 1)
                        else:
                            dve.tensor_reduce(pm, psS[:, lo:hi], X, ALU.max).then_inc(part_max, 1)
                    dve.wait_ge(part_max, g * 2 + 2 + ONE)
                    settle(dve)
                    dve.tensor_scalar(m, pmx[:, k, 0:1], pmx[:, k, 1:2], -1.0, ALU.max, ALU.mult
                                      ).then_inc(max_ready, 1)

                def high_context(loads, b, j, used):
                    dve.wait_ge(loaded[j], loads * LOADS + ONE)
                    dve.wait_ge(scores_ready, used + ONE)
                    dve.wait_ge(ctx_cut, b * 2 + ONE)
                    settle(dve)
                    dve.tensor_scalar(ctxM[:].bitcast(I32), ctxT[:, j, :].bitcast(I32), HIGH, None,
                                      ALU.bitwise_and).then_inc(ctx_high, 1)

                def high_queries(b, j):
                    dve.wait_ge(stat_ready, b + 1 + ONE)
                    dve.wait_ge(stat_cut, b * 2 + ONE)
                    settle(dve)
                    dve.tensor_scalar(statM[:].bitcast(I32), stat[:, j].rearrange("p h s -> p (h s)").bitcast(I32),
                                      HIGH, None, ALU.bitwise_and).then_inc(stat_high, 1)

                def inverse(g, t):
                    k = t % 2
                    dve.wait_ge(us_ready, (g if t == 0 else g - 1) + ONE)
                    if topk:
                        dve.wait_ge(u_ready, g + 1 + ONE)
                        src = psU[:, D:D + 1]
                    else:
                        dve.wait_ge(exp_done, g + 1 + ONE)
                        src = ls[:, k:k + 1]
                    dve.reciprocal(li[:, k:k + 1], src).then_inc(li_ready, 1)

                def copy_ut(g, t):
                    dve.wait_ge(ut_turned, g + 1 + ONE)
                    dve.tensor_copy(UT[:, t // TB, t % TB, :], psZ[:, 0:128]).then_inc(ut_ready, 1)

                def add(i, b, j, link):
                    dve.wait_ge(y_ready, b + 1 + ONE)
                    r = slice(j * S, j * S + S)
                    xt = c.x[r, i, :] if isinstance(i, int) else c.x[r, ds(i, 1), :].rearrange("p a d -> p (a d)")
                    link(dve.tensor_tensor(xt, xt, psZ[r, 128:256], ALU.add))
                    dve.tensor_tensor(xt, xt, c.bias_row[r, :], ALU.add).then_inc(x_done, 1)

                def finish(i, t, link, first):
                    g = i * T
                    inverse(g + t, t)
                    if t == 9:
                        add(i, i * 2, 0, link)
                    if t == 1 and not first:
                        add(i - 1, i * 2 - 1, 1, link)
                    if t:
                        copy_ut(g + (t - 1), t - 1)
                    elif not first:
                        copy_ut(g - 1, T - 1)

                def iteration(i, first, final):
                    g = i * T
                    link = Link(dve, order, HEAD if first else i * LINKS + (HEAD - 1))
                    link.batch = i * 2
                    for t in range(T):
                        more = t + (2 if topk else 1) < T or not final
                        if not topk:
                            if t == 2:
                                high_context(i + 1, i * 2 + 1, 1, g)
                            if t == 10 and not final:
                                high_context(i + 2, i * 2 + 2, 0, g + TB)
                            if t == 5:
                                high_queries(i * 2 + 1, 1)
                            if t == 13 and not final:
                                high_queries(i * 2 + 2, 0)
                        if topk and more:
                            maxima(g + (t + 2), t + 2, link, between=lambda: finish(i, t, link, first))
                        if not topk:
                            copy_weights(dve, dve.tensor_copy, g + t, t, 0)
                            copy_weights(dve, dve.tensor_copy, g + t, t, 1)
                            if more:
                                maxima(g + (t + 1), t + 1, link)
                        if not (topk and more):
                            finish(i, t, link, first)
                    assert final or link.n == LINKS - first, link.n
                    return link

                head = Link(dve, order)
                head.batch = 0
                if not topk:
                    high_context(1, 0, 0, 0)
                    high_queries(0, 0)
                maxima(0, 0, head, first=True)
                if topk:
                    maxima(1, 1, head, first=True)
                HEAD = head.n
                iteration(0, True, False)
                with dve.Fori(1, NI - 1) as i:
                    iteration(i, False, False)
                link = iteration(NI - 1, False, True)
                copy_ut(NI * T - 1, T - 1)
                add(NI - 1, B - 1, 1, link)
                dve.wait_ge(x_done, B + ONE)


def zero_bias(c):
    nc = c.nc
    z = c.sem("bias_zero")
    with nc.Block() as block:
        @block.gpsimd
        def _(pool):
            pool.memset(c.bias_row[:], 0.0).then_inc(z, 1)
            pool.wait_ge(z, 1 + ONE)


def wide_cross_attention(c, wq, wk, wv, wo, bo, scale, masked):
    with ExitStack() as st:
        M = c.sb(st, "M", [128, H, D])
        N = c.sb(st, "N", [128, H, D])
        with ExitStack() as s2:
            w = [c.sb(s2, f"w{n}", [128, 8, 128]) for n in range(4)]
            wT = [c.sb(s2, f"wT{n}", [128, 8, 128]) for n in range(3)]
            loads = [(w[n][:].rearrange("p a b -> p (a b)"), a) for n, a in enumerate((wq, wk, wv))]
            loads.append((w[3][:], wo.rearrange("(a p) d -> p a d", p=128)))
            if bo is not None:
                loads.append((c.bias_row[:], row_bcast(bo)))
            load_all(c, loads)
            if bo is None:
                zero_bias(c)
            turn_all(c, [(wT[n][:, a, :], w[n][:, a, :]) for n in range(3) for a in range(8)])

            def half(t, h):
                return t[(h % 2) * 64:(h % 2) * 64 + 64, h // 2, :]

            multiply_all(c, [(M[:, h, :], [(half(wT[0], h), half(wT[1], h))]) for h in range(H)]
                         + [(N[:, h, :], [(half(wT[2], h), half(w[3], h))]) for h in range(H)])
        cross_attention(c, M, N, scale, masked=masked)


def stage_l1_xattn(c):
    d = c.dram
    layernorm(c)
    wide_cross_attention(c, d["L1_xattn_Wq"], d["L1_xattn_Wk"], d["L1_xattn_Wv"], d["L1_xattn_Wo"],
                         d["L1_xattn_bo"], 0.125, True)


def stage_l2_xattn(c):
    d = c.dram
    layernorm(c)
    wide_cross_attention(c, d["L2_xattn_w_q"], d["L2_xattn_w_k"], d["L2_xattn_w_v"], d["L2_xattn_w_o"],
                         None, 0.125, False)


def stage_l3_xattn(c):
    nc, d = c.nc, c.dram
    layernorm(c)
    with ExitStack() as st:
        N = c.sb(st, "N3", [128, H, D])
        QT = c.sb(st, "QT", [128, B * S])
        WT = c.sb(st, "WT", [128, 3, D])
        bias = c.sb(st, "biases", [128, 3])
        with ExitStack() as s2:
            W = c.sb(s2, "W", [128, 4, D])
            WvN = c.sb(s2, "WvN", [128, D])
            bo = c.sb(s2, "bo", [128, D])
            bv_row = c.sb(s2, "bv_row", [128, 128])
            load_all(c, [(W[:, 0, :], d["L3_xattn_Wq"]), (W[:, 1, :], d["L3_xattn_Wk"]),
                         (W[:, 2, :], d["L3_xattn_Wo"]), (WvN[:], d["L3_xattn_Wv"]),
                         (bo[:], row_bcast(d["L3_xattn_bo"]))]
                     + [(bias[:, n:n + 1], d[f"L3_xattn_{v}"].rearrange("(p a) -> p a", a=1))
                        for n, v in enumerate(("bq", "bk", "bv"))])
            turn_all(c, [(WT[:, n, :], W[:, n, :]) for n in range(3)])
            head_blocks(c, s2, WvN[:], WT[:, 2, :], N)
            spread_bias(c, bias[:, 2:3], WT[:, 2, :], bo)
            project(c, QT, WT[:, 0, :], c.xnT, bias[:, 0:1], 8.0 ** -0.5)
        cross_attention(c, None, N, None, topk=(QT, WT[:, 1, :], bias[:, 1:2]))


def spread_bias(c, col, w, bo):
    nc = c.nc
    with ExitStack() as st:
        cols = c.sb(st, "bias_cols", [128, 128])
        pb = c.ps(st, "bias_ps", [128, D])
        made, summed, done = c.sem("cols_made"), c.sem("bias_summed"), c.sem("bias_done")
        with nc.Block() as block:
            @block.vector
            def _(dve):
                dve.tensor_scalar(cols[:], c.ones[:], col, None, ALU.mult).then_inc(made, 1)
                dve.wait_ge(summed, 1 + ONE)
                if bo is None:
                    dve.tensor_copy(c.bias_row[:], pb[:]).then_inc(done, 1)
                else:
                    dve.tensor_tensor(c.bias_row[:], pb[:], bo[:], ALU.add).then_inc(done, 1)
                dve.wait_ge(done, 1 + ONE)

            @block.tensor
            def _(pe):
                pe.wait_ge(made, 1 + ONE)
                pe.matmul(pb[:], cols[:], w, start=True, stop=True).then_inc(summed, 1)


def project(c, out, w, src, bias, scale):
    nc = c.nc
    with ExitStack() as st:
        pp = c.ps(st, "proj", [128, B * S])
        summed, done = c.sem("proj_summed"), c.sem("proj_done")
        with nc.Block() as block:
            @block.tensor
            def _(pe):
                for n in range(0, B * S, 512):
                    pe.matmul(pp[:, n:n + 512], w, src[:, n:n + 512], start=True, stop=True).then_inc(summed, 1)

            @block.vector
            def _(dve):
                dve.wait_ge(summed, B * S // 512 + ONE)
                if bias is None:
                    dve.tensor_scalar(out[:], pp[:], scale, None, ALU.mult).then_inc(done, 1)
                else:
                    dve.tensor_scalar(out[:], pp[:], bias, scale, ALU.add, ALU.mult).then_inc(done, 1)
                dve.wait_ge(done, 1 + ONE)


def attention_masks(c, st, kind):
    nc = c.nc
    mask = c.sb(st, "mask", [128, 1, S])
    flag = c.sb(st, "flag", [128, 1])
    order = c.sem("mask_order")
    with nc.Block() as block:
        @block.gpsimd
        def _(pool):
            link = Link(pool, order)
            link(pool.memset(mask[:], 0.0))
            link(pool.memset(flag[:], 1.0))
            for b in range(2):
                m = mask[b * S:b * S + S, 0, :]
                link(pool.affine_select(out=m, in_=m, compare_op=ALU.is_ge, fill=NEG, base=0,
                                        pattern=[[-1, S]], channel_multiplier=1))
                if kind == "h":
                    for k in range(0, S, 16):
                        mk = mask[b * S:b * S + S, 0, k:k + 16]
                        link(pool.affine_select(out=mk, in_=mk, compare_op=ALU.is_ge, fill=NEG, base=k + 15,
                                                pattern=[[0, 16]], channel_multiplier=-1))
                    f = flag[b * S:b * S + S, :]
                    link(pool.affine_select(out=f, in_=f, compare_op=ALU.is_ge, fill=0.0, base=-S // 2,
                                            pattern=[[0, 1]], channel_multiplier=1))
            if kind == "h":
                for e in range(0, 128, 2):
                    link(pool.affine_select(out=flag[:], in_=flag[:], compare_op=ALU.not_equal, fill=0.0,
                                            base=-e, pattern=[[0, 1]], channel_multiplier=1))
    return mask, flag


LINKS_SA = {"l0": 10, "l1": 7, "l2": 5, "h": 16}


def small_attention(c, kind, W, Wq=None, bq=None, Wk=None, bk=None, M=None, scale=1.0, bv_row=None, Wf=None):
    nc = c.nc
    V = 32 if kind == "l1" else D
    LANES = range(2)
    NI = NT // 2
    with ExitStack() as st:
        def lanes(name, shape):
            return [c.sb(st, f"{name}{l}", shape) for l in LANES]

        def signals(name):
            return [c.sem(f"{name}{l}") for l in LANES]

        mask, flag = attention_masks(c, st, kind) if kind != "l2" else (None, None)
        xs, qT, kT = lanes("xs", [128, 128]), lanes("qT", [128, 128]), lanes("kT", [128, 128])
        Kb = lanes("Kb", [128, 2, H, S]) if kind != "h" else None
        Sm, Pn, PT = lanes("Sm", [128, H, S]), lanes("Pn", [128, H, S]), lanes("PT", [128, 8, 128])
        mx, sm = lanes("mx", [128, H, 1]), lanes("sm", [128, H, 1])
        VW = lanes("VW", [128, 2, 8, 2 if kind == "l1" else 1, V])
        if kind == "l0":
            Ksq, qsq, qm2 = lanes("Ksq", [128, 2, H, S]), lanes("qsq", [128, 128]), lanes("qm2", [128, 128])
            hmx = c.sb(st, "hmx", [128, H, S])
        if kind == "l1":
            G, GT = lanes("G", [128, 512]), lanes("GT", [128, 4, 128])
        if kind == "h":
            qh, qc = lanes("qh", [128, H, 128]), lanes("qc", [128, H, 64, 2])
            xc, A1 = lanes("xc", [128, 2, 16]), lanes("A1", [128, H, 16])
            mx1, sm1 = lanes("mx1", [128, H, 1]), lanes("sm1", [128, H, 1])
        psS = [c.ps(st, f"psS{l}", [128, 2, 512]) for l in LANES]
        psW = [c.ps(st, f"psW{l}", [128, 1024]) for l in LANES]
        order = c.sem("order")
        xs_ready, proj_ready, qk_ready = signals("xs_ready"), signals("proj_ready"), signals("qk_ready")
        kb_ready, ksq_ready, s_ready = signals("kb_ready"), signals("ksq_ready"), signals("s_ready")
        sq_ready, w_free, sub_ready, e_ready = (signals(n) for n in ("sq_ready", "w_free", "sub_ready", "e_ready"))
        pn_ready, v_ready, vw_ready = signals("pn_ready"), signals("v_ready"), signals("vw_ready")
        turned, pt_ready, o_ready = signals("turned"), signals("pt_ready"), signals("o_ready")
        o_added, g_ready, g_turned = signals("o_added"), signals("g_ready"), signals("g_turned")
        gt_ready, y_ready, x_done = signals("gt_ready"), signals("y_ready"), signals("x_done")
        W2 = W.rearrange("p (a b) v -> p b a v", b=2)

        if kind in ("l0", "l1"):
            zeroed = c.sem("zeroed")
            with nc.Block() as block:
                @block.vector
                def _(dve):
                    if kind == "l1":
                        for l in LANES:
                            dve.memset(VW[l][:], 0.0).then_inc(zeroed, 1)
                        dve.wait_ge(zeroed, 2 + ONE)
                    else:
                        dve.tensor_copy(hmx[:], bc(c.headmask[:].rearrange("p (h a) -> p h a", a=1), [128, H, S])
                                        ).then_inc(zeroed, 1)
                        dve.wait_ge(zeroed, 1 + ONE)

        with nc.Block() as block:
            @block.vector
            def _(dve):
                def tokens(i, l, link):
                    dve.tensor_copy(xs[l][:], c.xnT[:, ds(i * 256 + l * 128, 128)]).then_inc(xs_ready[l], 1)

                def operands(i, l, link):
                    q, k = qT[l][:], kT[l][:]
                    dve.wait_ge(xs_ready[l], i + 1 + ONE)
                    settle(dve)
                    if kind in ("l0", "l1"):
                        dve.wait_ge(proj_ready[l], i + 1 + ONE)
                        if kind == "l0":
                            link(dve.tensor_scalar(q, psW[l][:, 0:128], bq, None, ALU.add))
                            link(dve.tensor_tensor(qsq[l][:], q, q, ALU.mult))
                            link(dve.tensor_scalar(qm2[l][:], q, -2.0, None, ALU.mult))
                        else:
                            link(dve.tensor_copy(q, xs[l][:]))
                        dve.tensor_scalar(k, psW[l][:, 512:640], bk, None, ALU.add).then_inc(qk_ready[l], 1)
                    elif kind == "l2":
                        link(dve.tensor_scalar(q, xs[l][:], scale, None, ALU.mult))
                        dve.tensor_copy(k, xs[l][:]).then_inc(qk_ready[l], 1)
                    else:
                        for b in range(2):
                            pair = xs[l][:, b * S:b * S + 32].rearrange("p (a b) -> p a b", b=2)
                            link(dve.tensor_tensor(xc[l][:, b, :], pair[:, :, 0], pair[:, :, 1], ALU.add))
                        link(dve.tensor_scalar(xc[l][:], xc[l][:], 0.5, None, ALU.mult))

                def head_queries(i, l, link):
                    for n in range(2):
                        dve.wait_ge(proj_ready[l], i * 2 + (n + 1) + ONE)
                        dve.tensor_scalar(qh[l][:, 8 * n:8 * n + 8, :].rearrange("p h t -> p (h t)"), psW[l][:],
                                          scale, None, ALU.mult).then_inc(w_free[l], 1)
                    dve.wait_ge(w_free[l], i * 2 + 2 + ONE)
                    settle(dve)
                    pair, qcl = qh[l][:].rearrange("p h (a b) -> p h a b", b=2), qc[l]
                    link(dve.tensor_tensor(qcl[:, :, :, 0], pair[:, :, :, 0], pair[:, :, :, 1], ALU.add))
                    link(dve.tensor_scalar(qcl[:, :, :, 0], qcl[:, :, :, 0], 0.5, None, ALU.mult))
                    dve.tensor_copy(qcl[:, :, :, 1], qcl[:, :, :, 0]).then_inc(qk_ready[l], 1)

                def out_of_w(i, l, link):
                    dve.wait_ge(s_ready[l], i + 1 + ONE)
                    if kind == "l0":
                        dve.tensor_scalar(Sm[l][:].rearrange("p h k -> p (h k)"), psW[l][:], 1e-6, None, ALU.add
                                          ).then_inc(w_free[l], 1)
                    else:
                        s1 = psW[l][:, 0:256].rearrange("p (h k) -> p h k", k=16)
                        link(dve.reduce_max(mx1[l][:, :, 0], s1, axis=X))
                        dve.tensor_tensor(A1[l][:], s1, bc(mx1[l][:], [128, H, 16]), ALU.subtract
                                          ).then_inc(sub_ready[l], 1)

                def shift(i, l, link):
                    dve.wait_ge(s_ready[l], i + 1 + ONE)
                    settle(dve)
                    scores, s = psS[l][:].rearrange("p a (h k) -> p (a h) k", k=S), Sm[l]
                    if kind == "l0":
                        dve.wait_ge(w_free[l], i + 1 + ONE)
                        link(dve.reciprocal(s[:], s[:]))
                        dve.wait_ge(sq_ready[l], i + 1 + ONE)
                        link(dve.tensor_tensor(s[:], s[:], Pn[l][:], ALU.mult))
                        scores = s[:]
                    if kind != "l2":
                        link(dve.tensor_tensor(s[:], scores, bc(mask[:], [128, H, S]), ALU.add))
                        scores = s[:]
                    link(dve.reduce_max(mx[l][:, :, 0], scores, axis=X))
                    dve.tensor_tensor(s[:], scores, bc(mx[l][:], [128, H, S]), ALU.subtract
                                      ).then_inc(sub_ready[l], 1)

                def weigh(i, l, link):
                    e, m = Pn[l], sm[l]
                    dve.wait_ge(e_ready[l], i * (2 if kind == "h" else 1) + (2 if kind == "h" else 1) + ONE)
                    link(dve.reduce_sum(m[:, :, 0], e[:], axis=X))
                    if kind == "h":
                        m1 = sm1[l]
                        link(dve.reduce_sum(m1[:, :, 0], A1[l][:], axis=X))
                        link(dve.tensor_scalar(m1[:], m1[:], flag[:], 1e-8, ALU.mult, ALU.add))
                        link(dve.tensor_tensor(m[:], m[:], m1[:], ALU.add))
                        pairs = e[:, :, 0:32].rearrange("p h (a b) -> p h a b", b=2)
                        for n in range(2):
                            link(dve.scalar_tensor_tensor(out=pairs[:, :, :, n], in0=A1[l][:], scalar=flag[:],
                                                          in1=pairs[:, :, :, n], op0=ALU.mult, op1=ALU.add))
                    link(dve.reciprocal(m[:, :, 0], m[:, :, 0]))
                    dve.tensor_tensor(e[:], e[:], bc(m[:], [128, H, S]), ALU.mult).then_inc(pn_ready[l], 1)

                def add_bias(i, l, link):
                    dve.wait_ge(o_ready[l], i + 1 + ONE)
                    dve.tensor_tensor(G[l][:], psS[l][:, 0, :], bv_row, ALU.add).then_inc(o_added[l], 1)

                def add(i, l, link):
                    xt = c.x[:, ds(i * 2 + l, 1), :].rearrange("p a d -> p (a d)")
                    if kind == "l1":
                        dve.wait_ge(y_ready[l], i + 1 + ONE)
                        link(dve.tensor_tensor(xt, xt, psS[l][:, 1, 0:128], ALU.add))
                        link(dve.tensor_tensor(xt, xt, c.xn[:, ds(i * 2 + l, 1), :].rearrange("p a d -> p (a d)"),
                                               ALU.add))
                    else:
                        dve.wait_ge(o_ready[l], i + 1 + ONE)
                        link(dve.tensor_tensor(xt, xt, psS[l][:, 0, 0:128], ALU.add))
                    dve.tensor_tensor(xt, xt, c.bias_row[:], ALU.add).then_inc(x_done[l], 1)

                steps = [tokens, operands]
                steps += [head_queries] if kind == "h" else []
                steps += [out_of_w] if kind in ("l0", "h") else []
                steps += [shift, weigh]
                steps += [add_bias] if kind == "l1" else []
                steps += [add]
                with dve.Fori(0, NI) as i:
                    link = Link(dve, order, i * (2 * LINKS_SA[kind]))
                    for step in steps:
                        for l in LANES:
                            step(i, l, link)
                    assert link.n == 2 * LINKS_SA[kind], (kind, link.n)
                for l in LANES:
                    dve.wait_ge(x_done[l], NI + ONE)

            @block.gpsimd
            def _(pool):
                if kind == "h":
                    return
                with pool.Fori(0, NI) as i:
                    for l in LANES:
                        pool.wait_ge(qk_ready[l], i + 1 + ONE)
                        for b in range(2):
                            pool.tensor_tensor(
                                Kb[l][:, b],
                                bc(kT[l][:, b * S:b * S + S].rearrange("p (a s) -> p a s", a=1), [128, H, S]),
                                bc(c.headmask[:].rearrange("p (h a) -> p h a", a=1), [128, H, S]), ALU.mult
                                ).then_inc(kb_ready[l], 1)

            @block.scalar
            def _(act):
                def key_squares(i, l):
                    act.wait_ge(kb_ready[l], i * 2 + 2 + ONE)
                    act.activation(Ksq[l][:], Kb[l][:], ACT.Square).then_inc(ksq_ready[l], 1)

                def dot_squares(i, l):
                    act.wait_ge(s_ready[l], i + 1 + ONE)
                    act.activation(Pn[l][:].rearrange("p h k -> p (h k)"), psS[l][:].rearrange("p a b -> p (a b)"),
                                   ACT.Square).then_inc(sq_ready[l], 1)

                def values(i, l, b):
                    act.wait_ge(v_ready[l], i * 2 + (b + 1) + ONE)
                    if kind == "l1":
                        for e in range(2):
                            r = slice(e * 64, e * 64 + 64)
                            last = act.activation(VW[l][r, b, :, e, :],
                                                  psW[l][r, 0:256].rearrange("p (a v) -> p a v", v=V), ACT.Copy)
                    else:
                        last = act.activation(VW[l][:, b].rearrange("p a c v -> p (a c v)"), psW[l][:], ACT.Copy)
                    last.then_inc(vw_ready[l], 1)

                def exps(i, l):
                    if kind == "h":
                        act.wait_ge(sub_ready[l], i * 2 + 1 + ONE)
                        act.activation(A1[l][:], A1[l][:], ACT.Exp).then_inc(e_ready[l], 1)
                        act.wait_ge(sub_ready[l], i * 2 + 2 + ONE)
                    else:
                        act.wait_ge(sub_ready[l], i + 1 + ONE)
                    act.activation(Pn[l][:], Sm[l][:], ACT.Exp).then_inc(e_ready[l], 1)

                def weights(i, l):
                    act.wait_ge(turned[l], i + 1 + ONE)
                    act.activation(PT[l][:].rearrange("p a t -> p (a t)"), psW[l][:], ACT.Copy
                                   ).then_inc(pt_ready[l], 1)

                def gelu(i, l):
                    act.wait_ge(o_added[l], i + 1 + ONE)
                    act.activation(G[l][:], G[l][:], ACT.Gelu).then_inc(g_ready[l], 1)

                def gelu_turned(i, l):
                    act.wait_ge(g_turned[l], i + 1 + ONE)
                    act.activation(GT[l][:].rearrange("p a t -> p (a t)"), psW[l][:, 0:512], ACT.Copy
                                   ).then_inc(gt_ready[l], 1)

                steps = [key_squares, dot_squares] if kind == "l0" else []
                steps += [lambda i, l, b=b: values(i, l, b) for b in range(2)]
                steps += [exps, weights]
                steps += [gelu, gelu_turned] if kind == "l1" else []
                with act.Fori(0, NI) as i:
                    for step in steps:
                        for l in LANES:
                            step(i, l)

            @block.tensor
            def _(pe):
                def project(i, l):
                    pe.wait_ge(xs_ready[l], i + 1 + ONE)
                    if kind == "l0":
                        pe.matmul(psW[l][:, 0:128], Wq, xs[l][:], start=True, stop=True)
                    if kind in ("l0", "l1"):
                        pe.matmul(psW[l][:, 512:640], Wk, xs[l][:], start=True, stop=True).then_inc(proj_ready[l], 1)

                def project_heads(i, l, n):
                    if n:
                        pe.wait_ge(w_free[l], i * 2 + 1 + ONE)
                    for h in range(8):
                        last = pe.matmul(psW[l][:, h * 128:h * 128 + 128], M[:, 8 * n + h, :], xs[l][:],
                                         start=True, stop=True)
                    last.then_inc(proj_ready[l], 1)

                def scores(i, l):
                    pe.wait_ge(qk_ready[l], i + 1 + ONE)
                    if kind != "h":
                        pe.wait_ge(kb_ready[l], i * 2 + 2 + ONE)
                    if kind == "l0":
                        pe.wait_ge(ksq_ready[l], i + 1 + ONE)
                    pe.wait_ge(x_done[l], i + ONE)
                    for b in range(2):
                        r = slice(b * S, b * S + S)
                        if kind == "h":
                            for h in range(H):
                                pe.matmul(psS[l][r, h // 8, (h % 8) * S:(h % 8) * S + S], qh[l][:, h, r],
                                          xs[l][:, r], start=True, stop=True)
                                last = pe.matmul(psW[l][r, h * 16:h * 16 + 16],
                                                 qc[l][:].rearrange("p h a b -> p h (a b)")[:, h, r],
                                                 xc[l][:, b, :], start=True, stop=True)
                            continue
                        for n in range(2):
                            hs = slice(8 * n, 8 * n + 8)
                            last = pe.matmul(psS[l][r, n, :], qT[l][:, r], Kb[l][:, b, hs, :], start=True, stop=True)
                            if kind == "l0":
                                far = psW[l][r, n * 512:n * 512 + 512]
                                pe.matmul(far, c.ones[:, 0:S], Ksq[l][:, b, hs, :], start=True, stop=False)
                                pe.matmul(far, qsq[l][:, r], hmx[:, hs, :], start=False, stop=False)
                                last = pe.matmul(far, qm2[l][:, r], Kb[l][:, b, hs, :], start=False, stop=True)
                    last.then_inc(s_ready[l], 1)

                def values(i, l, b):
                    if kind == "l0":
                        pe.wait_ge(w_free[l], i + 1 + ONE)
                    if kind == "h":
                        pe.wait_ge(sub_ready[l], i * 2 + 1 + ONE)
                    pe.wait_ge(vw_ready[l], i * 2 + b + ONE)
                    for e in range(2):
                        for n in range(0, 8 * V, 512):
                            w = min(512, 8 * V)
                            hs = slice(n // V, (n + w) // V)
                            last = pe.matmul(psW[l][e * 64:e * 64 + 64, n:n + w],
                                             xs[l][:, b * S:b * S + S], W2[:, e, hs, :], start=True, stop=True)
                    last.then_inc(v_ready[l], 1)

                def turn(i, l):
                    pe.wait_ge(pn_ready[l], i + 1 + ONE)
                    pe.wait_ge(vw_ready[l], i * 2 + 2 + ONE)
                    for a in range(8):
                        last = pe.transpose(psW[l][:, a * 128:a * 128 + 128],
                                            Pn[l][:, 2 * a:2 * a + 2, :].rearrange("p h k -> p (h k)"), c.ident[:])
                    last.then_inc(turned[l], 1)

                def sums(i, l):
                    pe.wait_ge(pt_ready[l], i + 1 + ONE)
                    for b in range(2):
                        r = slice(b * S, b * S + S)
                        for a in range(8):
                            if kind == "l1":
                                last = pe.matmul(psS[l][r, 0, a * 64:a * 64 + 64], PT[l][:, a, r],
                                                 VW[l][:, b, a].rearrange("p c v -> p (c v)"), start=True, stop=True)
                            else:
                                last = pe.matmul(psS[l][r, 0, 0:128], PT[l][:, a, r], VW[l][:, b, a, 0, :],
                                                 start=(a == 0), stop=(a == 7))
                    last.then_inc(o_ready[l], 1)

                def turn_gelu(i, l):
                    pe.wait_ge(g_ready[l], i + 1 + ONE)
                    for a in range(4):
                        last = pe.transpose(psW[l][:, a * 128:a * 128 + 128], G[l][:, a * 128:a * 128 + 128],
                                            c.ident[:])
                    last.then_inc(g_turned[l], 1)

                def output(i, l):
                    pe.wait_ge(gt_ready[l], i + 1 + ONE)
                    for a in range(4):
                        last = pe.matmul(psS[l][:, 1, 0:128], GT[l][:, a, :], Wf[:, a, :],
                                         start=(a == 0), stop=(a == 3))
                    last.then_inc(y_ready[l], 1)

                steps = [project]
                steps += [lambda i, l, n=n: project_heads(i, l, n) for n in range(2)] if kind == "h" else []
                steps += [scores]
                steps += [lambda i, l, b=b: values(i, l, b) for b in range(2)]
                steps += [turn, sums]
                steps += [turn_gelu, output] if kind == "l1" else []
                with pe.Fori(0, NI) as i:
                    for step in steps:
                        for l in LANES:
                            step(i, l)


def stage_l0_attn(c):
    d = c.dram
    layernorm(c)
    with ExitStack() as st:
        W = c.sb(st, "W", [128, H, D])
        Wqkv = c.sb(st, "Wqkv", [128, 3, D])
        bias = c.sb(st, "bias", [128, 3])
        with ExitStack() as s2:
            Wo = c.sb(s2, "Wo", [128, D])
            bo = c.sb(s2, "bo", [128, D])
            WvT = c.sb(s2, "WvT", [128, D])
            load_all(c, [(Wqkv[:].rearrange("p a d -> p (a d)"), d["L0_attn_w_qkv"]), (Wo[:], d["L0_attn_w_out"]),
                         (bo[:], row_bcast(d["L0_attn_b_out"]))]
                     + [(bias[:, n:n + 1], d["L0_attn_b_qkv"][n * D:n * D + D].rearrange("(p a) -> p a", a=1))
                        for n in range(3)])
            turn_all(c, [(WvT[:], Wqkv[:, 2, :])])
            head_blocks(c, s2, WvT[:], Wo[:], W)
            spread_bias(c, bias[:, 2:3], Wo[:], bo)
        small_attention(c, "l0", W[:], Wq=Wqkv[:, 0, :], bq=bias[:, 0:1], Wk=Wqkv[:, 1, :], bk=bias[:, 1:2])


def stage_l1_attn(c):
    d = c.dram
    layernorm(c)
    with ExitStack() as st:
        W = c.sb(st, "W", [128, H, 32])
        Wk = c.sb(st, "Wk", [128, D])
        bk = c.sb(st, "bk", [128, 1])
        bv = c.sb(st, "bv", [128, 512])
        Wf = c.sb(st, "Wf", [128, 4, D])
        load_all(c, [(W[:].rearrange("p h v -> p (h v)"), d["L1_attn_Wv"]), (Wk[:], d["L1_attn_Wk"]),
                     (bk[:], d["L1_attn_bk"].rearrange("(p a) -> p a", a=1)), (bv[:], row_bcast(d["L1_attn_bv"])),
                     (Wf[:], d["L1_attn_Wf"].rearrange("(a p) d -> p a d", p=128)),
                     (c.bias_row[:], row_bcast(d["L1_attn_bf"]))])
        small_attention(c, "l1", W[:], Wk=Wk[:], bk=bk[:], bv_row=bv[:], Wf=Wf)


def stage_l2_attn(c):
    d = c.dram
    layernorm(c)
    with ExitStack() as st:
        W = c.sb(st, "W", [128, H, D])
        load_all(c, [(W[:], d["L2_attn_weight"].rearrange("(h p) d -> p h d", p=128))])
        zero_bias(c)
        small_attention(c, "l2", W[:], scale=8.0 ** -0.5)


def stage_l3_attn(c):
    d = c.dram
    layernorm(c)
    with ExitStack() as st:
        M = c.sb(st, "M", [128, H, D])
        W = c.sb(st, "W", [128, H, D])
        with ExitStack() as s2:
            w = c.sb(s2, "w", [128, 3, 8, D])
            wo = c.sb(s2, "wo", [128, 8, 128])
            woT = c.sb(s2, "woT", [128, 8, 128])
            load_all(c, [(w[:].rearrange("p q a d -> p (q a) d"),
                          d["L3_attn_w_qkv"].rearrange("(a p) d -> p a d", p=128)),
                         (wo[:].rearrange("p a b -> p (a b)"), d["L3_attn_w_out"]),
                         (c.bias_row[:], row_bcast(d["L3_attn_b_out"]))])
            turn_all(c, [(woT[:, a, :], wo[:, a, :]) for a in range(8)])

            def half(t, h):
                return t[(h % 2) * 64:(h % 2) * 64 + 64, h // 2, :]

            multiply_all(c, [(M[:, h, :], [(half(w[:, 0], h), half(w[:, 1], h))]) for h in range(H)]
                         + [(W[:, h, :], [(half(w[:, 2], h), half(woT, h))]) for h in range(H)])
        small_attention(c, "h", W[:], M=M, scale=0.125)


def route(c, st, Wr, br, weights, cap=None):
    nc = c.nc
    coef = c.sb(st, "coef", [128, NT, E])
    with ExitStack() as s:
        p = c.sb(s, "p", [128, NT, E])
        rest = c.sb(s, "rest", [128, NT, E])
        first = c.sb(s, "first", [128, 2, NT, E])
        rank = c.sb(s, "rank", [128, NT, E])
        m = c.sb(s, "m", [128, 2, NT, 1])
        r = c.sb(s, "r", [128, NT, 1])
        tri = c.sb(s, "tri", [128, 128])
        off = c.sb(s, "off", [128, 2, NT + 1, E])
        ps = c.ps(s, "logits", [128, NT * E])
        pc = c.ps(s, "counts", [128, 4, NT * E])
        made, order, logits, sub, expd = (c.sem(n) for n in ("made", "order", "logits", "sub", "expd"))
        picked, counted, done = c.sem("picked"), c.sem("counted"), c.sem("done")
        with nc.Block() as block:
            @block.gpsimd
            def _(pool):
                link = Link(pool, made)
                link(pool.iota(rank[:], pattern=[[0, NT], [-1, E]], base=E, channel_multiplier=0,
                               allow_small_or_imprecise_dtypes=True))
                link(pool.memset(tri[:], 1.0))
                link(pool.affine_select(out=tri[:], in_=tri[:], compare_op=ALU.is_ge, fill=0.0, base=0,
                                        pattern=[[1, 128]], channel_multiplier=-1))

            @block.tensor
            def _(pe):
                for t in range(NT):
                    last = pe.matmul(ps[:, t * E:t * E + E], c.xnT[:, t * 128:t * 128 + 128], Wr,
                                     start=True, stop=True)
                last.then_inc(logits, 1)
                if cap:
                    pe.wait_ge(picked, 1 + ONE)
                    pe.wait_ge(made, 3 + ONE)
                    for k in range(2):
                        f = first[:, k].rearrange("p t e -> p (t e)")
                        pe.matmul(pc[:, k, :], tri[:], f, start=True, stop=True)
                        last = pe.matmul(pc[:, 2 + k, :], c.ones[:], f, start=True, stop=True)
                    last.then_inc(counted, 1)

            @block.scalar
            def _(act):
                act.wait_ge(sub, 1 + ONE)
                act.activation(p[:], p[:], ACT.Exp).then_inc(expd, 1)

            @block.vector
            def _(dve):
                link = Link(dve, order)
                dve.wait_ge(logits, 1 + ONE)
                link(dve.tensor_copy(p[:].rearrange("p t e -> p (t e)"), ps[:]))
                if br is not None:
                    link(dve.tensor_tensor(p[:], p[:], bc(br, [128, NT, E]), ALU.add))
                link(dve.reduce_max(r[:, :, 0], p[:], axis=X))
                dve.tensor_tensor(p[:], p[:], bc(r[:], [128, NT, E]), ALU.subtract).then_inc(sub, 1)
                dve.wait_ge(expd, 1 + ONE)
                link(dve.reduce_sum(r[:, :, 0], p[:], axis=X))
                link(dve.reciprocal(r[:, :, 0], r[:, :, 0]))
                link(dve.tensor_tensor(p[:], p[:], bc(r[:], [128, NT, E]), ALU.mult))
                link(dve.tensor_copy(rest[:], p[:]))
                dve.wait_ge(made, 3 + ONE)
                for k in range(2):
                    f = first[:, k]
                    link(dve.reduce_max(m[:, k, :, 0], rest[:], axis=X))
                    link(dve.tensor_tensor(f, rest[:], bc(m[:, k], [128, NT, E]), ALU.is_equal))
                    link(dve.tensor_tensor(f, f, rank[:], ALU.mult))
                    link(dve.reduce_max(r[:, :, 0], f, axis=X))
                    link(dve.tensor_tensor(f, f, bc(r[:], [128, NT, E]), ALU.is_equal))
                    if k == 0:
                        link(dve.scalar_tensor_tensor(out=rest[:], in0=f, scalar=-2.0, in1=rest[:],
                                                      op0=ALU.mult, op1=ALU.add))
                if cap:
                    link(dve.tensor_tensor(r[:], m[:, 0], m[:, 1], ALU.add))
                    link(dve.reciprocal(r[:, :, 0], r[:, :, 0]))
                    link(dve.tensor_tensor(p[:], p[:], bc(r[:], [128, NT, E]), ALU.mult))
                    dve.memset(off[:, 0, 0, :], 0.0).then_inc(picked, 1)
                    dve.wait_ge(counted, 1 + ONE)
                    for k in range(2):
                        if k:
                            link(dve.tensor_copy(off[:, 1, 0, :], off[:, 0, NT, :]))
                        for t in range(NT):
                            link(dve.tensor_tensor(off[:, k, t + 1, :], off[:, k, t, :],
                                                   pc[:, 2 + k, t * E:t * E + E], ALU.add))
                        link(dve.tensor_tensor(rest[:].rearrange("p t e -> p (t e)"),
                                               off[:, k, 0:NT, :].rearrange("p t e -> p (t e)"),
                                               pc[:, k, :], ALU.add))
                        link(dve.tensor_scalar(rest[:], rest[:], float(cap), None, ALU.is_le))
                        link(dve.tensor_tensor(first[:, k], first[:, k], rest[:], ALU.mult))
                link(dve.tensor_tensor(coef[:], first[:, 0], first[:, 1], ALU.add))
                if weights != "one":
                    link(dve.tensor_tensor(coef[:], coef[:], p[:], ALU.mult))
    return coef


def add_expert_bias(c, coef, b):
    nc = c.nc
    with ExitStack() as st:
        cT = c.sb(st, "coefT", [E, NT, 128])
        pb = c.ps(st, "pb", [128, NT, 128])
        summed, added = c.sem("bias_summed"), c.sem("bias_added")
        turn_all(c, [(cT[:, t, :], coef[:, t, :]) for t in range(NT)])
        with nc.Block() as block:
            @block.tensor
            def _(pe):
                for t in range(NT):
                    last = pe.matmul(pb[:, t, :], cT[:, t, :], b, start=True, stop=True)
                last.then_inc(summed, 1)

            @block.vector
            def _(dve):
                dve.wait_ge(summed, 1 + ONE)
                dve.tensor_tensor(c.x[:], c.x[:], pb[:], ALU.add).then_inc(added, 1)
                dve.wait_ge(added, 1 + ONE)


def experts(c, coef, w1, w2, C, func, b1=None):
    nc = c.nc
    turn = b1 is not None
    with ExitStack() as st:
        w1n = c.sb(st, "w1n", [128, 2, C, 128])
        w2n = c.sb(st, "w2n", [128, 2, C, 128])
        w1T = c.sb(st, "w1T", [128, 2, C, 128]) if turn else w1n
        hT = c.sb(st, "hT", [128, 2, C, 512])
        ce = c.sb(st, "ce", [128, 2, NT])
        be = c.sb(st, "be", [128, 2, C])
        psH = c.ps(st, "psH", [128, C, 512])
        psY = c.ps(st, "psY", [128, 2, 512])
        psX = c.ps(st, "psX", [128, 512])
        loaded = [c.sem("w_loaded0"), c.sem("w_loaded1")]
        w1_turned, w1_ready, coef_ready = c.sem("w1_turned"), c.sem("w1_ready"), c.sem("coef_ready")
        h_ready, h_done, y_ready, y_used = (c.sem(n) for n in ("h_ready", "h_done", "y_ready", "y_used"))
        with nc.Block() as block:
            def load(sp, e, j):
                sp.dma_start(w1n[:, j], w1[ds(e, 1)].rearrange("e (c p) d -> p (e c) d", p=128)
                             ).then_inc(loaded[j], 16)
                sp.dma_start(w2n[:, j], w2[ds(e, 1)].rearrange("e (c p) d -> p (e c) d", p=128)
                             ).then_inc(loaded[j], 16)

            @block.sync
            def _(sp):
                load(sp, 0, 0)
                load(sp, 1, 1)
                with sp.Fori(0, E // 2 - 1) as i:
                    for j in range(2):
                        sp.wait_ge(y_ready, i * 4 + (2 * j + 2) + ONE)
                        settle(sp)
                        load(sp, i * 2 + (2 + j), j)

            @block.tensor
            def _(pe):
                with pe.Fori(0, E // 2) as i:
                    def up(k):
                        j, half = k // 2, k % 2
                        if half == 0:
                            pe.wait_ge(loaded[j], (i + 1) * 32 + ONE)
                            if turn:
                                for q in range(C):
                                    last = pe.transpose(psX[:, q * 128:q * 128 + 128], w1n[:, j, q, :], c.ident[:])
                                last.then_inc(w1_turned, 1)
                                pe.wait_ge(w1_ready, i * 2 + (j + 1) + ONE)
                        pe.wait_ge(h_done, (i * 4 + k) * C + ONE)
                        for q in range(C):
                            pe.matmul(psH[:, q, :], w1T[:, j, q, :], c.xnT[:, half * 512:half * 512 + 512],
                                      start=True, stop=True).then_inc(h_ready, 1)

                    def down(k):
                        j = k // 2
                        pe.wait_ge(h_done, (i * 4 + k + 1) * C + ONE)
                        pe.wait_ge(y_used, i * 4 + (k - 1 if k else 0) + ONE)
                        for t in range(4):
                            for q in range(C):
                                last = pe.matmul(psY[:, k % 2, t * 128:t * 128 + 128],
                                                 hT[:, k % 2, q, t * 128:t * 128 + 128], w2n[:, j, q, :],
                                                 start=(q == 0), stop=(q == C - 1))
                        last.then_inc(y_ready, 1)

                    for k in range(5):
                        if k < 4:
                            up(k)
                        if k:
                            down(k - 1)

            @block.scalar
            def _(act):
                with act.Fori(0, E // 2) as i:
                    for k in range(4):
                        j = k // 2
                        if k % 2 == 0:
                            act.wait_ge(coef_ready, i * 2 + (j + 1) + ONE)
                        act.wait_ge(y_ready, i * 4 + (k - 1 if k else 0) + ONE)
                        for q in range(C):
                            act.wait_ge(h_ready, (i * 4 + k) * C + (q + 1) + ONE)
                            act.activation(hT[:, k % 2, q, :], psH[:, q, :], func,
                                           bias=be[:, j, q:q + 1] if turn else 0.0).then_inc(h_done, 1)

            @block.vector
            def _(dve):
                with dve.Fori(0, E // 2) as i:
                    def prepare(j):
                        dve.wait_ge(y_used, i * 4 + ONE)
                        dve.wait_ge(h_done, i * (4 * C) + ONE)
                        if turn:
                            dve.tensor_copy(be[:, j, :], b1[:, ds(i * 2 + j, 1), :].rearrange("p a q -> p (a q)"))
                        dve.tensor_copy(ce[:, j, :], coef[:, :, ds(i * 2 + j, 1)].rearrange("p t a -> p (t a)")
                                        ).then_inc(coef_ready, 1)
                        if turn:
                            dve.wait_ge(w1_turned, i * 2 + (j + 1) + ONE)
                            dve.tensor_copy(w1T[:, j].rearrange("p q d -> p (q d)"), psX[:, 0:C * 128]
                                            ).then_inc(w1_ready, 1)

                    def add(k):
                        j, half = k // 2, k % 2
                        dve.wait_ge(coef_ready, i * 2 + (j + 1) + ONE)
                        dve.wait_ge(y_used, i * 4 + k + ONE)
                        dve.wait_ge(y_ready, i * 4 + (k + 1) + ONE)
                        for t in range(4):
                            tt = half * 4 + t
                            last = dve.scalar_tensor_tensor(
                                out=c.x[:, tt, :], in0=psY[:, k % 2, t * 128:t * 128 + 128],
                                scalar=ce[:, j, tt:tt + 1], in1=c.x[:, tt, :], op0=ALU.mult, op1=ALU.add)
                        last.then_inc(y_used, 1)

                    prepare(0)
                    add(0)
                    prepare(1)
                    for k in range(1, 4):
                        add(k)
                dve.wait_ge(y_used, 2 * E + ONE)


def stage_l1_ffn(c):
    d = c.dram
    layernorm(c)
    with ExitStack() as st:
        b1 = c.sb(st, "b1", [128, E, 4])
        b2 = c.sb(st, "b2", [E, D])
        Wr = c.sb(st, "Wr", [128, E])
        with ExitStack() as s2:
            g = c.sb(s2, "g", [E, D])
            b1n = c.sb(s2, "b1n", [32, 128])
            load_all(c, [(g[:], d["L1_ffn_gate_w"]), (b1n[:], d["L1_ffn_fc1_b"].rearrange("e a (q p) -> (e a q) p", p=128)),
                         (b2[:], d["L1_ffn_fc2_b"].rearrange("e a d -> (e a) d"))])
            turn_all(c, [(Wr[:], g[:]), (b1[:].rearrange("p e q -> p (e q)"), b1n[:])])
        cap = 2 * ((B * S + E - 1) // E)
        coef = route(c, st, Wr[:], None, "share", cap)
        add_expert_bias(c, coef, b2[:])
        experts(c, coef, d["L1_ffn_fc1_w"], d["L1_ffn_fc2_w"], 4, ACT.Relu, b1=b1)


def stage_l2_ffn(c):
    nc, d = c.nc, c.dram
    layernorm(c)
    with ExitStack() as st:
        Wr = c.sb(st, "Wr", [128, E])
        br = c.sb(st, "br", [128, 1, E])
        be = c.sb(st, "be", [E, D])
        g = c.sb(st, "g", [E, D])
        We = c.sb(st, "We", [128, E, D])
        WeT = c.sb(st, "WeT", [128, E, D])
        load_all(c, [(g[:], d["L2_ffn_w_router"]), (br[:, 0, :], row_bcast(d["L2_ffn_b_router"])),
                     (be[:], d["L2_ffn_b_experts"]), (We[:], d["L2_ffn_w_experts"].rearrange("e o d -> o e d"))])
        turn_all(c, [(Wr[:], g[:])] + [(WeT[:, e, :], We[:, e, :]) for e in range(E)])
        coef = route(c, st, Wr[:], br[:], "one")
        add_expert_bias(c, coef, be[:])
        ps = c.ps(st, "psE", [128, 2, E * D])
        made, used = c.sem("made"), c.sem("used")
        flat = WeT[:].rearrange("p e d -> p (e d)")
        with nc.Block() as block:
            @block.tensor
            def _(pe):
                for t in range(NT):
                    if t >= 2:
                        pe.wait_ge(used, E * (t - 1) + ONE)
                    for n in range(0, E * D, 512):
                        last = pe.matmul(ps[:, t % 2, n:n + 512], c.xnT[:, t * 128:t * 128 + 128],
                                         flat[:, n:n + 512], start=True, stop=True)
                    last.then_inc(made, 1)

            @block.vector
            def _(dve):
                for t in range(NT):
                    dve.wait_ge(made, t + 1 + ONE)
                    for e in range(E):
                        dve.scalar_tensor_tensor(out=c.x[:, t, :], in0=ps[:, t % 2, e * D:e * D + D],
                                                 scalar=coef[:, t, e:e + 1], in1=c.x[:, t, :],
                                                 op0=ALU.mult, op1=ALU.add).then_inc(used, 1)
                        dve.wait_ge(used, E * t + e + 1 + ONE)


def stage_l3_ffn(c):
    nc, d = c.nc, c.dram
    layernorm(c)
    with ExitStack() as st:
        Wr = c.sb(st, "Wr", [128, E])
        load_all(c, [(Wr[:], d["L3_ffn_router_w"])])
        coef = route(c, st, Wr[:], None, "prob")
        experts(c, coef, d["L3_ffn_w1"], d["L3_ffn_w2"], 1, ACT.Silu)
        gu = c.sb(st, "gu", [128, 2, 128])
        down = c.sb(st, "down", [128, D])
        gw = c.sb(st, "gw", [128, 1])
        gate = c.sb(st, "gate", [128, B * S])
        sg = c.sb(st, "sg", [128, NT])
        psG = c.ps(st, "psG", [128, B * S])
        psUp = c.ps(st, "psUp", [128, B * S])
        psY = c.ps(st, "psY", [128, NT, D])
        psg = c.ps(st, "psg", [128, NT])
        made, gated, ready, summed, done = (c.sem(n) for n in ("made", "gated", "ready", "summed", "done"))
        load_all(c, [(gu[:].rearrange("p a f -> p (a f)"), d["L3_ffn_shared_gate_up"]),
                     (down[:], d["L3_ffn_shared_down"]), (gw[:], d["L3_ffn_shared_gate_w"])])
        with nc.Block() as block:
            @block.tensor
            def _(pe):
                for n in range(0, B * S, 512):
                    pe.matmul(psG[:, n:n + 512], gu[:, 0, :], c.xnT[:, n:n + 512], start=True, stop=True)
                    pe.matmul(psUp[:, n:n + 512], gu[:, 1, :], c.xnT[:, n:n + 512], start=True, stop=True)
                for t in range(NT):
                    last = pe.matmul(psg[:, t:t + 1], c.xnT[:, t * 128:t * 128 + 128], gw[:], start=True, stop=True)
                last.then_inc(made, 1)
                pe.wait_ge(ready, 1 + ONE)
                for t in range(NT):
                    last = pe.matmul(psY[:, t, :], gate[:, t * 128:t * 128 + 128], down[:], start=True, stop=True)
                last.then_inc(summed, 1)

            @block.scalar
            def _(act):
                act.wait_ge(made, 1 + ONE)
                act.activation(gate[:], psG[:], ACT.Silu).then_inc(gated, 1)
                act.activation(sg[:], psg[:], ACT.Sigmoid).then_inc(gated, 1)

            @block.vector
            def _(dve):
                dve.wait_ge(gated, 2 + ONE)
                dve.tensor_tensor(gate[:], gate[:], psUp[:], ALU.mult).then_inc(ready, 1)
                dve.wait_ge(summed, 1 + ONE)
                for t in range(NT):
                    last = dve.scalar_tensor_tensor(out=c.x[:, t, :], in0=psY[:, t, :], scalar=sg[:, t:t + 1],
                                                    in1=c.x[:, t, :], op0=ALU.mult, op1=ALU.add)
                last.then_inc(done, 1)
                dve.wait_ge(done, 1 + ONE)


def quantize(dve, link, v, a, q, s, r):
    shape = list(v.shape)
    link(dve.tensor_reduce(s[:, :, 0], v, X, ALU.max, apply_absolute_value=True))
    link(dve.tensor_scalar(s, s, 1.0 / 6.0, 1e-12, ALU.mult, ALU.max))
    link(dve.reciprocal(r, s))
    link(dve.tensor_tensor(v, v, bc(r, shape), ALU.mult))
    link(dve.scalar_tensor_tensor(out=a, in0=v, scalar=-1.0, in1=v, op0=ALU.mult, op1=ALU.max))
    link(dve.tensor_scalar(q, a, 5.0, 2.0, ALU.is_gt, ALU.mult))
    for mid in (3.5, 2.5):
        link(dve.scalar_tensor_tensor(out=q, in0=a, scalar=mid, in1=q, op0=ALU.is_gt, op1=ALU.add))
    link(dve.tensor_scalar(q, q, 2.0, None, ALU.mult))
    for mid in (1.75, 1.25, 0.75, 0.25):
        link(dve.scalar_tensor_tensor(out=q, in0=a, scalar=mid, in1=q, op0=ALU.is_gt, op1=ALU.add))
    link(dve.tensor_scalar(v, v, 0.0, -0.5, ALU.is_ge, ALU.add))
    link(dve.tensor_tensor(v, v, q, ALU.mult))
    link(dve.tensor_tensor(v, v, bc(s, shape), ALU.mult))


def stage_l0_ffn(c):
    nc, d = c.nc, c.dram
    I = 352
    IC = [(0, 128), (128, 128), (256, 96)]
    layernorm(c)
    with ExitStack() as st:
        wT = c.sb(st, "wT", [128, 2, I])
        wdT = c.sb(st, "wdT", [128, 3, D])
        h = c.sb(st, "h", [128, NT, I])
        u = c.sb(st, "u", [128, NT, I])
        a = c.sb(st, "a", [128, NT * I // 16, 16])
        q = c.sb(st, "q", [128, NT * I // 16, 16])
        s = c.sb(st, "s", [128, NT * I // 16, 1])
        r = c.sb(st, "r", [128, NT * I // 16, 1])
        xqT = c.sb(st, "xqT", [128, NT, 128])
        hT = c.sb(st, "hT", [128, 3, NT, 128])
        w = c.sb(st, "w", [128, 2, 3, D])
        wd = c.sb(st, "wd", [128, I])
        wl = [(w[0:n, g, k, :], d[name][o:o + n, :]) for g, name in enumerate(("L0_ffn_w_gate", "L0_ffn_w_up"))
              for k, (o, n) in enumerate(IC)]
        load_all(c, wl + [(wd[:], d["L0_ffn_w_down"])])

        def quantize_all(parts):
            order = c.sem("quant_order")
            with nc.Block() as block:
                @block.vector
                def _(dve):
                    link = Link(dve, order)
                    for v in parts:
                        p, n = v.shape[0], v.shape[1]
                        quantize(dve, link, v, a[0:p, 0:n, :], q[0:p, 0:n, :], s[0:p, 0:n, :], r[0:p, 0:n, :])

        quantize_all([c.xn[:].rearrange("p t (n b) -> p (t n) b", b=16), wd[:].rearrange("p (n b) -> p n b", b=16)]
                     + [v.rearrange("p (n b) -> p n b", b=16) for v, _ in wl])
        turn_all(c, [(xqT[:, t, :], c.xn[:, t, :]) for t in range(NT)]
                 + [(wT[:, g, o:o + n], w[0:n, g, k, :]) for g in range(2) for k, (o, n) in enumerate(IC)]
                 + [(wdT[0:n, k, :], wd[:, o:o + n]) for k, (o, n) in enumerate(IC)])
        with ExitStack() as s2:
            pg = c.ps(s2, "pg", [128, 2, 512])
            pu = c.ps(s2, "pu", [128, 2, 512])
            made, silu, used = c.sem("made"), c.sem("silu"), c.sem("used")
            with nc.Block() as block:
                @block.tensor
                def _(pe):
                    for t in range(NT):
                        if t >= 2:
                            pe.wait_ge(used, t - 1 + ONE)
                        pe.matmul(pg[:, t % 2, 0:I], xqT[:, t, :], wT[:, 0, :], start=True, stop=True)
                        pe.matmul(pu[:, t % 2, 0:I], xqT[:, t, :], wT[:, 1, :], start=True, stop=True
                                  ).then_inc(made, 1)

                @block.scalar
                def _(act):
                    for t in range(NT):
                        act.wait_ge(made, t + 1 + ONE)
                        act.activation(u[:, t, :], pg[:, t % 2, 0:I], ACT.Silu).then_inc(silu, 1)

                @block.vector
                def _(dve):
                    for t in range(NT):
                        dve.wait_ge(silu, t + 1 + ONE)
                        dve.tensor_tensor(h[:, t, :], u[:, t, :], pu[:, t % 2, 0:I], ALU.mult).then_inc(used, 1)
                    dve.wait_ge(used, NT + ONE)
        quantize_all([h[:].rearrange("p t (n b) -> p (t n) b", b=16)])
        turn_all(c, [(hT[0:n, k, t, :], h[:, t, o:o + n]) for k, (o, n) in enumerate(IC) for t in range(NT)])
        py = c.ps(st, "py", [128, NT, D])
        summed, added = c.sem("summed"), c.sem("added")
        with nc.Block() as block:
            @block.tensor
            def _(pe):
                for t in range(NT):
                    for k, (o, n) in enumerate(IC):
                        last = pe.matmul(py[:, t, :], hT[0:n, k, t, :], wdT[0:n, k, :], start=(k == 0), stop=(k == 2))
                last.then_inc(summed, 1)

            @block.vector
            def _(dve):
                dve.wait_ge(summed, 1 + ONE)
                dve.tensor_tensor(c.x[:], c.x[:], py[:], ALU.add).then_inc(added, 1)
                dve.wait_ge(added, 1 + ONE)


BIG = 1.0e30


def stage_l0_xattn(c):
    nc = c.nc
    layernorm(c)
    dist = nc.dram_tensor("dist_scratch", [NT, 128, K], F32, kind="Internal").ap()
    cost = nc.dram_tensor("cost_scratch", [B, S + 1, K], F32, kind="Internal").ap()
    step = nc.dram_tensor("step_scratch", [B, S, K], F32, kind="Internal").ap()
    hi_dram = nc.dram_tensor("hi_scratch", [B * S], F32, kind="Internal").ap()
    lo_dram = nc.dram_tensor("lo_scratch", [B * S], F32, kind="Internal").ap()
    distances(c, dist)
    accumulate_costs(c, dist.rearrange("t (b s) k -> (t b) s k", b=2), cost)
    with ExitStack() as st:
        iota1 = c.sb(st, "iota1", [128, K])
        lows = c.sb(st, "lows", [128, NT, K])
        choose_steps(c, cost, step, iota1, lows)
        trace_back(c, step, iota1, hi_dram)
        look_up_lows(c, iota1, lows, hi_dram, lo_dram)
    add_aligned(c, hi_dram, lo_dram)


def distances(c, dist):
    nc = c.nc
    with ExitStack() as st:
        ctxT = c.sb(st, "ctxT", [128, 2, 2, K])
        ctxsq = c.sb(st, "ctxsq", [128, 2, 2, K])
        xm2 = c.sb(st, "xm2", [128, 2, 128])
        dsq = c.sb(st, "dsq", [128, 2, K])
        dd = c.sb(st, "dd", [128, 2, K])
        sq = c.sb(st, "sq", [128, NT, D])
        bb = c.sb(st, "bb", [128, NT])
        bcur = c.sb(st, "bcur", [128, 2])
        psD = [c.ps(st, f"psD{u}", [128, 2048]) for u in range(2)]

        def signals(name):
            return [c.sem(f"{name}{u}") for u in range(2)]

        loaded = [[c.sem(f"loaded{u}{j}") for j in range(2)] for u in range(2)]
        order, xm2_ready = c.sem("order"), c.sem("xm2")
        sq_ready, made, clamped = signals("sq"), signals("made"), signals("clamped")
        rooted, stored = signals("rooted"), signals("stored")
        with nc.Block() as block:
            def load(sp, p, u):
                for j in range(2):
                    sp.dma_start(ctxT[:, u, j, :], c.ctxT[ds(p * 2 + j, 1)].rearrange("b p k -> p (b k)")
                                 ).then_inc(loaded[u][j], 16)

            @block.sync
            def _(sp):
                load(sp, 0, 0)
                load(sp, 1, 1)
                with sp.Fori(0, NT // 2 - 1) as i:
                    for u in range(2):
                        sp.wait_ge(made[u], i + 1 + ONE)
                        settle(sp)
                        load(sp, i * 2 + (2 + u), u)

            @block.gpsimd
            def _(pool):
                with pool.Fori(0, NT // 2) as i:
                    for u in range(2):
                        pool.wait_ge(made[u], i + ONE)
                        for j in range(2):
                            pool.wait_ge(loaded[u][j], i * 16 + 16 + ONE)
                            pool.tensor_tensor(ctxsq[:, u, j, :], ctxT[:, u, j, :], ctxT[:, u, j, :], ALU.mult
                                               ).then_inc(sq_ready[u], 1)

            @block.tensor
            def _(pe):
                with pe.Fori(0, NT // 2) as i:
                    for u in range(2):
                        pe.wait_ge(xm2_ready, i * 2 + (u + 1) + ONE)
                        pe.wait_ge(clamped[u], i + ONE)
                        for j in range(2):
                            pe.wait_ge(loaded[u][j], i * 16 + 16 + ONE)
                            pe.wait_ge(sq_ready[u], i * 2 + (j + 1) + ONE)
                            r = slice(j * S, j * S + S)
                            for o, w in KB:
                                pe.matmul(psD[u][r, o:o + w], xm2[:, u, r],
                                          ctxT[:, u, j, o:o + w], start=True, stop=False)
                                last = pe.matmul(psD[u][r, o:o + w], c.ones[:, 0:S], ctxsq[:, u, j, o:o + w],
                                                 start=False, stop=True)
                        last.then_inc(made[u], 1)

            @block.vector
            def _(dve):
                def tokens(p, u):
                    dve.tensor_scalar(xm2[:, u, :], c.xnT[:, ds(p * 128, 128)], -2.0, None, ALU.mult
                                      ).then_inc(xm2_ready, 1)

                def pairs(i, final):
                    link = Link(dve, order, i * 2 + 2)
                    for u in range(2):
                        link(dve.tensor_copy(bcur[:, u:u + 1], bb[:, ds(i * 2 + u, 1)]))
                        dve.wait_ge(rooted[u], i + ONE)
                        dve.wait_ge(made[u], i + 1 + ONE)
                        dve.tensor_scalar(dsq[:, u, :], psD[u][:, 0:K], bcur[:, u:u + 1], 0.0, ALU.add, ALU.max
                                          ).then_inc(clamped[u], 1)
                        if not final:
                            tokens(i * 2 + (u + 2), u)
                        dve.wait_ge(clamped[u], i + 1 + ONE)
                        settle(dve)

                for u in range(2):
                    tokens(u, u)
                link = Link(dve, order)
                link(dve.tensor_tensor(sq[:], c.xn[:], c.xn[:], ALU.mult))
                link(dve.reduce_sum(bb[:], sq[:], axis=X))
                with dve.Fori(0, NT // 2 - 1) as i:
                    pairs(i, False)
                pairs(NT // 2 - 1, True)

            @block.scalar
            def _(act):
                with act.Fori(0, NT // 2) as i:
                    for u in range(2):
                        act.wait_ge(clamped[u], i + 1 + ONE)
                        act.wait_ge(stored[u], i * 16 + ONE)
                        act.activation(dd[:, u, :], dsq[:, u, :], ACT.Sqrt).then_inc(rooted[u], 1)
                        act.wait_ge(rooted[u], i + 1 + ONE)
                        act.dma_start(dist[ds(i * 2 + u, 1)].rearrange("t p k -> p (t k)"), dd[:, u, :]
                                      ).then_inc(stored[u], 16)
                for u in range(2):
                    act.wait_ge(stored[u], 16 * (NT // 2) + ONE)


BLOCKS = 128 // B
ROWS = (K + BLOCKS - 1) // BLOCKS
FROM = [(r * ROWS, min(ROWS, K - r * ROWS)) for r in range(BLOCKS)]
CG = 16


def by_block(pool, link, tile, values):
    link(pool.memset(tile, values[-1]))
    for r in range(BLOCKS - 1, 0, -1):
        link(pool.affine_select(out=tile, in_=tile, compare_op=ALU.is_ge, fill=values[r - 1], base=-r * B,
                                pattern=[[0, 1]], channel_multiplier=1))


def accumulate_costs(c, dist, cost):
    nc = c.nc
    STEPS = S + BLOCKS - 1
    with ExitStack() as st:
        dcol = c.sb(st, "dcol", [128, STEPS, ROWS + 1])
        rcol = c.sb(st, "rcol", [128, STEPS + 1, ROWS + 1])
        m = c.sb(st, "m", [128, ROWS + 1])
        next_block = c.sb(st, "next_block", [128, 128])
        top = c.sb(st, "top", [128, 1])
        big = c.sb(st, "big", [B, K])
        psB = c.ps(st, "psB", [128, 1])
        loaded = [c.sem(f"loaded{g}") for g in range(S // CG)]
        order, filled, stored, pool_order = (c.sem(n) for n in ("order", "filled", "stored", "pool_order"))
        scanned, moved = c.sem("scanned"), c.sem("moved")
        with nc.Block() as block:
            @block.vector
            def _(dve):
                dve.memset(dcol[:, 0:STEPS // 2, :], 0.0).then_inc(filled, 1)
                dve.memset(rcol[:, 0, :], BIG).then_inc(filled, 1)
                dve.memset(big[:], BIG).then_inc(filled, 1)
                dve.memset(next_block[:, 0:B], 0.0).then_inc(filled, 1)
                dve.tensor_copy(next_block[:, B:128], c.ident[:, 0:128 - B]).then_inc(filled, 1)
                dve.wait_ge(filled, 5 + ONE)
                dve.memset(rcol[0:B, 0, 0:1], 0.0).then_inc(filled, 1)
                dve.wait_ge(filled, 6 + ONE)

            @block.gpsimd
            def _(pool):
                link = Link(pool, pool_order)
                link(pool.memset(dcol[:, STEPS // 2:STEPS, :], 0.0))
                by_block(pool, link, top[:], [BIG] + [0.0] * (BLOCKS - 1))

        with nc.Block() as block:
            def load(eng, g, r):
                o, w = FROM[r]
                eng.dma_start(dcol[r * B:r * B + B, g * CG + r:g * CG + r + CG, 1:1 + w],
                              dist[:, g * CG:g * CG + CG, o:o + w]).then_inc(loaded[g], 16)

            def store(eng, g, r):
                o, w = FROM[r]
                eng.dma_start(cost[:, 1 + g * CG:1 + g * CG + CG, o:o + w],
                              rcol[r * B:r * B + B, 1 + g * CG + r:1 + g * CG + r + CG, 1:1 + w]).then_inc(stored, 16)

            @block.sync
            def _(sp):
                for g in range(S // CG):
                    for r in range(0, BLOCKS, 2):
                        load(sp, g, r)
                sp.dma_start(cost[:, 0, :], big[:]).then_inc(stored, 16)
                for g in range(S // CG):
                    for r in range(0, BLOCKS, 2):
                        sp.wait_ge(scanned, (g + 1) * CG + r + ONE)
                        store(sp, g, r)
                sp.wait_ge(stored, 16 * (1 + BLOCKS * S // CG) + ONE)

            @block.scalar
            def _(act):
                for g in range(S // CG):
                    for r in range(1, BLOCKS, 2):
                        load(act, g, r)
                for g in range(S // CG):
                    for r in range(1, BLOCKS, 2):
                        act.wait_ge(scanned, (g + 1) * CG + r + ONE)
                        store(act, g, r)

            @block.tensor
            def _(pe):
                for s in range(STEPS):
                    pe.wait_ge(scanned, s + ONE)
                    pe.matmul(psB[:], next_block[:],
                              rcol[:, ds(s, 1), ROWS:ROWS + 1].rearrange("p a k -> p (a k)"),
                              start=True, stop=True).then_inc(moved, 1)

            @block.vector
            def _(dve):
                def step(s):
                    link = Link(dve, order, s * 2)
                    before = rcol[:, ds(s, 1), :].rearrange("p a k -> p (a k)")
                    link(dve.tensor_tensor(m[:, 1:ROWS + 1], before[:, 0:ROWS], before[:, 1:ROWS + 1], ALU.min))
                    dve.wait_ge(moved, s + 1 + ONE)
                    link(dve.tensor_tensor(m[:, 0:1], psB[:], top[:], ALU.add))
                    dve.tensor_tensor_scan(rcol[:, ds(s + 1, 1), :].rearrange("p a k -> p (a k)"), m[:],
                                           dcol[:, ds(s, 1), :].rearrange("p a k -> p (a k)"), BIG,
                                           ALU.min, ALU.add).then_inc(scanned, 1)
                    dve.wait_ge(scanned, s + 1 + ONE)

                for g in range(S // CG):
                    dve.wait_ge(loaded[g], 16 * BLOCKS + ONE)
                    for s in range(g * CG, g * CG + CG):
                        step(s)
                for s in range(S, STEPS):
                    step(s)


def choose_steps(c, cost, step, iota1, lows):
    nc = c.nc
    with ExitStack() as st:
        cur = c.sb(st, "cur", [128, 2, K + 1])
        left = c.sb(st, "left", [128, 2, K + 1])
        a = c.sb(st, "a", [128, K])
        leave = c.sb(st, "leave", [128, K])
        diag = c.sb(st, "diag", [128, K])
        lcur = c.sb(st, "lcur", [128, 2, K])
        nxt = c.sb(st, "nxt", [128, 2, K])
        zero = c.sb(st, "zero", [128, K])
        loaded = [c.sem("loaded0"), c.sem("loaded1")]
        stored = [c.sem("stored0"), c.sem("stored1")]
        order, used, ready, low_ready, kept = (c.sem(n) for n in ("order", "used", "ready", "low_ready", "kept"))
        made, filled = c.sem("iota_made"), c.sem("filled")
        LINKS = 6
        with nc.Block() as block:
            def load(sp, t, j):
                for b in range(2):
                    r = slice(b * S, b * S + S)
                    sp.dma_start(cur[r, j, 1:K + 1], cost[ds(t * 2 + b, 1), 1:S + 1, :].rearrange("b s k -> (b s) k")
                                 ).then_inc(loaded[j], 16)
                    sp.dma_start(left[r, j, 1:K + 1], cost[ds(t * 2 + b, 1), 0:S, :].rearrange("b s k -> (b s) k")
                                 ).then_inc(loaded[j], 16)

            @block.sync
            def _(sp):
                load(sp, 0, 0)
                load(sp, 1, 1)
                with sp.Fori(0, NT // 2 - 1) as i:
                    for j in range(2):
                        sp.wait_ge(used, i * 2 + (j + 1) + ONE)
                        settle(sp)
                        load(sp, i * 2 + (2 + j), j)

            @block.gpsimd
            def _(pool):
                pool.iota(iota1[:], pattern=[[1, K]], base=1, channel_multiplier=0,
                          allow_small_or_imprecise_dtypes=True).then_inc(made, 1)

            @block.vector
            def _(dve):
                dve.memset(cur[:, :, 0:1], BIG).then_inc(filled, 1)
                dve.memset(left[:, :, 0:1], BIG).then_inc(filled, 1)
                dve.memset(zero[:], 0.0).then_inc(filled, 1)
                dve.wait_ge(filled, 3 + ONE)
                dve.wait_ge(made, 1 + ONE)
                with dve.Fori(0, NT // 2) as i:
                    for j in range(2):
                        t = i * 2 + j
                        link = Link(dve, order, i * (2 * LINKS) + j * LINKS)
                        dve.wait_ge(loaded[j], i * 64 + 64 + ONE)
                        dve.wait_ge(ready, t + ONE)
                        cu, cl, cd = cur[:, j, 0:K], left[:, j, 1:K + 1], left[:, j, 0:K]
                        link(dve.tensor_tensor(a[:], cu, cl, ALU.min))
                        link(dve.tensor_tensor(diag[:], cd, a[:], ALU.is_le))
                        link(dve.tensor_tensor(a[:], cu, cl, ALU.is_gt))
                        link(dve.tensor_tensor(leave[:], cu, cd, ALU.is_ge))
                        dve.tensor_tensor(leave[:], leave[:], a[:], ALU.max).then_inc(used, 1)
                        dve.wait_ge(used, t + 1 + ONE)
                        settle(dve)
                        link(dve.tensor_tensor(a[:], iota1[:], leave[:], ALU.mult))
                        dve.wait_ge(kept, t + ONE)
                        settle(dve)
                        dve.tensor_tensor_scan(lcur[:, j, :], a[:], zero[:], 0.0, ALU.max, ALU.add
                                               ).then_inc(low_ready, 1)
                        dve.wait_ge(low_ready, t + 1 + ONE)
                        settle(dve)
                        link(dve.tensor_tensor(a[:], a[:], diag[:], ALU.subtract))
                        dve.wait_ge(stored[j], i * 16 + ONE)
                        settle(dve)
                        dve.tensor_tensor_scan(nxt[:, j, :], a[:], zero[:], 0.0, ALU.max, ALU.add).then_inc(ready, 1)
                        assert link.n == LINKS, link.n

            @block.scalar
            def _(act):
                with act.Fori(0, NT // 2) as i:
                    for j in range(2):
                        t = i * 2 + j
                        act.wait_ge(low_ready, t + 1 + ONE)
                        act.activation(lows[:, ds(t, 1), :].rearrange("p a k -> p (a k)"), lcur[:, j, :], ACT.Copy
                                       ).then_inc(kept, 1)
                        act.wait_ge(ready, t + 1 + ONE)
                        settle(act)
                        act.dma_start(step.rearrange("(t b) s k -> t (b s) k", b=2)[ds(t, 1)].rearrange(
                            "t p k -> p (t k)"), nxt[:, j, :]).then_inc(stored[j], 16)
                act.wait_ge(kept, NT + ONE)
                for j in range(2):
                    act.wait_ge(stored[j], 16 * (NT // 2) + ONE)


def trace_back(c, step, iota1, hi_dram):
    nc = c.nc
    with ExitStack() as st:
        col = c.sb(st, "col", [128, S, ROWS])
        junk = c.sb(st, "junk", [128, ROWS])
        part = c.sb(st, "part", [128, 1])
        same_batch = c.sb(st, "same_batch", [128, BLOCKS, B])
        before = c.sb(st, "before", [128, 1])
        hi = c.sb(st, "hi", [128, S + 1])
        psH = c.ps(st, "psH", [128, 1])
        loaded = [c.sem(f"loaded{g}") for g in range(S // CG)]
        found, summed, set_, stored = c.sem("found"), c.sem("summed"), c.sem("hi_set"), c.sem("hi_stored")
        filled, pool_order = c.sem("filled"), c.sem("pool_order")
        with nc.Block() as block:
            @block.gpsimd
            def _(pool):
                link = Link(pool, pool_order)
                by_block(pool, link, before[:], [float(-r * ROWS) for r in range(BLOCKS)])

            @block.vector
            def _(dve):
                dve.memset(col[96:128, :, FROM[-1][1]:ROWS], 0.0).then_inc(filled, 1)
                blocks = c.ident[:].rearrange("p (r b) -> p b r", b=B)
                dve.reduce_sum(same_batch[:, 0, :], blocks, axis=X).then_inc(filled, 1)
                dve.wait_ge(filled, 2 + ONE)
                for r in range(1, BLOCKS):
                    dve.tensor_copy(same_batch[:, r, :], same_batch[:, 0, :]).then_inc(filled, 1)
                dve.wait_ge(filled, 1 + BLOCKS + ONE)

        with nc.Block() as block:
            def load(eng, g, r):
                o, w = FROM[r]
                eng.dma_start(col[r * B:r * B + B, g * CG:g * CG + CG, 0:w],
                              step[:, g * CG:g * CG + CG, o:o + w]).then_inc(loaded[g], 16)

            @block.sync
            def _(sp):
                for g in reversed(range(S // CG)):
                    for r in range(0, BLOCKS, 2):
                        load(sp, g, r)
                sp.wait_ge(set_, S + 1 + ONE)
                sp.dma_start(hi_dram.rearrange("(b s) -> b s", b=B), hi[0:B, 1:S + 1]).then_inc(stored, 16)
                sp.wait_ge(stored, 16 + ONE)

            @block.scalar
            def _(act):
                for g in reversed(range(S // CG)):
                    for r in range(1, BLOCKS, 2):
                        load(act, g, r)

            @block.tensor
            def _(pe):
                for n in range(S):
                    pe.wait_ge(found, n + 1 + ONE)
                    pe.matmul(psH[:], same_batch[:].rearrange("p r b -> p (r b)"), part[:],
                              start=True, stop=True).then_inc(summed, 1)

            @block.vector
            def _(dve):
                dve.tensor_scalar(hi[:, S:S + 1], before[:], float(K), None, ALU.add).then_inc(set_, 1)
                dve.wait_ge(set_, 1 + ONE)
                for g in range(S // CG):
                    dve.wait_ge(loaded[S // CG - 1 - g], 16 * BLOCKS + ONE)
                    for n in range(g * CG, g * CG + CG):
                        place = n * -1 + S
                        dve.scalar_tensor_tensor(out=junk[:], in0=iota1[:, 0:ROWS], scalar=hi[:, ds(place, 1)],
                                                 in1=col[:, ds(place - 1, 1), :].rearrange("p a k -> p (a k)"),
                                                 op0=ALU.is_equal, op1=ALU.mult, accum_out=part[:]
                                                 ).then_inc(found, 1)
                        dve.wait_ge(summed, n + 1 + ONE)
                        dve.tensor_tensor(hi[:, ds(place - 1, 1)], psH[:], before[:], ALU.add).then_inc(set_, 1)
                        dve.wait_ge(set_, n + 2 + ONE)


def look_up_lows(c, iota1, lows, hi_dram, lo_dram):
    nc = c.nc
    with ExitStack() as st:
        hi = c.sb(st, "hi", [128, NT])
        lo = c.sb(st, "lo", [128, NT])
        junk = c.sb(st, "junk", [128, K])
        loaded, order, stored = c.sem("loaded"), c.sem("order"), c.sem("stored")
        with nc.Block() as block:
            @block.sync
            def _(sp):
                with nc.allow_non_contiguous_dma(reason="1024 single numbers"):
                    sp.dma_start(hi[:], hi_dram.rearrange("(t p) -> p t", p=128)).then_inc(loaded, 16)
                    sp.wait_ge(order, NT + ONE)
                    sp.dma_start(lo_dram.rearrange("(t p) -> p t", p=128), lo[:]).then_inc(stored, 16)
                    sp.wait_ge(stored, 16 + ONE)

            @block.vector
            def _(dve):
                link = Link(dve, order)
                dve.wait_ge(loaded, 16 + ONE)
                for t in range(NT):
                    link(dve.scalar_tensor_tensor(out=junk[:], in0=iota1[:], scalar=hi[:, t:t + 1],
                                                  in1=lows[:, t, :], op0=ALU.is_equal, op1=ALU.mult,
                                                  accum_out=lo[:, t:t + 1]))


def add_aligned(c, hi_dram, lo_dram):
    nc = c.nc
    RING = 4
    HALF = B * S // 2
    with ExitStack() as st:
        hi = c.sb(st, "hi", [128, B * S])
        lo = c.sb(st, "lo", [128, B * S])
        tmp = c.sb(st, "tmp", [128, HALF])
        row1 = c.sb(st, "row1", [128, len(KC)])
        inside = c.sb(st, "inside", [128, len(KC), B * S])
        ctxN = c.sb(st, "ctxN", [128, RING, len(KC), D])
        sumT = c.sb(st, "sumT", [128, B * S])
        psA = c.ps(st, "psA", [128, 2, 512])
        psX = c.ps(st, "psX", [128, NT, 128])
        ends, made, order = c.sem("ends"), c.sem("made"), c.sem("order")
        loaded = [c.sem(f"loaded{j}") for j in range(RING)]
        summed, copied, turned, done = (c.sem(n) for n in ("summed", "copied", "turned", "done"))
        with nc.Block() as block:
            def load(sp, b, j):
                n = K // 128
                sp.dma_start(ctxN[:, j, 0:n, :], c.dram["ctx_1024"][ds(b, 1), 0:n * 128, :].rearrange(
                    "b (c p) d -> p (b c) d", p=128)).then_inc(loaded[j], 16)
                sp.dma_start(ctxN[0:K - n * 128, j, n, :], c.dram["ctx_1024"][ds(b, 1), n * 128:K, :].rearrange(
                    "b p d -> p (b d)")).then_inc(loaded[j], 16)

            @block.sync
            def _(sp):
                sp.dma_start(hi[:], row_bcast(hi_dram)).then_inc(ends, 16)
                sp.dma_start(lo[:], row_bcast(lo_dram)).then_inc(ends, 16)
                for j in range(RING):
                    load(sp, j, j)
                with sp.Fori(0, B // RING - 1) as i:
                    for j in range(RING):
                        sp.wait_ge(summed, i * RING + (j + 1) + ONE)
                        settle(sp)
                        load(sp, i * RING + (RING + j), j)

            @block.gpsimd
            def _(pool):
                pool.iota(row1[:], pattern=[[128, len(KC)]], base=1, channel_multiplier=1,
                          allow_small_or_imprecise_dtypes=True).then_inc(made, 1)

            @block.vector
            def _(dve):
                link = Link(dve, order)
                dve.wait_ge(made, 1 + ONE)
                dve.wait_ge(ends, 32 + ONE)
                for h in range(2):
                    t = slice(h * HALF, h * HALF + HALF)
                    for k in range(len(KC)):
                        link(dve.tensor_scalar(tmp[:], lo[:, t], row1[:, k:k + 1], None, ALU.is_le))
                        link(dve.scalar_tensor_tensor(out=inside[:, k, t], in0=hi[:, t], scalar=row1[:, k:k + 1],
                                                      in1=tmp[:], op0=ALU.is_ge, op1=ALU.mult))

            @block.scalar
            def _(act):
                with act.Fori(0, NT) as i:
                    for j in range(2):
                        act.wait_ge(summed, i * 2 + (j + 1) + ONE)
                        act.activation(sumT[:, ds(i * 128 + j * S, S)], psA[:, j, 0:S], ACT.Copy).then_inc(copied, 1)

            @block.vector
            def _(dve):
                dve.wait_ge(turned, 1 + ONE)
                dve.tensor_tensor(c.x[:], c.x[:], psX[:], ALU.add).then_inc(done, 1)
                dve.wait_ge(done, 1 + ONE)

            @block.tensor
            def _(pe):
                NI = B // RING
                for h in range(2):
                    pe.wait_ge(order, 2 * len(KC) * (h + 1) + ONE)
                    with pe.Fori(h * NI // 2, (h + 1) * NI // 2) as i:
                        for j in range(RING):
                            pe.wait_ge(loaded[j], i * 32 + 32 + ONE)
                            pe.wait_ge(copied, i * RING + j // 2 * 2 + ONE)
                            for k, (o, w) in enumerate(KC):
                                last = pe.matmul(psA[:, j % 2, 0:S], ctxN[0:w, j, k, :],
                                                 inside[0:w, k, ds(i * (RING * S) + j * S, S)],
                                                 start=(k == 0), stop=(k == len(KC) - 1))
                            last.then_inc(summed, 1)
                pe.wait_ge(copied, 2 * NT + ONE)
                for t in range(NT):
                    last = pe.transpose(psX[:, t, :], sumT[:, t * 128:t * 128 + 128], c.ident[:])
                last.then_inc(turned, 1)


STAGES = [stage_l0_xattn, stage_l0_attn, stage_l0_ffn, stage_l1_xattn, stage_l1_attn, stage_l1_ffn, stage_l2_xattn,
          stage_l2_attn, stage_l2_ffn, stage_l3_xattn, stage_l3_attn, stage_l3_ffn]


def perceiver(nc, dram, out):
    with ExitStack() as ctx:
        c = Core(nc, ctx, dram)
        c.ctxT = nc.dram_tensor("ctxT_scratch", [B, 128, K], F32, kind="Internal").ap()
        constants(c)
        transpose_context(c)
        for stage in STAGES:
            stage(c)
            c.end_stage()
        stored = c.sem("out_stored")
        with nc.Block() as block:
            @block.sync
            def _(sp):
                sp.dma_start(out.rearrange("(t b) s d -> (b s) t d", b=2), c.x[:]).then_inc(stored, 16)
                sp.wait_ge(stored, 16 + ONE)


def kernel(**inputs):
    import numpy as np
    import concourse.bacc as bacc
    from concourse.bass_utils import run_bass_kernel_spmd

    nc = bacc.Bacc("TRN2", target_bir_lowering=False, num_devices=1)
    arrays, dram = {}, {}
    for name, value in inputs.items():
        a = np.ascontiguousarray(value)
        if a.dtype == np.bool_:
            a = a.view(np.uint8)
        arrays[f"in_{name}"] = a
        dram[name] = nc.dram_tensor(f"in_{name}", a.shape, mybir.dt.from_np(a.dtype), kind="ExternalInput").ap()
    out = nc.dram_tensor("out", [B, S, D], F32, kind="ExternalOutput").ap()
    perceiver(nc, dram, out)
    result = run_bass_kernel_spmd(nc, [arrays], core_ids=[0])
    return result.results[0]["out"]
```
